# Optimizing a Trainium2 kernel written in Bass

```python
import numpy as np
import jax
import jax.numpy as jnp

def _softmax(x, axis=-1):
    return jax.nn.softmax(x, axis=axis)

def _gelu(x):
    return jax.nn.gelu(x, approximate=True)

def _silu(x):
    return jax.nn.silu(x)

def _sigmoid(x):
    return jax.nn.sigmoid(x)

def _layernorm(x, axis=-1, eps=1e-05):
    m = jnp.mean(x, axis=axis, keepdims=True)
    v = jnp.var(x, axis=axis, keepdims=True)
    return (x - m) / jnp.sqrt(v + eps)

def _scatter_add(tgt, idx, src, axis=0):
    return tgt.at[idx].add(src)

def _segment_sum(src, seg, n):
    return jax.ops.segment_sum(src, seg, n)
kernel_name = 'mk_adaln_d1_jaxref_r8_2824ef'

def setup_inputs(seed: int=0):
    np.random.seed(seed)
    _w = jnp.asarray

    def _L0_attn_setup():
        import jax, jax.numpy as jnp
        import numpy as np
        D_MODEL = 128
        N_HEADS = 16
        D_K = D_MODEL // N_HEADS
        MAX_POS = 64
        ATT_SPAN = MAX_POS
        B, T = (4, 128)
        SCALE_FACTOR = 3

        def _heads(y):
            b, t, _ = y.shape
            return y.reshape(b, t, N_HEADS, D_K).transpose(0, 2, 1, 3)
        key = jax.random.key(seed)
        ks = jax.random.split(key, 16)
        init = lambda k, shape: jax.random.normal(k, shape, dtype=jnp.float32) * 0.02
        inp = {'x': jax.random.normal(ks[0], (B, T, D_MODEL), dtype=jnp.float32), 'Wq': init(ks[1], (D_MODEL, D_MODEL)), 'bq': jnp.zeros((D_MODEL,), jnp.float32), 'Wk': init(ks[2], (D_MODEL, D_MODEL)), 'bk': jnp.zeros((D_MODEL,), jnp.float32), 'Wv': init(ks[3], (D_MODEL, D_MODEL)), 'bv': jnp.zeros((D_MODEL,), jnp.float32), 'Wo': init(ks[4], (D_MODEL, D_MODEL)), 'bo': jnp.zeros((D_MODEL,), jnp.float32), 'Wpk': init(ks[5], (D_MODEL, D_MODEL)), 'bpk': jnp.zeros((D_MODEL,), jnp.float32), 'Wpq': init(ks[6], (D_MODEL, D_MODEL)), 'bpq': jnp.zeros((D_MODEL,), jnp.float32), 'rel_emb': init(ks[7], (2 * ATT_SPAN, D_MODEL))}
        return inp
    _L0_attn_in = _L0_attn_setup()

    def _L0_ffn_setup():
        import jax, jax.numpy as jnp
        import numpy as np
        D = 128
        LW = 16
        DEPTH = 8
        NN = 2 ** DEPTH - 1
        NL = 2 ** DEPTH
        B, S = (2, 128)

        def _fff(x, nw, nb, w1, b1, w2, b2, act):
            node = jnp.zeros(x.shape[:2], dtype=jnp.int32)
            for _ in range(DEPTH):
                logit = jnp.einsum('bsd,bsd->bs', x, nw[node]) + nb[node]
                node = 2 * node + 1 + (logit > 0).astype(jnp.int32)
            leaf = node - NN
            h = act(jnp.einsum('bsd,bsdl->bsl', x, w1[leaf]) + b1[leaf])
            return jnp.einsum('bsl,bsld->bsd', h, w2[leaf]) + b2[leaf]

        def _forward(x, q_nw, q_nb, q_w1, q_b1, q_w2, q_b2, k_nw, k_nb, k_w1, k_b1, k_w2, k_b2, v_nw, v_nb, v_w1, v_b1, v_w2, v_b2, f_nw, f_nb, f_w1, f_b1, f_w2, f_b2):
            mu = jnp.mean(x, -1, keepdims=True)
            sd = jnp.std(x, -1, ddof=1, keepdims=True)
            xn = (x - mu) / jnp.sqrt(sd + 1e-05)
            relu = jax.nn.relu
            q = _fff(xn, q_nw, q_nb, q_w1, q_b1, q_w2, q_b2, relu)
            k = _fff(xn, k_nw, k_nb, k_w1, k_b1, k_w2, k_b2, relu)
            v = _fff(xn, v_nw, v_nb, v_w1, v_b1, v_w2, v_b2, relu)
            att = jax.nn.softmax(jnp.einsum('bqd,bkd->bqk', q, k) / jnp.sqrt(jnp.float32(D)), axis=-1)
            y = xn + jnp.einsum('bqk,bkd->bqd', att, v)
            gelu = lambda t: jax.nn.gelu(t, approximate=False)
            return y + _fff(y, f_nw, f_nb, f_w1, f_b1, f_w2, f_b2, gelu)

        def _make_fff_params(key, scale_in, scale_leaf):
            ks = jax.random.split(key, 4)
            nw = jax.random.normal(ks[0], (NN, D), jnp.float32) * scale_in
            nb = jnp.zeros((NN,), jnp.float32)
            w1 = jax.random.normal(ks[1], (NL, D, LW), jnp.float32) * scale_in
            b1 = jax.random.normal(ks[2], (NL, LW), jnp.float32) * 0.01
            w2 = jax.random.normal(ks[3], (NL, LW, D), jnp.float32) * scale_leaf
            b2 = jnp.zeros((NL, D), jnp.float32)
            return (nw, nb, w1, b1, w2, b2)
        key = jax.random.key(seed)
        kx, kq, kk, kv, kf = jax.random.split(key, 5)
        s_in = 1.0 / np.sqrt(D)
        s_lf = 1.0 / np.sqrt(LW)
        inp = {'x': jax.random.normal(kx, (B, S, D), jnp.float32)}
        for name, kk_ in (('q', kq), ('k', kk), ('v', kv), ('f', kf)):
            nw, nb, w1, b1, w2, b2 = _make_fff_params(kk_, s_in, s_lf)
            inp.update({f'{name}_nw': nw, f'{name}_nb': nb, f'{name}_w1': w1, f'{name}_b1': b1, f'{name}_w2': w2, f'{name}_b2': b2})
        return inp
    _L0_ffn_in = _L0_ffn_setup()
    _L0_c = _w((lambda *s: np.random.randn(*s).astype(np.float32) * 0.05)(1, 128))
    _L0_wmod = _w((lambda *s: np.random.randn(*s).astype(np.float32) * 0.05)(128, 6 * 128) * 128 ** (-0.5))
    _d = {'L0_attn_x': _L0_attn_in['x'], 'L0_attn_Wq': _L0_attn_in['Wq'], 'L0_attn_bq': _L0_attn_in['bq'], 'L0_attn_Wk': _L0_attn_in['Wk'], 'L0_attn_bk': _L0_attn_in['bk'], 'L0_attn_Wv': _L0_attn_in['Wv'], 'L0_attn_bv': _L0_attn_in['bv'], 'L0_attn_Wo': _L0_attn_in['Wo'], 'L0_attn_bo': _L0_attn_in['bo'], 'L0_attn_Wpk': _L0_attn_in['Wpk'], 'L0_attn_bpk': _L0_attn_in['bpk'], 'L0_attn_Wpq': _L0_attn_in['Wpq'], 'L0_attn_bpq': _L0_attn_in['bpq'], 'L0_attn_rel_emb': _L0_attn_in['rel_emb'], 'L0_ffn_q_nw': _L0_ffn_in['q_nw'], 'L0_ffn_q_nb': _L0_ffn_in['q_nb'], 'L0_ffn_q_w1': _L0_ffn_in['q_w1'], 'L0_ffn_q_b1': _L0_ffn_in['q_b1'], 'L0_ffn_q_w2': _L0_ffn_in['q_w2'], 'L0_ffn_q_b2': _L0_ffn_in['q_b2'], 'L0_ffn_k_nw': _L0_ffn_in['k_nw'], 'L0_ffn_k_nb': _L0_ffn_in['k_nb'], 'L0_ffn_k_w1': _L0_ffn_in['k_w1'], 'L0_ffn_k_b1': _L0_ffn_in['k_b1'], 'L0_ffn_k_w2': _L0_ffn_in['k_w2'], 'L0_ffn_k_b2': _L0_ffn_in['k_b2'], 'L0_ffn_v_nw': _L0_ffn_in['v_nw'], 'L0_ffn_v_nb': _L0_ffn_in['v_nb'], 'L0_ffn_v_w1': _L0_ffn_in['v_w1'], 'L0_ffn_v_b1': _L0_ffn_in['v_b1'], 'L0_ffn_v_w2': _L0_ffn_in['v_w2'], 'L0_ffn_v_b2': _L0_ffn_in['v_b2'], 'L0_ffn_f_nw': _L0_ffn_in['f_nw'], 'L0_ffn_f_nb': _L0_ffn_in['f_nb'], 'L0_ffn_f_w1': _L0_ffn_in['f_w1'], 'L0_ffn_f_b1': _L0_ffn_in['f_b1'], 'L0_ffn_f_w2': _L0_ffn_in['f_w2'], 'L0_ffn_f_b2': _L0_ffn_in['f_b2'], 'L0_c': _L0_c, 'L0_wmod': _L0_wmod}
    _x0 = _d['L0_attn_x']
    _d['L0_attn_x'] = jax.random.normal(jax.random.fold_in(jax.random.key(seed), 1), (1, 2048, 128), dtype=_x0.dtype)
    del _x0
    return _d

def reference(L0_attn_x, L0_attn_Wq, L0_attn_bq, L0_attn_Wk, L0_attn_bk, L0_attn_Wv, L0_attn_bv, L0_attn_Wo, L0_attn_bo, L0_attn_Wpk, L0_attn_bpk, L0_attn_Wpq, L0_attn_bpq, L0_attn_rel_emb, L0_ffn_q_nw, L0_ffn_q_nb, L0_ffn_q_w1, L0_ffn_q_b1, L0_ffn_q_w2, L0_ffn_q_b2, L0_ffn_k_nw, L0_ffn_k_nb, L0_ffn_k_w1, L0_ffn_k_b1, L0_ffn_k_w2, L0_ffn_k_b2, L0_ffn_v_nw, L0_ffn_v_nb, L0_ffn_v_w1, L0_ffn_v_b1, L0_ffn_v_w2, L0_ffn_v_b2, L0_ffn_f_nw, L0_ffn_f_nb, L0_ffn_f_w1, L0_ffn_f_b1, L0_ffn_f_w2, L0_ffn_f_b2, L0_c, L0_wmod):

    def _L0_attn_ref(x, Wq, bq, Wk, bk, Wv, bv, Wo, bo, Wpk, bpk, Wpq, bpq, rel_emb):
        import jax, jax.numpy as jnp
        import numpy as np
        D_MODEL = 128
        N_HEADS = 16
        D_K = D_MODEL // N_HEADS
        MAX_POS = 64
        ATT_SPAN = MAX_POS
        B, T = (4, 128)
        SCALE_FACTOR = 3

        def _heads(y):
            b, t, _ = y.shape
            return y.reshape(b, t, N_HEADS, D_K).transpose(0, 2, 1, 3)
        b, t, c = x.shape
        scale = 1.0 / jnp.sqrt(jnp.asarray(D_K * SCALE_FACTOR, x.dtype))
        Q = _heads(x @ Wq.T + bq)
        K = _heads(x @ Wk.T + bk)
        V = _heads(x @ Wv.T + bv)
        rel = jnp.arange(t)[None, :] - jnp.arange(t)[:, None]
        rel_pos = jnp.clip(rel + ATT_SPAN, 0, 2 * ATT_SPAN - 1)
        p2c_pos = jnp.clip(-rel + ATT_SPAN, 0, 2 * ATT_SPAN - 1)
        scores = jnp.einsum('bhqd,bhkd->bhqk', Q, K) * scale
        pos_key = (rel_emb @ Wpk.T + bpk).reshape(2 * ATT_SPAN, N_HEADS, D_K)
        c2p = jnp.einsum('bhqd,shd->bhqs', Q, pos_key) * scale
        c2p = jnp.take_along_axis(c2p, rel_pos[None, None, :, :], axis=-1)
        pos_query = (rel_emb @ Wpq.T + bpq).reshape(2 * ATT_SPAN, N_HEADS, D_K)
        p2c = jnp.einsum('bhkd,shd->bhks', K, pos_query) * scale
        p2c = jnp.take_along_axis(p2c, p2c_pos[None, None, :, :], axis=-1)
        p2c = jnp.swapaxes(p2c, -1, -2)
        scores = scores + c2p + p2c
        probs = jax.nn.softmax(scores, axis=-1)
        ctx = jnp.einsum('bhqk,bhkd->bhqd', probs, V)
        ctx = ctx.transpose(0, 2, 1, 3).reshape(b, t, c)
        return ctx @ Wo.T + bo

    def _L0_ffn_ref(x, q_nw, q_nb, q_w1, q_b1, q_w2, q_b2, k_nw, k_nb, k_w1, k_b1, k_w2, k_b2, v_nw, v_nb, v_w1, v_b1, v_w2, v_b2, f_nw, f_nb, f_w1, f_b1, f_w2, f_b2):
        import jax, jax.numpy as jnp
        import numpy as np
        D = 128
        LW = 16
        DEPTH = 8
        NN = 2 ** DEPTH - 1
        NL = 2 ** DEPTH
        B, S = (2, 128)

        def _fff(x, nw, nb, w1, b1, w2, b2, act):
            node = jnp.zeros(x.shape[:2], dtype=jnp.int32)
            for _ in range(DEPTH):
                logit = jnp.einsum('bsd,bsd->bs', x, nw[node]) + nb[node]
                node = 2 * node + 1 + (logit > 0).astype(jnp.int32)
            leaf = node - NN
            h = act(jnp.einsum('bsd,bsdl->bsl', x, w1[leaf]) + b1[leaf])
            return jnp.einsum('bsl,bsld->bsd', h, w2[leaf]) + b2[leaf]

        def _forward(x, q_nw, q_nb, q_w1, q_b1, q_w2, q_b2, k_nw, k_nb, k_w1, k_b1, k_w2, k_b2, v_nw, v_nb, v_w1, v_b1, v_w2, v_b2, f_nw, f_nb, f_w1, f_b1, f_w2, f_b2):
            mu = jnp.mean(x, -1, keepdims=True)
            sd = jnp.std(x, -1, ddof=1, keepdims=True)
            xn = (x - mu) / jnp.sqrt(sd + 1e-05)
            relu = jax.nn.relu
            q = _fff(xn, q_nw, q_nb, q_w1, q_b1, q_w2, q_b2, relu)
            k = _fff(xn, k_nw, k_nb, k_w1, k_b1, k_w2, k_b2, relu)
            v = _fff(xn, v_nw, v_nb, v_w1, v_b1, v_w2, v_b2, relu)
            att = jax.nn.softmax(jnp.einsum('bqd,bkd->bqk', q, k) / jnp.sqrt(jnp.float32(D)), axis=-1)
            y = xn + jnp.einsum('bqk,bkd->bqd', att, v)
            gelu = lambda t: jax.nn.gelu(t, approximate=False)
            return y + _fff(y, f_nw, f_nb, f_w1, f_b1, f_w2, f_b2, gelu)

        def _make_fff_params(key, scale_in, scale_leaf):
            ks = jax.random.split(key, 4)
            nw = jax.random.normal(ks[0], (NN, D), jnp.float32) * scale_in
            nb = jnp.zeros((NN,), jnp.float32)
            w1 = jax.random.normal(ks[1], (NL, D, LW), jnp.float32) * scale_in
            b1 = jax.random.normal(ks[2], (NL, LW), jnp.float32) * 0.01
            w2 = jax.random.normal(ks[3], (NL, LW, D), jnp.float32) * scale_leaf
            b2 = jnp.zeros((NL, D), jnp.float32)
            return (nw, nb, w1, b1, w2, b2)
        return _forward(x, q_nw, q_nb, q_w1, q_b1, q_w2, q_b2, k_nw, k_nb, k_w1, k_b1, k_w2, k_b2, v_nw, v_nb, v_w1, v_b1, v_w2, v_b2, f_nw, f_nb, f_w1, f_b1, f_w2, f_b2)
    x = L0_attn_x
    mod = (_silu(L0_c) @ L0_wmod).reshape(L0_c.shape[0], 6, 1, -1)
    sa, ca, ga, sb, cb, gb = (mod[:, 0], mod[:, 1], mod[:, 2], mod[:, 3], mod[:, 4], mod[:, 5])
    ga = (2 * (ga >= 0) - 1) * jnp.maximum(jnp.abs(ga), 0.25)
    gb = (2 * (gb >= 0) - 1) * jnp.maximum(jnp.abs(gb), 0.25)
    h = _layernorm(x, axis=-1) * (1 + ca) + sa
    x = x + ga * _L0_attn_ref(h, L0_attn_Wq, L0_attn_bq, L0_attn_Wk, L0_attn_bk, L0_attn_Wv, L0_attn_bv, L0_attn_Wo, L0_attn_bo, L0_attn_Wpk, L0_attn_bpk, L0_attn_Wpq, L0_attn_bpq, L0_attn_rel_emb)
    h = _layernorm(x, axis=-1) * (1 + cb) + sb
    x = x + gb * _L0_ffn_ref(h, L0_ffn_q_nw, L0_ffn_q_nb, L0_ffn_q_w1, L0_ffn_q_b1, L0_ffn_q_w2, L0_ffn_q_b2, L0_ffn_k_nw, L0_ffn_k_nb, L0_ffn_k_w1, L0_ffn_k_b1, L0_ffn_k_w2, L0_ffn_k_b2, L0_ffn_v_nw, L0_ffn_v_nb, L0_ffn_v_w1, L0_ffn_v_b1, L0_ffn_v_w2, L0_ffn_v_b2, L0_ffn_f_nw, L0_ffn_f_nb, L0_ffn_f_w1, L0_ffn_f_b1, L0_ffn_f_w2, L0_ffn_f_b2)
    return x

_drawn_inputs = setup_inputs


def setup_inputs(seed=0):
    import zlib

    import numpy as np

    out = dict(_drawn_inputs(seed))
    spreads = {'L0_attn_bq': (0.0, 0.8),
     'L0_attn_bk': (0.0, 2.0),
     'L0_attn_bv': (0.0, 0.286),
     'L0_attn_bo': (0.0, 0.1),
     'L0_attn_bpk': (0.0, 2.0),
     'L0_attn_bpq': (0.0, 0.8),
     'L0_ffn_q_nb': (0.0, 0.372),
     'L0_ffn_q_b2': (0.0, 0.787),
     'L0_ffn_k_nb': (0.0, 0.1),
     'L0_ffn_k_b2': (0.0, 0.8),
     'L0_ffn_v_nb': (0.0, 0.1),
     'L0_ffn_v_b2': (0.0, 0.293),
     'L0_ffn_f_nb': (0.0, 0.1),
     'L0_ffn_f_b2': (0.0, 0.322)}
    factors = {'L0_attn_Wq': 8.0,
     'L0_attn_Wk': 8.0,
     'L0_attn_Wv': 7.191,
     'L0_attn_Wpk': 8.0,
     'L0_attn_Wpq': 8.0,
     'L0_attn_rel_emb': 8.0,
     'L0_ffn_q_b1': 27.725,
     'L0_ffn_k_b1': 26.195,
     'L0_ffn_v_b1': 23.042,
     'L0_ffn_f_b1': 33.855}
    for name, (base, spread) in spreads.items():
        noise = np.random.default_rng([zlib.crc32(name.encode()), seed]).standard_normal(out[name].shape)
        drawn = base * np.exp(spread * noise) if base else spread * noise
        out[name] = jnp.asarray(drawn.astype(out[name].dtype))
    for name, factor in factors.items():
        out[name] = (out[name] * factor).astype(out[name].dtype)
    return out
```

```python
from contextlib import ExitStack

import numpy as np

import concourse.bass as bass
from concourse import mybir

ALU = mybir.AluOpType
ACT = mybir.ActivationFunctionType
AX = mybir.AxisListType
F32 = mybir.dt.float32
BF16 = mybir.dt.bfloat16
I32 = mybir.dt.int32

P = 128
D = 128
T = 2048
NT = T // P
BANK = 512
NB = T // BANK
H = 16
DK = D // H
SPAN = 64
R = 2 * SPAN
SCALE = float((3 * DK) ** -0.5)
EPS = 1e-5

PART_A = (0, 0, 1, 1, 0, 2)
PART_B = (0, 1, 0, 1, 2, 0)
ROW_QK = len(PART_A) * DK
ROW_CL = ROW_QK
ROW_CR = ROW_CL + 3
ROW_S = ROW_CR + 3
ROW_M = ROW_S + 3
ROWS = ROW_M + 3

CL = P // DK
WIN = 2 * P
EXT = WIN + P - 1
TABW = EXT - CL + 1
KEY0 = P - CL
QRY0 = WIN - CL


def near_far(i):
    lo, hi = max(P * i - SPAN, 0), min(P * i - SPAN + WIN, T)
    return (lo, hi), (0, lo), (hi, T)


def far_units(i):
    _, left, right = near_far(i)
    pieces = [(True, *left), (False, *right)]
    total = sum(b - a for _, a, b in pieces)
    size = total // FU
    units = []
    for u in range(FU):
        a, b, at, unit = u * size, (u + 1) * size, 0, []
        for is_left, p, q in pieces:
            s, e = max(a, at), min(b, at + q - p)
            if e > s:
                unit.append((is_left, p + s - at, e - s, s - a))
            at += q - p
        units.append((size, unit))
    return units


FU = 4
N_C2P = 8
N_WIN = 8
N_FAR = NT * FU
N_A = N_C2P + N_WIN + N_FAR + 1
RING = 3
assert N_A % RING == 0
N_B = 2 * NT
GI = NT // 2


def setup_phase(nc, a, keep, scratch):
    x_nat, ident, modc, x_all = keep["x_nat"], keep["ident"], keep["modc"], None
    with ExitStack() as ctx:
        def sb(name, shape, dt=F32):
            return ctx.enter_context(nc.sbuf_tensor(name, shape, dt))

        def sem(name):
            return keep["semaphores"].enter_context(nc.semaphore(name))

        ps = ctx.enter_context(nc.psum_tensor("su_ps", [P, 8, BANK], F32))
        wmod = sb("su_wmod", [P, 6 * D])
        wts = sb("su_wts", [P, 6, D])
        rel = sb("su_rel", [P, 2, R])
        cols = sb("su_cols", [P, 8])
        bvrow = sb("su_bvrow", [1, D])
        ones_row = sb("su_ones_row", [1, P])
        silu = sb("su_silu", [P, 4])
        stats = sb("su_stats", [P, NT, 6])
        mv = sb("su_mv", [P, NT, 2])
        rstd = sb("su_rstd", [P, NT])
        expo = sb("su_expo", [P, NT])
        xn = sb("su_xn", [P, NT, D])
        hT = sb("su_hT", [P, T])
        qkT = sb("su_qkT", [P, 2, T])
        posT = sb("su_posT", [P, 2, R])
        ext = sb("su_ext", [P, 2, EXT])
        head_mask = sb("su_hm", [P, H])
        ends = sb("su_ends", [P, 2, 2, H])
        aux = sb("su_aux", [2 * H, 2, T])
        rest = sb("su_rest", [P, T])
        part = sb("su_part", [P, 2, 3, T], BF16)
        auxp = sb("su_auxp", [2 * H, 2, 3, T], BF16)
        oz = sb("su_oz", [H, 2, T], BF16)
        zer = sb("su_zer", [P, P])
        clampt = sb("su_clamp", [P, 4, 2])
        wog = sb("su_wog", [P, D])

        in_x, in_w, in_small = sem("in_x"), sem("in_w"), sem("in_small")
        made, vec, sil = sem("made"), sem("vec"), sem("sil")
        mod_ps, xt_ps, pos_ps, qk_ps, aux_ps, v_ps, wo_ps = (
            sem(n) for n in ("mod_ps", "xt_ps", "pos_ps", "qk_ps", "aux_ps", "v_ps", "wo_ps"))
        xn_ok, hT_ok, pos_ok, qk_ok, ends_ok, wog_ok, v_ok, mod_ok = (
            sem(n) for n in ("xn_ok", "hT_ok", "pos_ok", "qk_ok", "ends_ok", "wog_ok", "v_ok", "mod_ok"))
        ext_ok, parts_ok, aux_ok, auxp_ok, stored = (
            sem(n) for n in ("ext_ok", "parts_ok", "aux_ok", "auxp_ok", "stored"))
        var_ok, rstd_ok = sem("var_ok"), sem("rstd_ok")
        block = ctx.enter_context(nc.Block())

        @block.sync
        def _(sp):
            sp.dma_start(x_nat[:], a["x"].rearrange("a (n p) d -> p (a n) d", p=P)).then_inc(in_x, 16)
            sp.dma_start(wmod[:], a["wmod"]).then_inc(in_w, 16)
            for n, name in enumerate(("WqT", "WkT", "WvT", "WpkT", "WpqT", "Wo")):
                sp.dma_start(wts[:, n, :], a[name]).then_inc(in_w, 16)
            sp.dma_start(rel[:, 0, :], a["relT"]).then_inc(in_w, 16)
            sp.dma_start(rel[:, 1, :], a["relT_rev"]).then_inc(in_w, 16)
            for n, name in enumerate(("c", "bq", "bk", "bpk", "bpq", "bo")):
                sp.dma_start(cols[:, n:n + 1], a[name]).then_inc(in_small, 16)
            sp.dma_start(bvrow[:], a["bv"]).then_inc(in_small, 16)
            n_stored = 0

            def store(dst, src):
                nonlocal n_stored
                sp.dma_start(dst, src).then_inc(stored, 16)
                n_stored += 1

            sp.wait_ge(made, 9)
            qs, kl, kr = scratch["qst"], scratch["klst"], scratch["krst"]
            for r in range(3):
                store(qs[:, ROW_S + r, :], oz[:, 0, :])
                store(kl[:, ROW_CL + r, :], oz[:, 0, :])
                store(kl[:, ROW_CR + r, :], oz[:, 1, :])
                store(kr[:, ROW_CL + r, :], oz[:, 1, :])
                store(kr[:, ROW_CR + r, :], oz[:, 0, :])
                store(kl[:, ROW_M + r, :], oz[:, 0, :])
                store(kr[:, ROW_M + r, :], oz[:, 0, :])
            sp.wait_ge(ext_ok, 2)
            store(scratch["ext"].rearrange("w c e -> c w e"), ext[:])
            sp.wait_ge(qk_ok, 2 * NB)
            store(scratch["qk"].rearrange("w c t -> c w t"), qkT[:])
            for w in range(2):
                sp.wait_ge(parts_ok, 3 * (w + 1))
                for g in range(len(PART_A)):
                    rows = slice(g * DK, (g + 1) * DK)
                    if w == 0:
                        store(qs[:, rows, :], part[:, 0, PART_A[g], :])
                    else:
                        store(kl[:, rows, :], part[:, 1, PART_B[g], :])
                        store(kr[:, rows, :], part[:, 1, PART_B[g], :])
            sp.wait_ge(auxp_ok, 6)
            for r in range(3):
                store(qs[:, ROW_CL + r, :], auxp[0:H, 0, r, :])
                store(qs[:, ROW_CR + r, :], auxp[H:2 * H, 0, r, :])
                store(kl[:, ROW_S + r, :], auxp[0:H, 1, r, :])
                store(kr[:, ROW_S + r, :], auxp[H:2 * H, 1, r, :])
            sp.wait_ge(stored, 16 * n_stored)

        @block.gpsimd
        def _(pool):
            n_made = 0

            def make(ins):
                nonlocal n_made
                n_made += 1
                ins.then_inc(made, 1)
                pool.wait_ge(made, n_made)

            make(nc.gpsimd.memset(ident[:], 0.0))
            make(nc.gpsimd.affine_select(out=ident[:], in_=ident[:], compare_op=ALU.not_equal, fill=1.0,
                                         base=0, pattern=[[-1, P]], channel_multiplier=1))
            make(nc.gpsimd.memset(oz[:, 0, :], 1.0))
            make(nc.gpsimd.memset(oz[:, 1, :], 0.0))
            make(nc.gpsimd.memset(ones_row[:], 1.0))
            make(nc.gpsimd.memset(zer[:], 0.0))
            make(nc.gpsimd.memset(head_mask[:], 1.0))
            make(nc.gpsimd.affine_select(out=head_mask[:], in_=head_mask[:], compare_op=ALU.is_ge, fill=0.0,
                                         base=0, pattern=[[-DK, H]], channel_multiplier=1))
            make(nc.gpsimd.affine_select(out=head_mask[:], in_=head_mask[:], compare_op=ALU.is_ge, fill=0.0,
                                         base=DK - 1, pattern=[[DK, H]], channel_multiplier=-1))
            pool.wait_ge(var_ok, 1)
            make(nc.gpsimd.memset(expo[:], -0.5))
            make(nc.gpsimd.tensor_scalar(rstd[:], mv[:, :, 1], EPS, None, ALU.add))
            nc.gpsimd.tensor_tensor(rstd[:], rstd[:], expo[:], ALU.pow).then_inc(rstd_ok, 1)

        @block.scalar
        def _(act):
            act.wait_ge(in_small, 16 * 7)
            nc.scalar.activation(silu[:, 0:1], cols[:, 0:1], ACT.Exp, scale=-1.0).then_inc(sil, 1)

        @block.tensor
        def _(pe):
            pe.wait_ge(in_w, 16 * 9)
            pe.wait_ge(sil, 2)
            for n in range(6):
                last = nc.tensor.matmul(ps[:, 0, n:n + 1], wmod[:, n * D:(n + 1) * D], silu[:, 3:4],
                                        start=True, stop=True)
            last.then_inc(mod_ps, 1)
            for w in range(2):
                last = nc.tensor.matmul(ps[:, 1 + w, 0:R], wts[:, 3 + w, :], rel[:, w, :], start=True, stop=True)
            last.then_inc(pos_ps, 1)
            pe.wait_ge(made, 9)
            pe.wait_ge(xn_ok, NT)
            for b in range(NB):
                for s in range(4):
                    last = nc.tensor.transpose(ps[:, 4 + b, s * P:(s + 1) * P], xn[:, 4 * b + s, :], ident[:])
                last.then_inc(xt_ps, 1)
            pe.wait_ge(pos_ok, 2)
            pe.wait_ge(mod_ok, 1)
            for w in range(2):
                if w == 1:
                    pe.wait_ge(qk_ok, NB)
                for b in range(NB):
                    pe.wait_ge(hT_ok, b + 1)
                    nc.tensor.matmul(ps[:, b, :], wts[:, w, :], hT[:, b * BANK:(b + 1) * BANK],
                                     start=True, stop=True).then_inc(qk_ps, 1)
            pe.wait_ge(ends_ok, 4)
            for w in range(2):
                if w == 1:
                    pe.wait_ge(aux_ok, NB)
                for b in range(NB):
                    pe.wait_ge(qk_ok, 2 * NB)
                    nc.tensor.matmul(ps[0:2 * H, 4 + b, :], ends[:, w, :, :].rearrange("p e h -> p (e h)"),
                                     qkT[:, w, b * BANK:(b + 1) * BANK], start=True, stop=True).then_inc(aux_ps, 1)
            for b in range(NB):
                for s in range(4):
                    t = 4 * b + s
                    nc.tensor.matmul(ps[:, b, s * P:(s + 1) * P], hT[:, t * P:(t + 1) * P], wts[:, 2, :],
                                     start=True, stop=False)
                    last = nc.tensor.matmul(ps[:, b, s * P:(s + 1) * P], ones_row[:], bvrow[:],
                                            start=False, stop=True)
                last.then_inc(v_ps, 1)
            pe.wait_ge(wog_ok, 2)
            pe.wait_ge(aux_ok, 2 * NB)
            nc.tensor.transpose(ps[:, 4, 0:D], wog[:], ident[:])
            nc.tensor.matmul(ps[0:1, 5, 0:D], cols[:, 6:7], ident[:], start=True, stop=True).then_inc(wo_ps, 1)

        @block.vector
        def _(dve):
            n_vec = 0

            def step(ins, *more):
                nonlocal n_vec
                n_vec += 1
                ins.then_inc(vec, 1)
                dve.wait_ge(vec, n_vec)

            dve.wait_ge(in_x, 16)
            for t in range(NT):
                ins = nc.vector.bn_stats(stats[:, t, :], x_nat[:, t, :])
            step(ins)
            for t in range(NT):
                ins = nc.vector.bn_aggr(mv[:, t, :], stats[:, t, :])
            ins.then_inc(var_ok, 1)
            dve.wait_ge(rstd_ok, 1)
            for t in range(NT):
                nc.vector.tensor_scalar(xn[:, t, :], x_nat[:, t, :], mv[:, t, 0:1], rstd[:, t:t + 1],
                                        ALU.subtract, ALU.mult).then_inc(xn_ok, 1)
            dve.wait_ge(sil, 1)
            step(nc.vector.tensor_scalar(silu[:, 1:2], silu[:, 0:1], 1.0, None, ALU.add))
            step(nc.vector.reciprocal(silu[:, 2:3], silu[:, 1:2]))
            nc.vector.tensor_tensor(silu[:, 3:4], silu[:, 2:3], cols[:, 0:1], ALU.mult).then_inc(sil, 1)
            dve.wait_ge(mod_ps, 1)
            step(nc.vector.tensor_copy(modc[:, 0:6], ps[:, 0, 0:6]))
            for n, g in enumerate((2, 5)):
                step(nc.vector.tensor_scalar(clampt[:, 0, n:n + 1], modc[:, g:g + 1], 0.0, 2.0, ALU.is_ge, ALU.mult))
                step(nc.vector.tensor_scalar(clampt[:, 1, n:n + 1], clampt[:, 0, n:n + 1], -1.0, None, ALU.add))
                step(nc.vector.tensor_scalar(clampt[:, 2, n:n + 1], modc[:, g:g + 1], -1.0, None, ALU.mult))
                step(nc.vector.tensor_tensor(clampt[:, 3, n:n + 1], modc[:, g:g + 1], clampt[:, 2, n:n + 1], ALU.max))
                step(nc.vector.scalar_tensor_tensor(out=modc[:, g:g + 1], in0=clampt[:, 3, n:n + 1], scalar=0.25,
                                                    in1=clampt[:, 1, n:n + 1], op0=ALU.max, op1=ALU.mult))
                step(nc.vector.tensor_scalar(modc[:, g - 1:g], modc[:, g - 1:g], 1.0, None, ALU.add))
            nc.vector.tensor_copy(silu[:, 0:1], modc[:, 0:1]).then_inc(mod_ok, 1)
            dve.wait_ge(pos_ps, 1)
            for w in range(2):
                nc.vector.tensor_scalar(posT[:, w, :], ps[:, 1 + w, 0:R], cols[:, 3 + w:4 + w], None,
                                        ALU.add).then_inc(pos_ok, 1)
            dve.wait_ge(pos_ok, 2)
            dve.wait_ge(made, 9)
            for w in range(2):
                first = P - 1 + w
                nc.vector.tensor_scalar(ext[:, w, 0:first], ident_fill(zer, first), posT[:, w, 0:1], None, ALU.add)
                nc.vector.tensor_copy(ext[:, w, first:first + R], posT[:, w, :])
                nc.vector.tensor_scalar(ext[:, w, first + R:EXT], ident_fill(zer, EXT - first - R), posT[:, w, R - 1:R],
                                        None, ALU.add).then_inc(ext_ok, 1)
                for e in range(2):
                    col = 0 if e == w else R - 1
                    nc.vector.tensor_scalar(ends[:, w, e, :], head_mask[:], posT[:, w, col:col + 1], None,
                                            ALU.mult).then_inc(ends_ok, 1)
            for b in range(NB):
                dve.wait_ge(xt_ps, b + 1)
                nc.vector.tensor_scalar(hT[:, b * BANK:(b + 1) * BANK], ps[:, 4 + b, :], modc[:, 1:2], modc[:, 0:1],
                                        ALU.mult, ALU.add).then_inc(hT_ok, 1)
            for w in range(2):
                for b in range(NB):
                    dve.wait_ge(qk_ps, NB * w + b + 1)
                    nc.vector.tensor_scalar(qkT[:, w, b * BANK:(b + 1) * BANK], ps[:, b, :], cols[:, 1 + w:2 + w],
                                            None, ALU.add).then_inc(qk_ok, 1)
            dve.wait_ge(qk_ok, 2 * NB)

            def split(out, whole, left, done):
                ins = nc.vector.tensor_copy(out[:, 0, :], whole)
                ins.then_inc(done, 1)
                dve.wait_ge(done, split.n + 1)
                step(nc.vector.tensor_tensor(left, whole, out[:, 0, :], ALU.subtract))
                nc.vector.tensor_copy(out[:, 1, :], left).then_inc(done, 1)
                dve.wait_ge(done, split.n + 2)
                step(nc.vector.tensor_tensor(left, left, out[:, 1, :], ALU.subtract))
                nc.vector.tensor_copy(out[:, 2, :], left).then_inc(done, 1)
                dve.wait_ge(done, split.n + 3)
                split.n += 3

            split.n = 0
            for w in range(2):
                split(part[:, w], qkT[:, w, :], rest[:], parts_ok)
            split.n = 0
            for w in range(2):
                for b in range(NB):
                    dve.wait_ge(aux_ps, NB * w + b + 1)
                    nc.vector.tensor_copy(aux[:, w, b * BANK:(b + 1) * BANK], ps[0:2 * H, 4 + b, :]).then_inc(aux_ok, 1)
                dve.wait_ge(aux_ok, NB * (w + 1))
                split(auxp[:, w], aux[:, w, :], rest[0:2 * H, :], auxp_ok)
            for b in range(NB):
                dve.wait_ge(v_ps, b + 1)
                nc.vector.tensor_copy(keep["v_all"][:, 4 * b:4 * b + 4, :],
                                      ps[:, b, :].rearrange("p (s d) -> p s d", s=4)).then_inc(v_ok, 1)
            nc.vector.tensor_scalar(wog[:], wts[:, 5, :], modc[:, 2:3], None, ALU.mult).then_inc(wog_ok, 1)
            nc.vector.tensor_tensor(cols[:, 6:7], cols[:, 5:6], modc[:, 2:3], ALU.mult).then_inc(wog_ok, 1)
            dve.wait_ge(wo_ps, 1)
            nc.vector.tensor_copy(keep["woT"][:], ps[:, 4, 0:D])
            nc.vector.tensor_copy(keep["bo_row"][:], ps[0:1, 5, 0:D])


def ident_fill(zer, n):
    return zer[:, 0:n]


def attention_phase(nc, keep, scratch):
    ident = keep["ident"]
    with ExitStack() as ctx:
        def sb(name, shape, dt=F32):
            return ctx.enter_context(nc.sbuf_tensor(name, shape, dt))

        def sem(name):
            return keep["semaphores"].enter_context(nc.semaphore(name))

        ring = ctx.enter_context(nc.psum_tensor("at_ring", [P, RING, BANK], F32))
        scores = ctx.enter_context(nc.psum_tensor("at_scores", [P, 2, 2, BANK], F32))
        ctx_ps = ctx.enter_context(nc.psum_tensor("at_ctx", [P, BANK], F32))

        qa, la, ra = (sb(f"at_{n}a", [P, 2, T], BF16) for n in "qlr")
        qb, lb, rb = (sb(f"at_{n}b", [ROWS, 2, T], BF16) for n in "qlr")
        tab = sb("at_tab", [P, 2, TABW])
        diag = sb("at_diag", [P, 2, T])
        class_mask = sb("at_class", [P, CL])
        c2p = sb("at_c2p", [P, 2, NT, P])
        win = sb("at_win", [P, 2, NT, WIN + 2 * SPAN])
        mx = sb("at_mx", [P, NT, 8])
        mrow = sb("at_mrow", [P, 2, NT])
        mpart = sb("at_mpart", [NT, 2, 3, P], BF16)
        mleft = sb("at_mleft", [NT, 2, P])
        onlym = sb("at_onlym", [ROWS, P], BF16)
        prob = sb("at_prob", [P, 4, 2 * BANK])
        vh = sb("at_vh", [P, 2, NT, 32])
        ctx_sb = sb("at_ctx_sb", [P, 2, BANK])

        stack_a = [sem("stack_a0"), sem("stack_a1")]
        stack_b = [sem("stack_b0"), sem("stack_b1")]
        m_rows = [sem("m_rows0"), sem("m_rows1")]
        tab_in, diag_in, made, diag_ok, v_ok = (sem(n) for n in ("tab_in", "diag_in", "at_made", "diag_ok", "vh_ok"))
        unit, c2p_kept, win_kept, win_max, far_max, m_turned, m_split, maxed = (
            sem(n) for n in ("unit", "c2p_kept", "win_kept", "win_max", "far_max", "m_turned", "m_split", "maxed"))
        cleared, m_left = sem("cleared"), sem("m_left")
        score, exped, pv, ctx_kept = (sem(n) for n in ("score", "exped", "pv", "ctx_kept"))
        ctx_out = [sem("ctx_out0"), sem("ctx_out1")]
        block = ctx.enter_context(nc.Block())

        STEPS = NT + 1

        def a_units(s):
            if s < 2:
                return range(N_C2P // 2 * s, N_C2P // 2 * (s + 1))
            if s < 4:
                return range(N_C2P + N_WIN // 2 * (s - 2), N_C2P + N_WIN // 2 * (s - 1))
            if s < NT:
                n = N_FAR * (s - 4) // (NT - 4), N_FAR * (s - 3) // (NT - 4)
                return range(N_C2P + N_WIN + n[0], N_C2P + N_WIN + n[1])
            return range(N_A - 1, N_A)

        def merged(ha, hb):
            for s in range(STEPS):
                us = [("a", n) for n in a_units(s)] if ha is not None else []
                ks = [("b", 2 * (s - 1)), ("b", 2 * (s - 1) + 1)] if hb is not None and s > 0 else []
                n = max(len(us), 1)
                for x in range(n):
                    yield from us[x:x + 1]
                    yield from ks[x * len(ks) // n:(x + 1) * len(ks) // n]

        def iterations(eng, run):
            run(0, 0, None, 1)
            with eng.Fori(0, H // 2 - 1) as pair:
                run(2 * pair + 1, 1, 2 * pair, 0)
                run(2 * pair + 2, 0, 2 * pair + 1, 1)
            run(H - 1, 1, H - 2, 0)
            run(None, 0, H - 1, 1)

        def loads_of(h, p):
            return h - p + 2

        def window_tiles(n):
            q, g = n // 2, n % 2
            first, end = g * GI, (g + 1) * GI
            if q == 0 and g == 0:
                first += 1
            if q == 3 and g == 1:
                end -= 1
            return q, first, end

        @block.sync
        def _(sp):
            def load_tables(h):
                for w in range(2):
                    src = scratch["ext"][w, bass.ds(h * DK, DK), :]
                    sp.dma_start(tab[:, w, :], shifted(src)).then_inc(tab_in, 16)
                for w in range(2):
                    sp.dma_start(diag[:, w, :], repeated(scratch["qk"][w, bass.ds(h * DK, DK), :])).then_inc(diag_in, 16)

            def load_rows(dst, stack, h, rows, done):
                sp.dma_start(dst, scratch[stack][bass.ds(h, 1), 0:rows].rearrange("a r t -> (a r) t")).then_inc(done, 16)

            def load_stacks(h, p, q, l, r, done):
                load_rows(q[0:ROW_M, p, :], "qst", h, ROW_M, done[p])
                load_rows(l[0:ROWS, p, :], "klst", h, ROWS, done[p])
                load_rows(r[0:ROWS, p, :], "krst", h, ROWS, done[p])

            def load_stacks_a(h, p):
                load_stacks(h, p, qa, la, ra, stack_a)
                load_rows(qa[SPAN:SPAN + ROW_QK, p, :], "qst", h, ROW_QK, stack_a[p])
                load_rows(la[SPAN:SPAN + ROW_QK, p, :], "klst", h, ROW_QK, stack_a[p])

            load_stacks_a(0, 0)
            load_tables(0)

            def run(ha, pa, hb, pb):
                if ha is not None and not (isinstance(ha, int) and ha == H - 1):
                    if hb is not None:
                        sp.wait_ge(m_turned, ha)
                    load_stacks_a(ha + 1, 1 - pa)
                if ha is not None:
                    if not isinstance(ha, int) or ha > 1:
                        sp.wait_ge(pv, (ha - 1) * N_B)
                    load_stacks(ha, pa, qb, lb, rb, stack_b)
                    if not (isinstance(ha, int) and ha == H - 1):
                        sp.wait_ge(win_max, (ha + 1) * N_WIN)
                        load_tables(ha + 1)
                    sp.wait_ge(m_split, 3 * (ha + 1))
                    for r in range(3):
                        sp.dma_start(qb[ROW_M + r:ROW_M + r + 1, pa, :].rearrange("a (n q) -> a n q", q=P),
                                     mpart[:, pa, r, :]).then_inc(m_rows[pa], 16)
                if hb is not None:
                    sp.wait_ge(ctx_kept, hb + 1)
                    for g in range(NB):
                        sp.dma_start(scratch["ctx"][bass.ds(hb, 1), :, g * BANK:(g + 1) * BANK].rearrange("a r t -> (a r) t"),
                                     ctx_sb[32 * g:32 * g + DK + 1, pb, :]).then_inc(ctx_out[pb], 16)

            iterations(sp, run)
            for p in range(2):
                sp.wait_ge(ctx_out[p], 16 * NB * (H // 2))

        @block.gpsimd
        def _(pool):
            n_made = 0

            def make(ins):
                nonlocal n_made
                n_made += 1
                ins.then_inc(made, 1)
                pool.wait_ge(made, n_made)

            make(nc.gpsimd.memset(class_mask[:], 1.0))
            make(nc.gpsimd.affine_select(out=class_mask[:], in_=class_mask[:], compare_op=ALU.is_ge, fill=0.0,
                                         base=-DK * (CL - 1), pattern=[[DK, CL]], channel_multiplier=1))
            make(nc.gpsimd.affine_select(out=class_mask[:], in_=class_mask[:], compare_op=ALU.is_ge, fill=0.0,
                                         base=P - 1, pattern=[[-DK, CL]], channel_multiplier=-1))
            make(nc.gpsimd.memset(onlym[:], 1.0))
            make(nc.gpsimd.affine_select(out=onlym[:], in_=onlym[:], compare_op=ALU.is_ge, fill=0.0,
                                         base=-ROW_M, pattern=[[0, P]], channel_multiplier=1))
            make(nc.gpsimd.memset(vh[:], 0.0))
            make(nc.gpsimd.memset(vh[:, :, :, DK:DK + 1], 1.0))
            make(nc.gpsimd.memset(win[:], 0.0))

            def run(ha, pa, hb, pb):
                if ha is None:
                    return
                for w in range(2):
                    pool.wait_ge(diag_in, (ha + 1) * 32)
                    v = diag[:, w, :].rearrange("p (n t) -> p n t", t=CL)
                    nc.gpsimd.tensor_tensor(v, v, class_mask[:, None, :].to_broadcast([P, T // CL, CL]), ALU.mult
                                            ).then_inc(diag_ok, 1)
                if not isinstance(ha, int) or ha > 1:
                    pool.wait_ge(pv, (ha - 1) * N_B)
                nc.gpsimd.tensor_copy(vh[:, pa, :, 0:DK], keep["v_all"][:, :, bass.ds(ha * DK, DK)]).then_inc(v_ok, 1)

            iterations(pool, run)

        @block.tensor
        def _(pe):
            def free_ring(ha, n):
                n -= RING
                if n < 0:
                    if isinstance(ha, int) and ha == 0:
                        return
                    ha, n = ha - 1, n + N_A
                if n < N_C2P:
                    pe.wait_ge(c2p_kept, ha * N_C2P + n + 1)
                elif n < N_C2P + N_WIN:
                    pe.wait_ge(win_kept, ha * N_WIN + n - N_C2P + 1)
                elif n < N_A - 1:
                    pe.wait_ge(far_max, ha * N_FAR + n - N_C2P - N_WIN + 1)
                else:
                    pe.wait_ge(m_split, 3 * (ha + 1))

            def unit_a(ha, pa, n):
                out = ring[:, n % RING, :]
                free_ring(ha, n)
                if n == 0:
                    pe.wait_ge(tab_in, (ha + 1) * 32)
                    pe.wait_ge(diag_ok, (ha + 1) * 2)
                    pe.wait_ge(stack_a[pa], loads_of(ha, pa) * 40)
                if n < N_C2P:
                    half, qh, g = n // 4, n // 2 % 2, n % 2
                    v = out.rearrange("p (i q) -> p i q", q=P // 2)
                    toks = diag[:, 0, g * GI * P:(g + 1) * GI * P].rearrange("p (i q) -> p i q", q=P)
                    for c in range(4):
                        col = KEY0 + P * half - CL * (4 * qh + c)
                        at = P // 2 * qh + CL * c
                        last = nc.tensor.matmul(v[:, :, CL * c:CL * (c + 1)], tab[:, 0, col:col + P],
                                                toks[:, :, at:at + CL], start=(c == 0), stop=True,
                                                skip_group_check=True)
                elif n < N_C2P + N_WIN:
                    q, first, end = window_tiles(n - N_C2P)
                    if n == N_C2P:
                        pe.wait_ge(c2p_kept, (ha + 1) * N_C2P)
                    v = out.rearrange("p (i k) -> p i k", k=SPAN)[:, 0:end - first, :]
                    k0 = P * first - SPAN + SPAN * q
                    for c in range(4):
                        col = QRY0 - CL * (4 * q + c)
                        nc.tensor.matmul(v[:, :, CL * c:CL * (c + 1)], tab[:, 1, col:col + P],
                                         strided(diag[:, 1, k0 + CL * c:k0 + CL * (c + 1)], P, end - first),
                                         start=(c == 0), stop=False, skip_group_check=True)
                    keys = slice(SPAN * (q % 2), SPAN * (q % 2 + 1))
                    rows = slice(keys.start, keys.start + ROW_QK)
                    for i in range(first, end):
                        nc.tensor.matmul(v[:, i - first, :], qa[rows, pa, P * i:P * (i + 1)],
                                         la[rows, pa, P * i - SPAN + SPAN * q:P * i + SPAN * q],
                                         start=False, stop=False, skip_group_check=True)
                    for i in range(first, end):
                        last = nc.tensor.matmul(v[:, i - first, :], c2p[keys, q // 2, i, :], ident[keys, keys],
                                                is_transpose=True, start=False, stop=True, skip_group_check=True)
                elif n < N_A - 1:
                    i, u = divmod(n - N_C2P - N_WIN, FU)
                    for is_left, k, width, col in far_units(i)[u][1]:
                        last = nc.tensor.matmul(out[:, col:col + width], qa[0:ROW_M, pa, P * i:P * (i + 1)],
                                                (la if is_left else ra)[0:ROW_M, pa, k:k + width],
                                                start=True, stop=True, skip_group_check=True)
                else:
                    pe.wait_ge(maxed, ha + 1)
                    last = nc.tensor.transpose(out[0:NT, 0:P], mrow[:, pa, :], ident[:])
                    last.then_inc(m_turned, 1)
                    return
                last.then_inc(unit, 1)

            def scores_b(hb, pb, n):
                j, half = divmod(n, 2)
                if n == 0:
                    pe.wait_ge(stack_b[pb], loads_of(hb, pb) * 24)
                    pe.wait_ge(m_rows[pb], loads_of(hb, pb) * 24)
                    pe.wait_ge(win_kept, (hb + 1) * N_WIN)
                if n >= 2:
                    pe.wait_ge(exped, hb * N_B + n - 1)
                for b in range(2):
                    bank = scores[:, half, b, :]
                    i = first = 4 * (2 * half + b)
                    while i < first + 4:
                        o = P * (i - first)
                        if abs(i - j) <= 1:
                            off = P - P * (i - j)
                            blk = bank[:, o:o + P]
                            nc.tensor.matmul(blk, win[:, pb, i, off:off + P], ident[:], is_transpose=True,
                                             start=True, stop=False, skip_group_check=True)
                            last = nc.tensor.matmul(blk, onlym[:], qb[0:ROWS, pb, P * i:P * (i + 1)],
                                                    start=False, stop=(i == j), skip_group_check=True)
                            if i != j:
                                lo = 0 if i == j + 1 else SPAN
                                last = nc.tensor.matmul(bank[lo:lo + SPAN, o:o + P],
                                                        (lb if i > j else rb)[0:ROW_M, pb, P * j + lo:P * j + lo + SPAN],
                                                        qb[0:ROW_M, pb, P * i:P * (i + 1)],
                                                        start=False, stop=True, skip_group_check=True)
                            i += 1
                        else:
                            e = i
                            while e < first + 4 and abs(e - j) > 1 and (e > j) == (i > j):
                                e += 1
                            last = nc.tensor.matmul(bank[:, o:o + P * (e - i)],
                                                    (lb if i > j else rb)[:, pb, P * j:P * (j + 1)],
                                                    qb[:, pb, P * i:P * e], start=True, stop=True,
                                                    skip_group_check=True)
                            i = e
                last.then_inc(score, 1)

            def values_b(hb, pb, n):
                j, half = divmod(n, 2)
                if n == 0:
                    pe.wait_ge(v_ok, hb + 1)
                    if not (isinstance(hb, int) and hb == 0):
                        pe.wait_ge(ctx_kept, hb)
                pe.wait_ge(exped, hb * N_B + n + 1)
                for b in range(2):
                    g = 2 * half + b
                    last = nc.tensor.matmul(ctx_ps[32 * g:32 * (g + 1), :], vh[:, pb, j, :],
                                            prob[:, n % 4, b * BANK:(b + 1) * BANK], start=(j == 0), stop=(j == NT - 1),
                                            skip_group_check=True)
                last.then_inc(pv, 1)

            pe.wait_ge(made, 8)

            def run(ha, pa, hb, pb):
                for kind, n in merged(ha, hb):
                    if kind == "a":
                        unit_a(ha, pa, n)
                    else:
                        scores_b(hb, pb, n)
                        if n > 0:
                            values_b(hb, pb, n - 1)
                if hb is not None:
                    values_b(hb, pb, N_B - 1)

            iterations(pe, run)

        @block.scalar
        def _(act):
            act.wait_ge(made, 8)

            def run(ha, pa, hb, pb):
                for kind, n in merged(ha, hb):
                    if kind == "b":
                        act.wait_ge(score, hb * N_B + n + 1)
                        act.wait_ge(pv, hb * N_B + max(n - 3, 0))
                        nc.scalar.activation(prob[:, n % 4, :], scores[:, n % 2, :, :].rearrange("p b q -> p (b q)"),
                                             ACT.Exp, scale=SCALE).then_inc(exped, 1)
                    elif n < N_C2P:
                        act.wait_ge(unit, ha * (N_A - 1) + n + 1)
                        if n == 0 and not (isinstance(ha, int) and ha == 0):
                            act.wait_ge(unit, ha * (N_A - 1))
                        half, qh, g = n // 4, n // 2 % 2, n % 2
                        nc.scalar.copy(c2p[:, half, g * GI:(g + 1) * GI, P // 2 * qh:P // 2 * (qh + 1)],
                                       ring[:, n % RING, :].rearrange("p (i q) -> p i q", q=P // 2)
                                       ).then_inc(c2p_kept, 1)
                    elif n < N_C2P + N_WIN:
                        act.wait_ge(unit, ha * (N_A - 1) + n + 1)
                        if n == N_C2P and not (isinstance(ha, int) and ha < 2):
                            act.wait_ge(pv, (ha - 1) * N_B)
                        q, first, end = window_tiles(n - N_C2P)
                        nc.scalar.copy(win[:, pa, first:end, SPAN * (q + 1):SPAN * (q + 2)],
                                       ring[:, n % RING, 0:SPAN * (end - first)].rearrange("p (i k) -> p i k", k=SPAN)
                                       ).then_inc(win_kept, 1)

            iterations(act, run)

        @block.vector
        def _(dve):
            nc.vector.memset(mx[:], -3.0e38).then_inc(cleared, 1)
            dve.wait_ge(cleared, 1)

            def run(ha, pa, hb, pb):
                if ha is not None:
                    for n in range(N_C2P, N_A - 1):
                        if n >= N_C2P + N_WIN:
                            dve.wait_ge(unit, ha * (N_A - 1) + n + 1)
                        if n == N_C2P and not (isinstance(ha, int) and ha == 0):
                            dve.wait_ge(maxed, ha)
                        if n < N_C2P + N_WIN:
                            q, first, end = window_tiles(n - N_C2P)
                            dve.wait_ge(win_kept, ha * N_WIN + n - N_C2P + 1)
                            nc.vector.reduce_max(mx[:, first:end, q], win[:, pa, first:end, SPAN * (q + 1):SPAN * (q + 2)], AX.X).then_inc(win_max, 1)
                        else:
                            i, u = divmod(n - N_C2P - N_WIN, FU)
                            nc.vector.reduce_max(mx[:, i, 4 + u:5 + u], ring[:, n % RING, 0:far_units(i)[u][0]], AX.X
                                                 ).then_inc(far_max, 1)
                    dve.wait_ge(far_max, (ha + 1) * N_FAR)
                    nc.vector.reduce_max(mrow[:, pa, :], mx[:], AX.X).then_inc(maxed, 1)
                    dve.wait_ge(m_turned, ha + 1)
                    if not isinstance(ha, int) or ha > 1:
                        dve.wait_ge(m_rows[pa], (loads_of(ha, pa) - 2) * 24)
                    turned, left = ring[0:NT, (N_A - 1) % RING, 0:P], mleft[:, pa, :]
                    nc.vector.tensor_scalar(mpart[:, pa, 0, :], turned, -1.0, None, ALU.mult).then_inc(m_split, 1)
                    dve.wait_ge(m_split, 3 * ha + 1)
                    nc.vector.scalar_tensor_tensor(out=left, in0=turned, scalar=-1.0, in1=mpart[:, pa, 0, :],
                                                   op0=ALU.mult, op1=ALU.subtract).then_inc(m_left, 1)
                    dve.wait_ge(m_left, 2 * ha + 1)
                    nc.vector.tensor_copy(mpart[:, pa, 1, :], left).then_inc(m_split, 1)
                    dve.wait_ge(m_split, 3 * ha + 2)
                    nc.vector.tensor_tensor(left, left, mpart[:, pa, 1, :], ALU.subtract).then_inc(m_left, 1)
                    dve.wait_ge(m_left, 2 * ha + 2)
                    nc.vector.tensor_copy(mpart[:, pa, 2, :], left).then_inc(m_split, 1)
                if hb is not None:
                    dve.wait_ge(pv, (hb + 1) * N_B)
                    if not isinstance(hb, int) or hb > 1:
                        dve.wait_ge(ctx_out[pb], (loads_of(hb, pb) - 2) * 8 * NB)
                    nc.vector.tensor_copy(ctx_sb[:, pb, :], ctx_ps[:]).then_inc(ctx_kept, 1)

            iterations(dve, run)


def shifted(rows):
    (step, _), _ = rows.ap
    return bass.AP(rows.tensor, rows.offset, [[1, CL], [step, DK], [1, TABW]])


def repeated(rows):
    (step, _), _ = rows.ap
    return bass.AP(rows.tensor, rows.offset, [[0, CL], [step, DK], [1, T]])


def strided(cols, step, n):
    part, (one, w) = cols.ap
    return bass.AP(cols.tensor, cols.offset, [list(part), [step, n], [one, w]])


def output_phase(nc, keep, scratch):
    with ExitStack() as ctx:
        def sb(name, shape, dt=F32):
            return ctx.enter_context(nc.sbuf_tensor(name, shape, dt))

        def sem(name):
            return keep["semaphores"].enter_context(nc.semaphore(name))

        ps = ctx.enter_context(nc.psum_tensor("ou_ps", [P, 8, BANK], F32))
        ctxT = sb("ou_ctxT", [P, T])
        den = sb("ou_den", [H, T])
        spread = sb("ou_spread", [H, P])
        ones_row = sb("ou_ones", [1, P])
        loaded, made, inverse, spread_ps, normed, out_ps, added = (
            sem(n) for n in ("ou_loaded", "ou_made", "inverse", "spread_ps", "normed", "out_ps", "added"))
        block = ctx.enter_context(nc.Block())

        @block.sync
        def _(sp):
            for h in range(H):
                sp.dma_start(ctxT[DK * h:DK * (h + 1), :], scratch["ctx"][h, 0:DK, :]).then_inc(loaded, 16)
            sp.dma_start(den[:], scratch["ctx"][:, DK, :]).then_inc(loaded, 16)

        @block.gpsimd
        def _(pool):
            nc.gpsimd.memset(ones_row[:], 1.0).then_inc(made, 1)
            nc.gpsimd.memset(spread[:], 1.0).then_inc(made, 1)
            pool.wait_ge(made, 2)
            nc.gpsimd.affine_select(out=spread[:], in_=spread[:], compare_op=ALU.is_ge, fill=0.0,
                                    base=0, pattern=[[1, P]], channel_multiplier=-DK).then_inc(made, 1)
            pool.wait_ge(made, 3)
            nc.gpsimd.affine_select(out=spread[:], in_=spread[:], compare_op=ALU.is_ge, fill=0.0,
                                    base=DK - 1, pattern=[[-1, P]], channel_multiplier=DK).then_inc(made, 1)

        @block.tensor
        def _(pe):
            pe.wait_ge(inverse, 1)
            pe.wait_ge(made, 4)
            for b in range(NB):
                nc.tensor.matmul(ps[:, b, :], spread[:], den[:, b * BANK:(b + 1) * BANK],
                                 start=True, stop=True).then_inc(spread_ps, 1)
            for b in range(NB):
                pe.wait_ge(normed, b + 1)
                for s in range(4):
                    t = 4 * b + s
                    o = ps[:, 4 + b, s * P:(s + 1) * P]
                    nc.tensor.matmul(o, ctxT[:, t * P:(t + 1) * P], keep["woT"][:], start=True, stop=False)
                    last = nc.tensor.matmul(o, ones_row[:], keep["bo_row"][:], start=False, stop=True)
                last.then_inc(out_ps, 1)

        @block.vector
        def _(dve):
            dve.wait_ge(loaded, 16 * (H + 1))
            nc.vector.reciprocal(den[:], den[:]).then_inc(inverse, 1)
            for b in range(NB):
                dve.wait_ge(spread_ps, b + 1)
                c = ctxT[:, b * BANK:(b + 1) * BANK]
                nc.vector.tensor_tensor(c, c, ps[:, b, :], ALU.mult).then_inc(normed, 1)
            for b in range(NB):
                dve.wait_ge(out_ps, b + 1)
                c = keep["x_nat"][:, 4 * b:4 * b + 4, :].rearrange("p s d -> p (s d)")
                nc.vector.tensor_tensor(c, c, ps[:, 4 + b, :], ALU.add).then_inc(added, 1)
            dve.wait_ge(added, NB)


DEPTH = 8
NODES = 2 ** DEPTH - 1
LEAVES = 2 ** DEPTH
LW = 16
W1, W2, B1, B2 = 0, LW * D, 2 * LW * D, 2 * LW * D + LW
LEAF_ROW = B2 + D
SCALE_F = float(D ** -0.5)


def norm_phase(nc, keep):
    x_nat, ident, modc = keep["x_nat"], keep["ident"], keep["modc"]
    xf, xfT = keep["xf"], keep["xfT"]
    with ExitStack() as ctx:
        def sb(name, shape, dt=F32):
            return ctx.enter_context(nc.sbuf_tensor(name, shape, dt))

        def sem(name):
            return keep["semaphores"].enter_context(nc.semaphore(name))

        ps = ctx.enter_context(nc.psum_tensor("no_ps", [P, 8, BANK], F32))
        stats = sb("no_stats", [P, NT, 6])
        mv = sb("no_mv", [P, 2, NT, 2])
        rstd = sb("no_rstd", [P, 2, NT])
        expo = sb("no_expo", [P, 2, NT])
        mod_rows = sb("no_mod", [P, 2, D])
        h2 = sb("no_h2", [P, NT, D])
        rows_ps, vec, var_ok, rstd_ok, pooled, turned = (
            sem(n) for n in ("rows_ps", "no_vec", "no_var_ok", "no_rstd_ok", "pooled", "turned"))
        xf_ok, xfT_ok = sem("xf_ok"), sem("xfT_ok")
        block = ctx.enter_context(nc.Block())

        @block.gpsimd
        def _(pool):
            n_pooled = 0

            def step(ins):
                nonlocal n_pooled
                n_pooled += 1
                ins.then_inc(pooled, 1)
                pool.wait_ge(pooled, n_pooled)

            step(nc.gpsimd.memset(expo[:, 0, :], -0.5))
            step(nc.gpsimd.memset(expo[:, 1, :], 0.5))
            pool.wait_ge(var_ok, 1)
            step(nc.gpsimd.tensor_scalar(rstd[:, 0, :], mv[:, 0, :, 1], EPS, None, ALU.add))
            nc.gpsimd.tensor_tensor(rstd[:, 0, :], rstd[:, 0, :], expo[:, 0, :], ALU.pow).then_inc(rstd_ok, 1)
            pool.wait_ge(var_ok, 2)
            step(nc.gpsimd.tensor_scalar(rstd[:, 1, :], mv[:, 1, :, 1], D / (D - 1.0), None, ALU.mult))
            step(nc.gpsimd.tensor_tensor(rstd[:, 1, :], rstd[:, 1, :], expo[:, 1, :], ALU.pow))
            step(nc.gpsimd.tensor_scalar(rstd[:, 1, :], rstd[:, 1, :], EPS, None, ALU.add))
            nc.gpsimd.tensor_tensor(rstd[:, 1, :], rstd[:, 1, :], expo[:, 0, :], ALU.pow).then_inc(rstd_ok, 1)

        @block.tensor
        def _(pe):
            for n, col in enumerate((4, 3)):
                last = nc.tensor.matmul(ps[:, 0, n * D:(n + 1) * D], modc[:, col:col + 1].to_broadcast([P, P]),
                                        ident[:], start=True, stop=True)
            last.then_inc(rows_ps, 1)
            for t in range(NT):
                pe.wait_ge(xf_ok, t + 1)
                last = nc.tensor.transpose(ps[:, 4 + t // 4, t % 4 * P:(t % 4 + 1) * P], xf[:, t, :], ident[:])
                if t % 4 == 3:
                    last.then_inc(turned, 1)

        @block.vector
        def _(dve):
            n_vec = 0

            def step(ins):
                nonlocal n_vec
                n_vec += 1
                ins.then_inc(vec, 1)
                dve.wait_ge(vec, n_vec)

            def statistics(x, r):
                for t in range(NT):
                    ins = nc.vector.bn_stats(stats[:, t, :], x[:, t, :])
                step(ins)
                for t in range(NT):
                    ins = nc.vector.bn_aggr(mv[:, r, t, :], stats[:, t, :])
                ins.then_inc(var_ok, 1)
                dve.wait_ge(rstd_ok, r + 1)

            statistics(x_nat, 0)
            dve.wait_ge(rows_ps, 1)
            nc.vector.tensor_copy(mod_rows[:].rearrange("p a d -> p (a d)"), ps[:, 0, 0:2 * D])
            for t in range(NT):
                ins = nc.vector.tensor_scalar(h2[:, t, :], x_nat[:, t, :], mv[:, 0, t, 0:1], rstd[:, 0, t:t + 1],
                                              ALU.subtract, ALU.mult)
            step(ins)
            for n, op in enumerate((ALU.mult, ALU.add)):
                step(nc.vector.tensor_tensor(h2[:], h2[:], mod_rows[:, n:n + 1, :].to_broadcast([P, NT, D]), op))
            statistics(h2, 1)
            for t in range(NT):
                nc.vector.tensor_scalar(xf[:, t, :], h2[:, t, :], mv[:, 1, t, 0:1], rstd[:, 1, t:t + 1],
                                        ALU.subtract, ALU.mult).then_inc(xf_ok, 1)
            for b in range(NB):
                dve.wait_ge(turned, b + 1)
                nc.vector.tensor_copy(xfT[:, b * BANK:(b + 1) * BANK], ps[:, 4 + b, :]).then_inc(xfT_ok, 1)
            dve.wait_ge(xfT_ok, NB)


def route_phase(nc, a, keep, trees, srcT, leaf):
    tag = trees[0]
    with ExitStack() as ctx:
        def sb(name, shape, dt=F32):
            return ctx.enter_context(nc.sbuf_tensor(f"ro_{tag}_{name}", shape, dt))

        def sem(name):
            return keep["semaphores"].enter_context(nc.semaphore(f"ro_{tag}_{name}"))

        ps = ctx.enter_context(nc.psum_tensor(f"ro_{tag}_ps", [P, 8, BANK], F32))
        nw = sb("nw", [P, len(trees), NODES])
        nb = sb("nb", [P, len(trees), 2])
        paths = sb("paths", [P, 2, LEAVES], BF16)
        turns = sb("turns", [P, 2])
        number = sb("number", [P, 2], BF16)
        went = sb("went", [P, 2, 2, BANK], BF16)
        hit = sb("hit", [P, 2, 2, BANK], BF16)
        loaded, logits, decided, counted, found, numbered, kept = (
            sem(n) for n in ("loaded", "logits", "decided", "counted", "found", "numbered", "kept"))
        block = ctx.enter_context(nc.Block())
        steps = [(n, b) for n in range(len(trees)) for b in range(NB)]
        chunk = (P, NODES - P)

        @block.sync
        def _(sp):
            for n, tree in enumerate(trees):
                sp.dma_start(nw[:, n, :], a[f"{tree}_nwT"]).then_inc(loaded, 16)
                for c in range(2):
                    sp.dma_start(nb[0:chunk[c], n, c:c + 1], a[f"{tree}_nb"][c * P:c * P + chunk[c], :]
                                 ).then_inc(loaded, 16)
            for c in range(2):
                sp.dma_start(paths[0:chunk[c], c, :], a["paths"][c * P:c * P + chunk[c], :]).then_inc(loaded, 16)
            sp.dma_start(turns[:], a["turns"]).then_inc(loaded, 16)
            sp.dma_start(number[:], a["number"]).then_inc(loaded, 16)
        n_loaded = 3 * len(trees) + 4

        @block.tensor
        def _(pe):
            pe.wait_ge(loaded, 16 * n_loaded)

            def decide(k):
                n, b = steps[k]
                if k >= 1:
                    pe.wait_ge(decided, 2 * k)
                for c in range(2):
                    last = nc.tensor.matmul(ps[0:chunk[c], c, :], nw[:, n, c * P:c * P + chunk[c]],
                                            srcT[:, b * BANK:(b + 1) * BANK], start=True, stop=True)
                last.then_inc(logits, 1)

            def count(k):
                pe.wait_ge(decided, 2 * (k + 1))
                if k >= 1:
                    pe.wait_ge(found, 2 * k)
                for c in range(2):
                    for m in range(2):
                        last = nc.tensor.matmul(ps[:, 2 + c, :], paths[0:chunk[m], m, c * P:(c + 1) * P],
                                                went[0:chunk[m], k % 2, m, :], start=(m == 0), stop=(m == 1))
                last.then_inc(counted, 1)

            def name(k):
                n, b = steps[k]
                pe.wait_ge(found, 2 * (k + 1))
                for s in range(4):
                    at = n * NT + 4 * b + s
                    for c in range(2):
                        last = nc.tensor.matmul(ps[:, 4, at:at + 1], hit[:, k % 2, c, s * P:(s + 1) * P],
                                                number[:, c:c + 1], start=(c == 0), stop=(c == 1),
                                                skip_group_check=True)
                last.then_inc(numbered, 1)

            for k in range(len(steps)):
                decide(k)
                if k >= 1:
                    name(k - 1)
                count(k)
            name(len(steps) - 1)

        @block.vector
        def _(dve):
            dve.wait_ge(loaded, 16 * n_loaded)

            for k, (n, b) in enumerate(steps):
                dve.wait_ge(logits, k + 1)
                if k >= 2:
                    dve.wait_ge(counted, k - 1)
                for c in range(2):
                    nc.vector.tensor_scalar(went[0:chunk[c], k % 2, c, :], ps[0:chunk[c], c, :],
                                            nb[0:chunk[c], n, c:c + 1], 0.0, ALU.add, ALU.is_gt).then_inc(decided, 1)
                dve.wait_ge(counted, k + 1)
                if k >= 2:
                    dve.wait_ge(numbered, k - 1)
                for c in range(2):
                    nc.vector.tensor_scalar(hit[:, k % 2, c, :], ps[:, 2 + c, :], turns[:, c:c + 1], None,
                                            ALU.is_equal).then_inc(found, 1)
            dve.wait_ge(numbered, len(steps))
            nc.vector.tensor_copy(leaf[:].rearrange("p n t -> p (n t)"), ps[:, 4, 0:len(trees) * NT]).then_inc(kept, 1)
            dve.wait_ge(kept, 1)


ACT_PART = 8
SLOTS = 3


def leaves_phase(nc, a, trees, keep, leaf, out=None):
    tag, N = trees[0], len(trees)
    ident, x = keep["ident"], keep["xf"]
    with ExitStack() as ctx:
        def sb(name, shape, dt=F32):
            return ctx.enter_context(nc.sbuf_tensor(f"le_{tag}_{name}", shape, dt))

        def sem(name):
            return keep["semaphores"].enter_context(nc.semaphore(f"le_{tag}_{name}"))

        def sems(name):
            return [sem(f"{name}{s}") for s in range(SLOTS)]

        ps = ctx.enter_context(nc.psum_tensor(f"le_{tag}_ps", [P, 8, BANK], F32))
        rows = sb("rows", [P, SLOTS, LEAF_ROW])
        index = sb("index", [P, SLOTS], I32)
        prod1 = sb("prod1", [P, LW, D])
        prod2 = sb("prod2", [P, SLOTS, LW, D])
        hid = sb("hid", [P, SLOTS, 3, LW])
        mixT = sb("mixT", [P, SLOTS, D])
        outs = sb("outs", [P, SLOTS, D])
        gathered, summed, kept, added, stored = (sems(n) for n in ("gathered", "summed", "kept", "added", "stored"))
        indexed, asked, multiplied, reduced, biased, active, scaled_dve, scaled_act, back = (
            sem(n) for n in ("indexed", "asked", "multiplied", "reduced", "biased", "active", "scaled_dve",
                             "scaled_act", "back"))
        block = ctx.enter_context(nc.Block())

        def each(run, eng):
            steps, rest = (NT, 0) if N == SLOTS else divmod(NT, SLOTS)

            def work(k, n):
                return [(s, s, k) if N == SLOTS else (s, 0, SLOTS * k + s) for s in range(n)]

            with eng.Fori(0, steps) as k:
                run(k, work(k, SLOTS))
            if rest:
                run(steps, work(steps, rest))

        @block.gpsimd
        def _(pool):
            def run(k, work):
                for s, n, t in work:
                    pool.wait_ge(summed[s], k)
                    nc.gpsimd.tensor_copy(index[:, s:s + 1], leaf[:, n, bass.ds(t, 1)]).then_inc(indexed, 1)
                    pool.wait_ge(indexed, SLOTS * k + s + 1)
                    pool.sem_inc(asked, 1)
                    nc.gpsimd.indirect_dma_start(rows[:, s, :], None, a[f"{trees[n]}_leaves"],
                                                 bass.IndirectOffsetOnAxis(ap=index[:, s:s + 1], axis=0)
                                                 ).then_inc(gathered[s], 16)

            each(run, pool)

        @block.vector
        def _(dve):
            def run(k, work):
                for s, n, t in work:
                    row = rows[:, s, :]
                    dve.wait_ge(gathered[s], 16 * k + 16)
                    dve.wait_ge(reduced, SLOTS * k + s)
                    nc.vector.tensor_tensor(prod1[:], row[:, W1:W2].rearrange("p (l d) -> p l d", d=D),
                                            x[:, bass.ds(t, 1), :].to_broadcast([P, LW, D]), ALU.mult
                                            ).then_inc(multiplied, 1)
                    dve.wait_ge(multiplied, SLOTS * k + s + 1)
                    nc.vector.tensor_reduce(hid[:, s, 0, :], prod1[:], AX.X, ALU.add).then_inc(reduced, 1)
                    dve.wait_ge(reduced, SLOTS * k + s + 1)
                    nc.vector.tensor_tensor(hid[:, s, 1, :], hid[:, s, 0, :], row[:, B1:B2], ALU.add
                                            ).then_inc(biased, 1)
                    if out is None:
                        dve.wait_ge(biased, SLOTS * k + s + 1)
                        nc.vector.tensor_scalar(hid[:, s, 2, :], hid[:, s, 1, :], 0.0, None, ALU.max
                                                ).then_inc(active, 1)
                    dve.wait_ge(active, SLOTS * k + s + 1)
                    for l in range(ACT_PART, LW):
                        ins = nc.vector.tensor_scalar(prod2[:, s, l, :], row[:, W2 + l * D:W2 + (l + 1) * D],
                                                      hid[:, s, 2, l:l + 1], None, ALU.mult)
                    ins.then_inc(scaled_dve, 1)
                if out is not None:
                    for s, n, t in work:
                        dve.wait_ge(back, SLOTS * k + s + 1)
                        dve.wait_ge(stored[s], 16 * k)
                        nc.vector.tensor_tensor(outs[:, s, :], ps[:, SLOTS + s, 0:D],
                                                keep["x_nat"][:, bass.ds(t, 1), :].rearrange("p a d -> p (a d)"),
                                                ALU.add).then_inc(added[s], 1)

            each(run, dve)

        @block.scalar
        def _(act):
            def run(k, work):
                for s, n, t in work:
                    row = rows[:, s, :]
                    if out is not None:
                        act.wait_ge(biased, SLOTS * k + s + 1)
                        nc.scalar.activation(hid[:, s, 2, :], hid[:, s, 1, :], ACT.Gelu).then_inc(active, 1)
                    act.wait_ge(active, SLOTS * k + s + 1)
                    for l in range(ACT_PART):
                        ins = nc.scalar.mul(prod2[:, s, l, :], row[:, W2 + l * D:W2 + (l + 1) * D],
                                            hid[:, s, 2, l:l + 1])
                    ins.then_inc(scaled_act, 1)
                for s, n, t in work:
                    act.wait_ge(summed[s], k + 1)
                    if out is not None:
                        nc.scalar.mul(mixT[:, s, :], ps[:, s, 0:D], keep["modc"][:, 5:6]).then_inc(kept[s], 1)
                    else:
                        nc.scalar.copy(keep["qkvT"][:, n, bass.ds(t * P, P)], ps[:, s, 0:D]).then_inc(kept[s], 1)

            each(run, act)

        @block.tensor
        def _(pe):
            def run(k, work):
                for s, n, t in work:
                    pe.wait_ge(scaled_dve, SLOTS * k + s + 1)
                    pe.wait_ge(scaled_act, SLOTS * k + s + 1)
                    pe.wait_ge(kept[s], k)
                    o = ps[:, s, 0:D]
                    for l in range(LW):
                        nc.tensor.matmul(o, prod2[:, s, l, :], ident[:], is_transpose=True, start=(l == 0), stop=False)
                    end = nc.tensor.matmul(o, rows[:, s, B2:B2 + D], ident[:], is_transpose=True, start=False,
                                           stop=(out is None))
                    if out is not None:
                        end = nc.tensor.matmul(o, ident[:], keep["xfT"][:, bass.ds(t * P, P)], start=False, stop=True)
                    end.then_inc(summed[s], 1)
                if out is not None:
                    for s, n, t in work:
                        pe.wait_ge(kept[s], k + 1)
                        pe.wait_ge(added[s], k)
                        nc.tensor.transpose(ps[:, SLOTS + s, 0:D], mixT[:, s, :], ident[:]).then_inc(back, 1)

            each(run, pe)

        if out is not None:
            @block.sync
            def _(sp):
                def run(k, work):
                    for s, n, t in work:
                        sp.wait_ge(added[s], k + 1)
                        sp.dma_start(out[0, bass.ds(t * P, P), :], outs[:, s, :]).then_inc(stored[s], 16)

                each(run, sp)
                for s in range(SLOTS):
                    sp.wait_ge(stored[s], 16 * len(range(s, NT, SLOTS)))


def attend_phase(nc, keep):
    ident, qkvT, xf, xfT = keep["ident"], keep["qkvT"], keep["xf"], keep["xfT"]
    with ExitStack() as ctx:
        def sb(name, shape, dt=F32):
            return ctx.enter_context(nc.sbuf_tensor(f"fa_{name}", shape, dt))

        def sem(name):
            return keep["semaphores"].enter_context(nc.semaphore(f"fa_{name}"))

        scores = ctx.enter_context(nc.psum_tensor("fa_scores", [P, NB, BANK], F32))
        turn = ctx.enter_context(nc.psum_tensor("fa_turn", [P, 2, BANK], F32))
        mixed = ctx.enter_context(nc.psum_tensor("fa_mixed", [P, 2, BANK], F32))
        v = sb("v", [P, NT, D])
        q = sb("q", [P, 2, P])
        prob = sb("prob", [P, 2, T])
        probT = sb("probT", [P, 2, NT, P])
        top = sb("top", [P, 2, 4])
        den = sb("den", [P, 2, 2])
        v_ps, v_ok, q_ok, scored, half_max, max_ok, neg_ok, exped, turned, kept_act, kept_dve, mixed_ok, inv_ok, y_ok = (
            sem(n) for n in ("v_ps", "v_ok", "q_ok", "scored", "half_max", "max_ok", "neg_ok", "exped", "turned",
                             "kept_act", "kept_dve", "mixed", "inv_ok", "y_ok"))
        yT_ps, yT_ok = sem("yT_ps"), sem("yT_ok")
        block = ctx.enter_context(nc.Block())

        def iterations(eng, run):
            run(0, 0, None, 1)
            with eng.Fori(0, NT // 2 - 1) as pair:
                run(2 * pair + 1, 1, 2 * pair, 0)
                run(2 * pair + 2, 0, 2 * pair + 1, 1)
            run(NT - 1, 1, NT - 2, 0)
            run(None, 0, NT - 1, 1)

        @block.gpsimd
        def _(pool):
            def run(i, p, _j, _p):
                if i is None:
                    return
                if not isinstance(i, int) or i > 1:
                    pool.wait_ge(scored, NB * (i - 1))
                nc.gpsimd.tensor_copy(q[:, p, :], qkvT[:, 0, bass.ds(i * P, P)]).then_inc(q_ok, 1)

            iterations(pool, run)

        @block.tensor
        def _(pe):
            for g in range(4):
                if g >= 2:
                    pe.wait_ge(v_ok, g - 1)
                for s in range(4):
                    t = 4 * g + s
                    last = nc.tensor.transpose(turn[:, g % 2, s * P:(s + 1) * P], qkvT[:, 2, t * P:(t + 1) * P], ident[:])
                last.then_inc(v_ps, 1)
            pe.wait_ge(v_ok, 4)

            def run(i, p, j, pj):
                if i is not None:
                    pe.wait_ge(q_ok, i + 1)
                    pe.wait_ge(exped, i)
                    for b in range(NB):
                        nc.tensor.matmul(scores[:, b, :], q[:, p, :], qkvT[:, 1, b * BANK:(b + 1) * BANK],
                                         start=True, stop=True).then_inc(scored, 1)
                if j is not None:
                    pe.wait_ge(exped, j + 1)
                    for g in range(4):
                        if g < 2:
                            pe.wait_ge(kept_dve, 2 * j)
                        else:
                            pe.wait_ge(kept_act, 2 * j + g - 1)
                        for s in range(4):
                            t = 4 * g + s
                            last = nc.tensor.transpose(turn[:, g % 2, s * P:(s + 1) * P], prob[:, pj, t * P:(t + 1) * P],
                                                       ident[:])
                        last.then_inc(turned, 1)
                    pe.wait_ge(y_ok, j)
                    for t in range(NT):
                        if t % 4 == 0:
                            g = t // 4
                            pe.wait_ge(kept_act if g < 2 else kept_dve, 2 * j + g % 2 + 1)
                        last = nc.tensor.matmul(mixed[:, pj, 0:D], probT[:, pj, t, :], v[:, t, :],
                                                start=(t == 0), stop=(t == NT - 1))
                    last.then_inc(mixed_ok, 1)

            iterations(pe, run)
            for g in range(4):
                pe.wait_ge(y_ok, NT)
                for s in range(4):
                    t = 4 * g + s
                    last = nc.tensor.transpose(scores[:, g, s * P:(s + 1) * P], xf[:, t, :], ident[:])
                last.then_inc(yT_ps, 1)

        @block.scalar
        def _(act):
            def run(i, p, j, pj):
                if j is not None:
                    for g in range(2):
                        act.wait_ge(turned, 4 * j + g + 1)
                        if g == 0:
                            act.wait_ge(mixed_ok, j)
                        nc.scalar.copy(probT[:, pj, 4 * g:4 * g + 4, :].rearrange("p s q -> p (s q)"), turn[:, g, :]
                                       ).then_inc(kept_act, 1)
                if i is not None:
                    act.wait_ge(neg_ok, i + 1)
                    if not isinstance(i, int) or i > 1:
                        act.wait_ge(turned, 4 * (i - 1))
                        act.wait_ge(y_ok, i - 1)
                    nc.scalar.activation(prob[:, p, :], scores[:].rearrange("p b k -> p (b k)"), ACT.Exp,
                                         bias=top[:, p, 3:4], scale=SCALE_F, accum_out=den[:, p, 0:1]).then_inc(exped, 1)

            iterations(act, run)

        @block.vector
        def _(dve):
            for g in range(4):
                dve.wait_ge(v_ps, g + 1)
                nc.vector.tensor_copy(v[:, 4 * g:4 * g + 4, :].rearrange("p s d -> p (s d)"), turn[:, g % 2, :]
                                      ).then_inc(v_ok, 1)

            def run(i, p, j, pj):
                if i is not None:
                    if not isinstance(i, int) or i > 1:
                        dve.wait_ge(exped, i - 1)
                    for half in range(2):
                        dve.wait_ge(scored, NB * i + 2 * half + 2)
                        nc.vector.tensor_reduce(top[:, p, half:half + 1], scores[:, 2 * half:2 * half + 2, :], AX.XY,
                                                ALU.max).then_inc(half_max, 1)
                    dve.wait_ge(half_max, 2 * i + 2)
                    nc.vector.tensor_tensor(top[:, p, 2:3], top[:, p, 0:1], top[:, p, 1:2], ALU.max).then_inc(max_ok, 1)
                    dve.wait_ge(max_ok, i + 1)
                    nc.vector.tensor_scalar(top[:, p, 3:4], top[:, p, 2:3], -SCALE_F, None, ALU.mult).then_inc(neg_ok, 1)
                if j is not None:
                    for g in range(2, 4):
                        dve.wait_ge(turned, 4 * j + g + 1)
                        if g == 2:
                            dve.wait_ge(mixed_ok, j)
                        nc.vector.tensor_copy(probT[:, pj, 4 * g:4 * g + 4, :].rearrange("p s q -> p (s q)"),
                                              turn[:, g - 2, :]).then_inc(kept_dve, 1)
                    dve.wait_ge(exped, j + 1)
                    nc.vector.reciprocal(den[:, pj, 1:2], den[:, pj, 0:1]).then_inc(inv_ok, 1)
                    dve.wait_ge(inv_ok, j + 1)
                    dve.wait_ge(mixed_ok, j + 1)
                    tile = xf[:, bass.ds(j, 1), :].rearrange("p a d -> p (a d)")
                    nc.vector.scalar_tensor_tensor(out=tile, in0=mixed[:, pj, 0:D], scalar=den[:, pj, 1:2], in1=tile,
                                                   op0=ALU.mult, op1=ALU.add).then_inc(y_ok, 1)

            iterations(dve, run)
            for g in range(4):
                dve.wait_ge(yT_ps, g + 1)
                nc.vector.tensor_copy(xfT[:, g * BANK:(g + 1) * BANK], scores[:, g, :]).then_inc(yT_ok, 1)
            dve.wait_ge(yT_ok, 4)


def feed_forward_phase(nc, a, keep, out):
    with ExitStack() as ctx:
        def sb(name, shape, dt=F32):
            return ctx.enter_context(nc.sbuf_tensor(name, shape, dt))

        keep["xf"] = sb("xf", [P, NT, D])
        keep["xfT"] = sb("xfT", [P, T])
        keep["qkvT"] = sb("qkvT", [P, 3, T])
        leaf = sb("leaf", [P, 4, NT], I32)
        norm_phase(nc, keep)
        route_phase(nc, a, keep, ("q", "k", "v"), keep["xfT"], leaf[:, 0:3, :])
        leaves_phase(nc, a, ("q", "k", "v"), keep, leaf[:, 0:3, :])
        attend_phase(nc, keep)
        route_phase(nc, a, keep, ("f",), keep["xfT"], leaf[:, 3:4, :])
        leaves_phase(nc, a, ("f",), keep, leaf[:, 3:4, :], out)


def adaln_block(nc, a, out):
    with ExitStack() as ctx:
        def sb(name, shape, dt=F32):
            return ctx.enter_context(nc.sbuf_tensor(name, shape, dt))

        keep = {
            "semaphores": ctx,
            "x_nat": sb("x_nat", [P, NT, D]),
            "ident": sb("ident", [P, P]),
            "modc": sb("modc", [P, 8]),
            "woT": sb("woT", [P, D]),
            "bo_row": sb("bo_row", [1, D]),
        }
        scratch = {
            "ext": nc.dram_tensor("ext_scratch", [2, P, EXT], F32, kind="Internal").ap(),
            "qk": nc.dram_tensor("qk_scratch", [2, P, T], F32, kind="Internal").ap(),
            "qst": nc.dram_tensor("q_stack", [H, ROW_M, T], BF16, kind="Internal").ap(),
            "klst": nc.dram_tensor("k_left_stack", [H, ROWS, T], BF16, kind="Internal").ap(),
            "krst": nc.dram_tensor("k_right_stack", [H, ROWS, T], BF16, kind="Internal").ap(),
            "ctx": nc.dram_tensor("context", [H, DK + 1, T], F32, kind="Internal").ap(),
        }
        with ExitStack() as inner:
            keep["v_all"] = inner.enter_context(nc.sbuf_tensor("v_all", [P, NT, D], F32))
            setup_phase(nc, a, keep, scratch)
            attention_phase(nc, keep, scratch)
        output_phase(nc, keep, scratch)
        feed_forward_phase(nc, a, keep, out)


_OUT = (1, T, D)


def path_constants():
    paths = np.zeros((NODES, LEAVES), np.float32)
    turns = np.zeros((LEAVES, 1), np.float32)
    for leaf in range(LEAVES):
        for level in range(DEPTH):
            right = leaf >> (DEPTH - 1 - level) & 1
            paths[2 ** level - 1 + (leaf >> (DEPTH - level)), leaf] = 1 if right else -1
            turns[leaf] += right
    number = np.arange(LEAVES, dtype=np.float32).reshape(2, P).T
    return paths, np.ascontiguousarray(turns.reshape(2, P).T), np.ascontiguousarray(number)


def kernel(**inputs):
    import concourse.bacc as _bacc
    import ml_dtypes as _ml
    from concourse.bass_utils import run_bass_kernel_spmd as _run

    def given(name):
        return np.asarray(inputs[f"L0_{name}"])

    lay = {"x": given("attn_x"), "wmod": given("wmod"), "Wo": given("attn_Wo")}
    for w in ("Wq", "Wk", "Wv", "Wpk", "Wpq"):
        lay[w + "T"] = given("attn_" + w).T
    lay["relT"] = given("attn_rel_emb").T
    lay["relT_rev"] = given("attn_rel_emb")[::-1].T
    lay["c"] = given("c").reshape(D, 1)
    for b in ("bq", "bk", "bpk", "bpq", "bo"):
        lay[b] = given("attn_" + b).reshape(D, 1)
    lay["bv"] = given("attn_bv").reshape(1, D)
    for tree in "qkvf":
        w1, b1, w2, b2 = (given(f"ffn_{tree}_{n}") for n in ("w1", "b1", "w2", "b2"))
        lay[f"{tree}_leaves"] = np.concatenate(
            [w1.transpose(0, 2, 1).reshape(LEAVES, LW * D), w2.reshape(LEAVES, LW * D), b1, b2], axis=1)
        lay[f"{tree}_nwT"] = given(f"ffn_{tree}_nw").T
        lay[f"{tree}_nb"] = given(f"ffn_{tree}_nb").reshape(NODES, 1)
    paths, turns, number = path_constants()
    lay["paths"], lay["turns"], lay["number"] = paths.astype(_ml.bfloat16), turns, number.astype(_ml.bfloat16)

    nc = _bacc.Bacc("TRN2", target_bir_lowering=False, num_devices=1)
    arrays, a = {}, {}
    for name, value in lay.items():
        arrays[f"in_{name}"] = value = np.ascontiguousarray(value)
        a[name] = nc.dram_tensor(f"in_{name}", value.shape, mybir.dt.from_np(value.dtype), kind="ExternalInput").ap()
    out = nc.dram_tensor("out_0", _OUT, F32, kind="ExternalOutput").ap()
    adaln_block(nc, a, out)
    r = _run(nc, [arrays], core_ids=[0])
    return r.results[0]["out_0"]
```

```python
from contextlib import ExitStack

import numpy as np

import concourse.bass as bass
from concourse import mybir

ALU = mybir.AluOpType
ACT = mybir.ActivationFunctionType
AX = mybir.AxisListType
F32 = mybir.dt.float32
BF16 = mybir.dt.bfloat16
I32 = mybir.dt.int32

P = 128
D = 128
T = 2048
NT = T // P
BANK = 512
NB = T // BANK
H = 16
DK = D // H
SPAN = 64
R = 2 * SPAN
SCALE = float((3 * DK) ** -0.5)
EPS = 1e-5

PART_A = (0, 0, 1, 1, 0, 2)
PART_B = (0, 1, 0, 1, 2, 0)
ROW_QK = len(PART_A) * DK
ROW_CL = ROW_QK
ROW_CR = ROW_CL + 3
ROW_S = ROW_CR + 3
ROW_M = ROW_S + 3
ROWS = ROW_M + 3

CL = P // DK
WIN = 2 * P
EXT = WIN + P - 1
TABW = EXT - CL + 1
KEY0 = P - CL
QRY0 = WIN - CL


def near_far(i):
    lo, hi = max(P * i - SPAN, 0), min(P * i - SPAN + WIN, T)
    return (lo, hi), (0, lo), (hi, T)


def far_units(i):
    _, left, right = near_far(i)
    pieces = [(True, *left), (False, *right)]
    total = sum(b - a for _, a, b in pieces)
    size = total // FU
    units = []
    for u in range(FU):
        a, b, at, unit = u * size, (u + 1) * size, 0, []
        for is_left, p, q in pieces:
            s, e = max(a, at), min(b, at + q - p)
            if e > s:
                unit.append((is_left, p + s - at, e - s, s - a))
            at += q - p
        units.append((size, unit))
    return units


FU = 4
N_C2P = 8
N_WIN = 8
N_FAR = NT * FU
N_A = N_C2P + N_WIN + N_FAR + 1
RING = 3
assert N_A % RING == 0
FIRST_SHARE, LAST_SHARE = 1.5, 0.3
N_B = 2 * NT
GI = NT // 2


def setup_phase(nc, a, keep, scratch):
    x_nat, ident, modc, x_all = keep["x_nat"], keep["ident"], keep["modc"], None
    with ExitStack() as ctx:
        def sb(name, shape, dt=F32):
            return ctx.enter_context(nc.sbuf_tensor(name, shape, dt))

        def sem(name):
            return keep["semaphores"].enter_context(nc.semaphore(name))

        ps = ctx.enter_context(nc.psum_tensor("su_ps", [P, 8, BANK], F32))
        wmod = sb("su_wmod", [P, 6 * D])
        wts = sb("su_wts", [P, 6, D])
        rel = sb("su_rel", [P, 2, R])
        cols = sb("su_cols", [P, 8])
        bvrow = sb("su_bvrow", [1, D])
        ones_row = sb("su_ones_row", [1, P])
        silu = sb("su_silu", [P, 4])
        stats = sb("su_stats", [P, NT, 6])
        mv = sb("su_mv", [P, NT, 2])
        rstd = sb("su_rstd", [P, NT])
        expo = sb("su_expo", [P, NT])
        xn = sb("su_xn", [P, NT, D])
        hT = sb("su_hT", [P, T])
        qkT = sb("su_qkT", [P, 2, T])
        posT = sb("su_posT", [P, 2, R])
        ext = sb("su_ext", [P, 2, EXT])
        head_mask = sb("su_hm", [P, H])
        ends = sb("su_ends", [P, 2, 2, H])
        aux = sb("su_aux", [2 * H, 2, T])
        rest = sb("su_rest", [P, T])
        part = sb("su_part", [P, 2, 3, T], BF16)
        auxp = sb("su_auxp", [2 * H, 2, 3, T], BF16)
        oz = sb("su_oz", [H, 2, T], BF16)
        zer = sb("su_zer", [P, P])
        clampt = sb("su_clamp", [P, 4, 2])
        wog = sb("su_wog", [P, D])

        in_x, in_w, in_small = sem("in_x"), sem("in_w"), sem("in_small")
        made, vec, sil = sem("made"), sem("vec"), sem("sil")
        mod_ps, xt_ps, pos_ps, qk_ps, aux_ps, v_ps, wo_ps = (
            sem(n) for n in ("mod_ps", "xt_ps", "pos_ps", "qk_ps", "aux_ps", "v_ps", "wo_ps"))
        xn_ok, hT_ok, pos_ok, qk_ok, ends_ok, wog_ok, v_ok, mod_ok = (
            sem(n) for n in ("xn_ok", "hT_ok", "pos_ok", "qk_ok", "ends_ok", "wog_ok", "v_ok", "mod_ok"))
        ext_ok, parts_ok, aux_ok, auxp_ok, stored = (
            sem(n) for n in ("ext_ok", "parts_ok", "aux_ok", "auxp_ok", "stored"))
        var_ok, rstd_ok = sem("var_ok"), sem("rstd_ok")
        block = ctx.enter_context(nc.Block())

        @block.sync
        def _(sp):
            sp.dma_start(x_nat[:], a["x"].rearrange("a (n p) d -> p (a n) d", p=P)).then_inc(in_x, 16)
            sp.dma_start(wmod[:], a["wmod"]).then_inc(in_w, 16)
            for n, name in enumerate(("WqT", "WkT", "WvT", "WpkT", "WpqT", "Wo")):
                sp.dma_start(wts[:, n, :], a[name]).then_inc(in_w, 16)
            sp.dma_start(rel[:, 0, :], a["relT"]).then_inc(in_w, 16)
            sp.dma_start(rel[:, 1, :], a["relT_rev"]).then_inc(in_w, 16)
            for n, name in enumerate(("c", "bq", "bk", "bpk", "bpq", "bo")):
                sp.dma_start(cols[:, n:n + 1], a[name]).then_inc(in_small, 16)
            sp.dma_start(bvrow[:], a["bv"]).then_inc(in_small, 16)
            n_stored = 0

            def store(dst, src):
                nonlocal n_stored
                sp.dma_start(dst, src).then_inc(stored, 16)
                n_stored += 1

            sp.wait_ge(made, 9)
            qs, kl, kr = scratch["qst"], scratch["klst"], scratch["krst"]
            for r in range(3):
                store(qs[:, ROW_S + r, :], oz[:, 0, :])
                store(kl[:, ROW_CL + r, :], oz[:, 0, :])
                store(kl[:, ROW_CR + r, :], oz[:, 1, :])
                store(kr[:, ROW_CL + r, :], oz[:, 1, :])
                store(kr[:, ROW_CR + r, :], oz[:, 0, :])
                store(kl[:, ROW_M + r, :], oz[:, 0, :])
                store(kr[:, ROW_M + r, :], oz[:, 0, :])
            sp.wait_ge(ext_ok, 2)
            store(scratch["ext"].rearrange("w c e -> c w e"), ext[:])
            sp.wait_ge(qk_ok, 2 * NB)
            store(scratch["qk"].rearrange("w c t -> c w t"), qkT[:])
            for w in range(2):
                sp.wait_ge(parts_ok, 3 * (w + 1))
                for g in range(len(PART_A)):
                    rows = slice(g * DK, (g + 1) * DK)
                    if w == 0:
                        store(qs[:, rows, :], part[:, 0, PART_A[g], :])
                    else:
                        store(kl[:, rows, :], part[:, 1, PART_B[g], :])
                        store(kr[:, rows, :], part[:, 1, PART_B[g], :])
            sp.wait_ge(auxp_ok, 6)
            for r in range(3):
                store(qs[:, ROW_CL + r, :], auxp[0:H, 0, r, :])
                store(qs[:, ROW_CR + r, :], auxp[H:2 * H, 0, r, :])
                store(kl[:, ROW_S + r, :], auxp[0:H, 1, r, :])
                store(kr[:, ROW_S + r, :], auxp[H:2 * H, 1, r, :])
            sp.wait_ge(stored, 16 * n_stored)

        @block.gpsimd
        def _(pool):
            n_made = 0

            def make(ins):
                nonlocal n_made
                n_made += 1
                ins.then_inc(made, 1)
                pool.wait_ge(made, n_made)

            make(nc.gpsimd.memset(ident[:], 0.0))
            make(nc.gpsimd.affine_select(out=ident[:], in_=ident[:], compare_op=ALU.not_equal, fill=1.0,
                                         base=0, pattern=[[-1, P]], channel_multiplier=1))
            make(nc.gpsimd.memset(oz[:, 0, :], 1.0))
            make(nc.gpsimd.memset(oz[:, 1, :], 0.0))
            make(nc.gpsimd.memset(ones_row[:], 1.0))
            make(nc.gpsimd.memset(zer[:], 0.0))
            make(nc.gpsimd.memset(head_mask[:], 1.0))
            make(nc.gpsimd.affine_select(out=head_mask[:], in_=head_mask[:], compare_op=ALU.is_ge, fill=0.0,
                                         base=0, pattern=[[-DK, H]], channel_multiplier=1))
            make(nc.gpsimd.affine_select(out=head_mask[:], in_=head_mask[:], compare_op=ALU.is_ge, fill=0.0,
                                         base=DK - 1, pattern=[[DK, H]], channel_multiplier=-1))
            pool.wait_ge(var_ok, 1)
            make(nc.gpsimd.memset(expo[:], -0.5))
            make(nc.gpsimd.tensor_scalar(rstd[:], mv[:, :, 1], EPS, None, ALU.add))
            nc.gpsimd.tensor_tensor(rstd[:], rstd[:], expo[:], ALU.pow).then_inc(rstd_ok, 1)

        @block.scalar
        def _(act):
            act.wait_ge(in_small, 16 * 7)
            nc.scalar.activation(silu[:, 0:1], cols[:, 0:1], ACT.Exp, scale=-1.0).then_inc(sil, 1)

        @block.tensor
        def _(pe):
            pe.wait_ge(in_w, 16 * 9)
            pe.wait_ge(sil, 2)
            for n in range(6):
                last = nc.tensor.matmul(ps[:, 0, n:n + 1], wmod[:, n * D:(n + 1) * D], silu[:, 3:4],
                                        start=True, stop=True)
            last.then_inc(mod_ps, 1)
            for w in range(2):
                last = nc.tensor.matmul(ps[:, 1 + w, 0:R], wts[:, 3 + w, :], rel[:, w, :], start=True, stop=True)
            last.then_inc(pos_ps, 1)
            pe.wait_ge(made, 9)
            pe.wait_ge(xn_ok, NT)
            for b in range(NB):
                for s in range(4):
                    last = nc.tensor.transpose(ps[:, 4 + b, s * P:(s + 1) * P], xn[:, 4 * b + s, :], ident[:])
                last.then_inc(xt_ps, 1)
            pe.wait_ge(pos_ok, 2)
            pe.wait_ge(mod_ok, 1)
            for w in range(2):
                if w == 1:
                    pe.wait_ge(qk_ok, NB)
                for b in range(NB):
                    pe.wait_ge(hT_ok, b + 1)
                    nc.tensor.matmul(ps[:, b, :], wts[:, w, :], hT[:, b * BANK:(b + 1) * BANK],
                                     start=True, stop=True).then_inc(qk_ps, 1)
            pe.wait_ge(ends_ok, 4)
            for w in range(2):
                if w == 1:
                    pe.wait_ge(aux_ok, NB)
                for b in range(NB):
                    pe.wait_ge(qk_ok, 2 * NB)
                    nc.tensor.matmul(ps[0:2 * H, 4 + b, :], ends[:, w, :, :].rearrange("p e h -> p (e h)"),
                                     qkT[:, w, b * BANK:(b + 1) * BANK], start=True, stop=True).then_inc(aux_ps, 1)
            for b in range(NB):
                for s in range(4):
                    t = 4 * b + s
                    nc.tensor.matmul(ps[:, b, s * P:(s + 1) * P], hT[:, t * P:(t + 1) * P], wts[:, 2, :],
                                     start=True, stop=False)
                    last = nc.tensor.matmul(ps[:, b, s * P:(s + 1) * P], ones_row[:], bvrow[:],
                                            start=False, stop=True)
                last.then_inc(v_ps, 1)
            pe.wait_ge(wog_ok, 2)
            pe.wait_ge(aux_ok, 2 * NB)
            nc.tensor.transpose(ps[:, 4, 0:D], wog[:], ident[:])
            nc.tensor.matmul(ps[0:1, 5, 0:D], cols[:, 6:7], ident[:], start=True, stop=True).then_inc(wo_ps, 1)

        @block.vector
        def _(dve):
            n_vec = 0

            def step(ins, *more):
                nonlocal n_vec
                n_vec += 1
                ins.then_inc(vec, 1)
                dve.wait_ge(vec, n_vec)

            dve.wait_ge(in_x, 16)
            for t in range(NT):
                ins = nc.vector.bn_stats(stats[:, t, :], x_nat[:, t, :])
            step(ins)
            for t in range(NT):
                ins = nc.vector.bn_aggr(mv[:, t, :], stats[:, t, :])
            ins.then_inc(var_ok, 1)
            dve.wait_ge(rstd_ok, 1)
            for t in range(NT):
                nc.vector.tensor_scalar(xn[:, t, :], x_nat[:, t, :], mv[:, t, 0:1], rstd[:, t:t + 1],
                                        ALU.subtract, ALU.mult).then_inc(xn_ok, 1)
            dve.wait_ge(sil, 1)
            step(nc.vector.tensor_scalar(silu[:, 1:2], silu[:, 0:1], 1.0, None, ALU.add))
            step(nc.vector.reciprocal(silu[:, 2:3], silu[:, 1:2]))
            nc.vector.tensor_tensor(silu[:, 3:4], silu[:, 2:3], cols[:, 0:1], ALU.mult).then_inc(sil, 1)
            dve.wait_ge(mod_ps, 1)
            step(nc.vector.tensor_copy(modc[:, 0:6], ps[:, 0, 0:6]))
            for n, g in enumerate((2, 5)):
                step(nc.vector.tensor_scalar(clampt[:, 0, n:n + 1], modc[:, g:g + 1], 0.0, 2.0, ALU.is_ge, ALU.mult))
                step(nc.vector.tensor_scalar(clampt[:, 1, n:n + 1], clampt[:, 0, n:n + 1], -1.0, None, ALU.add))
                step(nc.vector.tensor_scalar(clampt[:, 2, n:n + 1], modc[:, g:g + 1], -1.0, None, ALU.mult))
                step(nc.vector.tensor_tensor(clampt[:, 3, n:n + 1], modc[:, g:g + 1], clampt[:, 2, n:n + 1], ALU.max))
                step(nc.vector.scalar_tensor_tensor(out=modc[:, g:g + 1], in0=clampt[:, 3, n:n + 1], scalar=0.25,
                                                    in1=clampt[:, 1, n:n + 1], op0=ALU.max, op1=ALU.mult))
                step(nc.vector.tensor_scalar(modc[:, g - 1:g], modc[:, g - 1:g], 1.0, None, ALU.add))
            nc.vector.tensor_copy(silu[:, 0:1], modc[:, 0:1]).then_inc(mod_ok, 1)
            dve.wait_ge(pos_ps, 1)
            for w in range(2):
                nc.vector.tensor_scalar(posT[:, w, :], ps[:, 1 + w, 0:R], cols[:, 3 + w:4 + w], None,
                                        ALU.add).then_inc(pos_ok, 1)
            dve.wait_ge(pos_ok, 2)
            dve.wait_ge(made, 9)
            for w in range(2):
                first = P - 1 + w
                nc.vector.tensor_scalar(ext[:, w, 0:first], ident_fill(zer, first), posT[:, w, 0:1], None, ALU.add)
                nc.vector.tensor_copy(ext[:, w, first:first + R], posT[:, w, :])
                nc.vector.tensor_scalar(ext[:, w, first + R:EXT], ident_fill(zer, EXT - first - R), posT[:, w, R - 1:R],
                                        None, ALU.add).then_inc(ext_ok, 1)
                for e in range(2):
                    col = 0 if e == w else R - 1
                    nc.vector.tensor_scalar(ends[:, w, e, :], head_mask[:], posT[:, w, col:col + 1], None,
                                            ALU.mult).then_inc(ends_ok, 1)
            for b in range(NB):
                dve.wait_ge(xt_ps, b + 1)
                nc.vector.tensor_scalar(hT[:, b * BANK:(b + 1) * BANK], ps[:, 4 + b, :], modc[:, 1:2], modc[:, 0:1],
                                        ALU.mult, ALU.add).then_inc(hT_ok, 1)
            for w in range(2):
                for b in range(NB):
                    dve.wait_ge(qk_ps, NB * w + b + 1)
                    nc.vector.tensor_scalar(qkT[:, w, b * BANK:(b + 1) * BANK], ps[:, b, :], cols[:, 1 + w:2 + w],
                                            None, ALU.add).then_inc(qk_ok, 1)
            dve.wait_ge(qk_ok, 2 * NB)

            def split(out, whole, left, done):
                ins = nc.vector.tensor_copy(out[:, 0, :], whole)
                ins.then_inc(done, 1)
                dve.wait_ge(done, split.n + 1)
                step(nc.vector.tensor_tensor(left, whole, out[:, 0, :], ALU.subtract))
                nc.vector.tensor_copy(out[:, 1, :], left).then_inc(done, 1)
                dve.wait_ge(done, split.n + 2)
                step(nc.vector.tensor_tensor(left, left, out[:, 1, :], ALU.subtract))
                nc.vector.tensor_copy(out[:, 2, :], left).then_inc(done, 1)
                dve.wait_ge(done, split.n + 3)
                split.n += 3

            split.n = 0
            for w in range(2):
                split(part[:, w], qkT[:, w, :], rest[:], parts_ok)
            split.n = 0
            for w in range(2):
                for b in range(NB):
                    dve.wait_ge(aux_ps, NB * w + b + 1)
                    nc.vector.tensor_copy(aux[:, w, b * BANK:(b + 1) * BANK], ps[0:2 * H, 4 + b, :]).then_inc(aux_ok, 1)
                dve.wait_ge(aux_ok, NB * (w + 1))
                split(auxp[:, w], aux[:, w, :], rest[0:2 * H, :], auxp_ok)
            for b in range(NB):
                dve.wait_ge(v_ps, b + 1)
                nc.vector.tensor_copy(keep["v_all"][:, 4 * b:4 * b + 4, :],
                                      ps[:, b, :].rearrange("p (s d) -> p s d", s=4)).then_inc(v_ok, 1)
            nc.vector.tensor_scalar(wog[:], wts[:, 5, :], modc[:, 2:3], None, ALU.mult).then_inc(wog_ok, 1)
            nc.vector.tensor_tensor(cols[:, 6:7], cols[:, 5:6], modc[:, 2:3], ALU.mult).then_inc(wog_ok, 1)
            dve.wait_ge(wo_ps, 1)
            nc.vector.tensor_copy(keep["woT"][:], ps[:, 4, 0:D])
            nc.vector.tensor_copy(keep["bo_row"][:], ps[0:1, 5, 0:D])


def ident_fill(zer, n):
    return zer[:, 0:n]


def attention_phase(nc, keep, scratch):
    ident = keep["ident"]
    with ExitStack() as ctx:
        def sb(name, shape, dt=F32):
            return ctx.enter_context(nc.sbuf_tensor(name, shape, dt))

        def sem(name):
            return keep["semaphores"].enter_context(nc.semaphore(name))

        ring = ctx.enter_context(nc.psum_tensor("at_ring", [P, RING, BANK], F32))
        scores = ctx.enter_context(nc.psum_tensor("at_scores", [P, 2, 2, BANK], F32))
        ctx_ps = ctx.enter_context(nc.psum_tensor("at_ctx", [P, BANK], F32))

        qa, la, ra = (sb(f"at_{n}a", [P, 2, T], BF16) for n in "qlr")
        qb, lb, rb = (sb(f"at_{n}b", [ROWS, 2, T], BF16) for n in "qlr")
        tab = sb("at_tab", [P, 2, TABW])
        diag = sb("at_diag", [P, 2, T])
        class_mask = sb("at_class", [P, CL])
        c2p = sb("at_c2p", [P, 2, NT, P])
        win = sb("at_win", [P, 2, NT, WIN + 2 * SPAN])
        mx = sb("at_mx", [P, NT, 8])
        mrow = sb("at_mrow", [P, 2, NT])
        mpart = sb("at_mpart", [NT, 2, 3, P], BF16)
        mleft = sb("at_mleft", [NT, 2, P])
        onlym = sb("at_onlym", [ROWS, P], BF16)
        prob = sb("at_prob", [P, 4, 2 * BANK])
        vh = sb("at_vh", [P, 2, NT, 32])
        ctx_sb = sb("at_ctx_sb", [P, 2, BANK])

        stack_a = [sem("stack_a0"), sem("stack_a1")]
        stack_b = [sem("stack_b0"), sem("stack_b1")]
        m_rows = [sem("m_rows0"), sem("m_rows1")]
        tables_in, tables_ok = ([sem(f"{n}{w}") for w in range(2)] for n in ("tables_in", "tables_ok"))
        made, v_ok = sem("at_made"), sem("vh_ok")
        unit, c2p_kept, win_kept, win_max, far_max, m_turned, m_split, maxed = (
            sem(n) for n in ("unit", "c2p_kept", "win_kept", "win_max", "far_max", "m_turned", "m_split", "maxed"))
        cleared, m_left = sem("cleared"), sem("m_left")
        score, exped, pv, ctx_kept = (sem(n) for n in ("score", "exped", "pv", "ctx_kept"))
        ctx_out = [sem("ctx_out0"), sem("ctx_out1")]
        block = ctx.enter_context(nc.Block())

        STEPS = NT + 1
        near, far = iter(range(N_C2P + N_WIN)), iter(range(N_C2P + N_WIN, N_A - 1))
        spaced = N_FAR // (N_C2P + N_WIN)
        ORDER = [n for first in near for n in (first, *(next(far) for _ in range(spaced)))] + [N_A - 1]
        weight = [2 if n < N_C2P else 4 if n < N_C2P + N_WIN else 1 for n in ORDER]
        share = [FIRST_SHARE] + [1.0] * (NT - 1) + [LAST_SHARE]
        ends = [sum(share[:s + 1]) * sum(weight[:-1]) / sum(share) for s in range(STEPS)]
        step_of = [next(s for s in range(STEPS) if sum(weight[:pos]) < ends[s] + 1e-6) for pos in range(N_A - 1)] + [NT]

        def merged(ha, hb):
            for s in range(STEPS):
                us = [("a", pos) for pos in range(N_A) if step_of[pos] == s] if ha is not None else []
                ks = [("b", 2 * (s - 1)), ("b", 2 * (s - 1) + 1)] if hb is not None and s > 0 else []
                n = max(len(us), 1)
                for x in range(n):
                    yield from us[x:x + 1]
                    yield from ks[x * len(ks) // n:(x + 1) * len(ks) // n]

        def iterations(eng, run):
            run(0, 0, None, 1)
            run(1, 1, 0, 0)
            with eng.Fori(0, H // 2 - 2) as pair:
                run(2 * pair + 2, 0, 2 * pair + 1, 1)
                run(2 * pair + 3, 1, 2 * pair + 2, 0)
            run(H - 2, 0, H - 3, 1)
            run(H - 1, 1, H - 2, 0)
            run(None, 0, H - 1, 1)

        def loads_of(h, p):
            return h - p + 2

        def window_tiles(n):
            q, g = n // 2, n % 2
            first, end = g * GI, (g + 1) * GI
            if q == 0 and g == 0:
                first += 1
            if q == 3 and g == 1:
                end -= 1
            return q, first, end

        @block.sync
        def _(sp):
            def load_tables(h, w):
                sp.dma_start(tab[:, w, :], shifted(scratch["ext"][w, bass.ds(h * DK, DK), :])).then_inc(tables_in[w], 16)
                sp.dma_start(diag[:, w, :], repeated(scratch["qk"][w, bass.ds(h * DK, DK), :])).then_inc(tables_in[w], 16)

            def load_rows(dst, stack, h, rows, done):
                sp.dma_start(dst, scratch[stack][bass.ds(h, 1), 0:rows].rearrange("a r t -> (a r) t")).then_inc(done, 16)

            def load_stacks(h, p, q, l, r, done):
                load_rows(q[0:ROW_M, p, :], "qst", h, ROW_M, done[p])
                load_rows(l[0:ROWS, p, :], "klst", h, ROWS, done[p])
                load_rows(r[0:ROWS, p, :], "krst", h, ROWS, done[p])

            def load_stacks_a(h, p):
                load_stacks(h, p, qa, la, ra, stack_a)
                load_rows(qa[SPAN:SPAN + ROW_QK, p, :], "qst", h, ROW_QK, stack_a[p])
                load_rows(la[SPAN:SPAN + ROW_QK, p, :], "klst", h, ROW_QK, stack_a[p])

            load_stacks_a(0, 0)
            for w in range(2):
                load_tables(0, w)

            def run(ha, pa, hb, pb):
                if ha is not None and not (isinstance(ha, int) and ha == H - 1):
                    if hb is not None:
                        sp.wait_ge(m_turned, ha)
                    load_stacks_a(ha + 1, 1 - pa)
                if ha is not None:
                    if not isinstance(ha, int) or ha > 1:
                        sp.wait_ge(pv, (ha - 1) * N_B)
                    load_stacks(ha, pa, qb, lb, rb, stack_b)
                    if not (isinstance(ha, int) and ha == H - 1):
                        sp.wait_ge(c2p_kept, (ha + 1) * N_C2P)
                        load_tables(ha + 1, 0)
                        sp.wait_ge(win_kept, (ha + 1) * N_WIN)
                        load_tables(ha + 1, 1)
                    sp.wait_ge(m_split, 3 * (ha + 1))
                    for r in range(3):
                        sp.dma_start(qb[ROW_M + r:ROW_M + r + 1, pa, :].rearrange("a (n q) -> a n q", q=P),
                                     mpart[:, pa, r, :]).then_inc(m_rows[pa], 16)
                if hb is not None:
                    sp.wait_ge(ctx_kept, hb + 1)
                    for g in range(NB):
                        sp.dma_start(scratch["ctx"][bass.ds(hb, 1), :, g * BANK:(g + 1) * BANK].rearrange("a r t -> (a r) t"),
                                     ctx_sb[32 * g:32 * g + DK + 1, pb, :]).then_inc(ctx_out[pb], 16)

            iterations(sp, run)
            for p in range(2):
                sp.wait_ge(ctx_out[p], 16 * NB * (H // 2))

        @block.gpsimd
        def _(pool):
            n_made = 0

            def make(ins):
                nonlocal n_made
                n_made += 1
                ins.then_inc(made, 1)
                pool.wait_ge(made, n_made)

            make(nc.gpsimd.memset(class_mask[:], 1.0))
            make(nc.gpsimd.affine_select(out=class_mask[:], in_=class_mask[:], compare_op=ALU.is_ge, fill=0.0,
                                         base=-DK * (CL - 1), pattern=[[DK, CL]], channel_multiplier=1))
            make(nc.gpsimd.affine_select(out=class_mask[:], in_=class_mask[:], compare_op=ALU.is_ge, fill=0.0,
                                         base=P - 1, pattern=[[-DK, CL]], channel_multiplier=-1))
            make(nc.gpsimd.memset(onlym[:], 1.0))
            make(nc.gpsimd.affine_select(out=onlym[:], in_=onlym[:], compare_op=ALU.is_ge, fill=0.0,
                                         base=-ROW_M, pattern=[[0, P]], channel_multiplier=1))
            make(nc.gpsimd.memset(vh[:], 0.0))
            make(nc.gpsimd.memset(vh[:, :, :, DK:DK + 1], 1.0))
            make(nc.gpsimd.memset(win[:], 0.0))

            def run(ha, pa, hb, pb):
                if ha is None:
                    return
                for w in range(2):
                    pool.wait_ge(tables_in[w], (ha + 1) * 32)
                    v = diag[:, w, :].rearrange("p (n t) -> p n t", t=CL)
                    nc.gpsimd.tensor_tensor(v, v, class_mask[:, None, :].to_broadcast([P, T // CL, CL]), ALU.mult
                                            ).then_inc(tables_ok[w], 1)
                if not isinstance(ha, int) or ha > 1:
                    pool.wait_ge(pv, (ha - 1) * N_B)
                nc.gpsimd.tensor_copy(vh[:, pa, :, 0:DK], keep["v_all"][:, :, bass.ds(ha * DK, DK)]).then_inc(v_ok, 1)

            iterations(pool, run)

        @block.tensor
        def _(pe):
            def free_ring(ha, pos):
                pos -= RING
                if pos < 0:
                    if isinstance(ha, int) and ha == 0:
                        return
                    ha, pos = ha - 1, pos + N_A
                n = ORDER[pos]
                if n < N_C2P:
                    pe.wait_ge(c2p_kept, ha * N_C2P + n + 1)
                elif n < N_C2P + N_WIN:
                    pe.wait_ge(win_kept, ha * N_WIN + n - N_C2P + 1)
                elif n < N_A - 1:
                    pe.wait_ge(far_max, ha * N_FAR + n - N_C2P - N_WIN + 1)
                else:
                    pe.wait_ge(m_split, 3 * (ha + 1))

            def unit_a(ha, pa, pos):
                n, out = ORDER[pos], ring[:, pos % RING, :]
                free_ring(ha, pos)
                if n == 0:
                    pe.wait_ge(tables_ok[0], ha + 1)
                    pe.wait_ge(stack_a[pa], loads_of(ha, pa) * 40)
                if n < N_C2P:
                    half, qh, g = n // 4, n // 2 % 2, n % 2
                    v = out.rearrange("p (i q) -> p i q", q=P // 2)
                    toks = diag[:, 0, g * GI * P:(g + 1) * GI * P].rearrange("p (i q) -> p i q", q=P)
                    for c in range(4):
                        col = KEY0 + P * half - CL * (4 * qh + c)
                        at = P // 2 * qh + CL * c
                        last = nc.tensor.matmul(v[:, :, CL * c:CL * (c + 1)], tab[:, 0, col:col + P],
                                                toks[:, :, at:at + CL], start=(c == 0), stop=True,
                                                skip_group_check=True)
                elif n < N_C2P + N_WIN:
                    q, first, end = window_tiles(n - N_C2P)
                    if n == N_C2P:
                        pe.wait_ge(tables_ok[1], ha + 1)
                        pe.wait_ge(c2p_kept, (ha + 1) * N_C2P)
                    v = out.rearrange("p (i k) -> p i k", k=SPAN)[:, 0:end - first, :]
                    k0 = P * first - SPAN + SPAN * q
                    for c in range(4):
                        col = QRY0 - CL * (4 * q + c)
                        nc.tensor.matmul(v[:, :, CL * c:CL * (c + 1)], tab[:, 1, col:col + P],
                                         strided(diag[:, 1, k0 + CL * c:k0 + CL * (c + 1)], P, end - first),
                                         start=(c == 0), stop=False, skip_group_check=True)
                    keys = slice(SPAN * (q % 2), SPAN * (q % 2 + 1))
                    rows = slice(keys.start, keys.start + ROW_QK)
                    for i in range(first, end):
                        nc.tensor.matmul(v[:, i - first, :], qa[rows, pa, P * i:P * (i + 1)],
                                         la[rows, pa, P * i - SPAN + SPAN * q:P * i + SPAN * q],
                                         start=False, stop=False, skip_group_check=True)
                    for i in range(first, end):
                        last = nc.tensor.matmul(v[:, i - first, :], c2p[keys, q // 2, i, :], ident[keys, keys],
                                                is_transpose=True, start=False, stop=True, skip_group_check=True)
                elif n < N_A - 1:
                    i, u = divmod(n - N_C2P - N_WIN, FU)
                    for is_left, k, width, col in far_units(i)[u][1]:
                        last = nc.tensor.matmul(out[:, col:col + width], qa[0:ROW_M, pa, P * i:P * (i + 1)],
                                                (la if is_left else ra)[0:ROW_M, pa, k:k + width],
                                                start=True, stop=True, skip_group_check=True)
                else:
                    pe.wait_ge(maxed, ha + 1)
                    last = nc.tensor.transpose(out[0:NT, 0:P], mrow[:, pa, :], ident[:])
                    last.then_inc(m_turned, 1)
                    return
                last.then_inc(unit, 1)

            def scores_b(hb, pb, n):
                j, half = divmod(n, 2)
                if n == 0:
                    pe.wait_ge(stack_b[pb], loads_of(hb, pb) * 24)
                    pe.wait_ge(m_rows[pb], loads_of(hb, pb) * 24)
                    pe.wait_ge(win_kept, (hb + 1) * N_WIN)
                if n >= 2:
                    pe.wait_ge(exped, hb * N_B + n - 1)
                for b in range(2):
                    bank = scores[:, half, b, :]
                    i = first = 4 * (2 * half + b)
                    while i < first + 4:
                        o = P * (i - first)
                        if abs(i - j) <= 1:
                            off = P - P * (i - j)
                            blk = bank[:, o:o + P]
                            nc.tensor.matmul(blk, win[:, pb, i, off:off + P], ident[:], is_transpose=True,
                                             start=True, stop=False, skip_group_check=True)
                            last = nc.tensor.matmul(blk, onlym[:], qb[0:ROWS, pb, P * i:P * (i + 1)],
                                                    start=False, stop=(i == j), skip_group_check=True)
                            if i != j:
                                lo = 0 if i == j + 1 else SPAN
                                last = nc.tensor.matmul(bank[lo:lo + SPAN, o:o + P],
                                                        (lb if i > j else rb)[0:ROW_M, pb, P * j + lo:P * j + lo + SPAN],
                                                        qb[0:ROW_M, pb, P * i:P * (i + 1)],
                                                        start=False, stop=True, skip_group_check=True)
                            i += 1
                        else:
                            e = i
                            while e < first + 4 and abs(e - j) > 1 and (e > j) == (i > j):
                                e += 1
                            last = nc.tensor.matmul(bank[:, o:o + P * (e - i)],
                                                    (lb if i > j else rb)[:, pb, P * j:P * (j + 1)],
                                                    qb[:, pb, P * i:P * e], start=True, stop=True,
                                                    skip_group_check=True)
                            i = e
                last.then_inc(score, 1)

            def values_b(hb, pb, n):
                j, half = divmod(n, 2)
                if n == 0:
                    pe.wait_ge(v_ok, hb + 1)
                    if not (isinstance(hb, int) and hb == 0):
                        pe.wait_ge(ctx_kept, hb)
                pe.wait_ge(exped, hb * N_B + n + 1)
                for b in range(2):
                    g = 2 * half + b
                    last = nc.tensor.matmul(ctx_ps[32 * g:32 * (g + 1), :], vh[:, pb, j, :],
                                            prob[:, n % 4, b * BANK:(b + 1) * BANK], start=(j == 0), stop=(j == NT - 1),
                                            skip_group_check=True)
                last.then_inc(pv, 1)

            pe.wait_ge(made, 8)

            def run(ha, pa, hb, pb):
                for kind, n in merged(ha, hb):
                    if kind == "a":
                        unit_a(ha, pa, n)
                    else:
                        scores_b(hb, pb, n)
                        if n > 1:
                            values_b(hb, pb, n - 2)
                if hb is not None:
                    values_b(hb, pb, N_B - 2)
                    values_b(hb, pb, N_B - 1)

            iterations(pe, run)

        @block.scalar
        def _(act):
            act.wait_ge(made, 8)

            def run(ha, pa, hb, pb):
                for kind, n in merged(ha, hb):
                    if kind == "a":
                        pos, n = n, ORDER[n]
                    if kind == "b":
                        act.wait_ge(score, hb * N_B + n + 1)
                        if not (isinstance(hb, int) and hb == 0 and n < 4):
                            act.wait_ge(pv, hb * N_B + max(n - 3, 0))
                        nc.scalar.activation(prob[:, n % 4, :], scores[:, n % 2, :, :].rearrange("p b q -> p (b q)"),
                                             ACT.Exp, scale=SCALE).then_inc(exped, 1)
                    elif n < N_C2P:
                        act.wait_ge(unit, ha * (N_A - 1) + pos + 1)
                        half, qh, g = n // 4, n // 2 % 2, n % 2
                        nc.scalar.copy(c2p[:, half, g * GI:(g + 1) * GI, P // 2 * qh:P // 2 * (qh + 1)],
                                       ring[:, pos % RING, :].rearrange("p (i q) -> p i q", q=P // 2)
                                       ).then_inc(c2p_kept, 1)
                    elif n < N_C2P + N_WIN:
                        act.wait_ge(unit, ha * (N_A - 1) + pos + 1)
                        if n == N_C2P and not (isinstance(ha, int) and ha < 2):
                            act.wait_ge(pv, (ha - 1) * N_B)
                        q, first, end = window_tiles(n - N_C2P)
                        nc.scalar.copy(win[:, pa, first:end, SPAN * (q + 1):SPAN * (q + 2)],
                                       ring[:, pos % RING, 0:SPAN * (end - first)].rearrange("p (i k) -> p i k", k=SPAN)
                                       ).then_inc(win_kept, 1)

            iterations(act, run)

        @block.vector
        def _(dve):
            nc.vector.memset(mx[:], -3.0e38).then_inc(cleared, 1)
            dve.wait_ge(cleared, 1)

            def run(ha, pa, hb, pb):
                if ha is not None:
                    if not (isinstance(ha, int) and ha == 0):
                        dve.wait_ge(maxed, ha)
                    for pos, n in enumerate(ORDER[:-1]):
                        if n < N_C2P:
                            continue
                        if n >= N_C2P + N_WIN:
                            dve.wait_ge(unit, ha * (N_A - 1) + pos + 1)
                        if n < N_C2P + N_WIN:
                            q, first, end = window_tiles(n - N_C2P)
                            dve.wait_ge(win_kept, ha * N_WIN + n - N_C2P + 1)
                            nc.vector.reduce_max(mx[:, first:end, q], win[:, pa, first:end, SPAN * (q + 1):SPAN * (q + 2)], AX.X).then_inc(win_max, 1)
                        else:
                            i, u = divmod(n - N_C2P - N_WIN, FU)
                            nc.vector.reduce_max(mx[:, i, 4 + u:5 + u], ring[:, pos % RING, 0:far_units(i)[u][0]], AX.X
                                                 ).then_inc(far_max, 1)
                    dve.wait_ge(far_max, (ha + 1) * N_FAR)
                    nc.vector.reduce_max(mrow[:, pa, :], mx[:], AX.X).then_inc(maxed, 1)
                    dve.wait_ge(m_turned, ha + 1)
                    if not isinstance(ha, int) or ha > 1:
                        dve.wait_ge(m_rows[pa], (loads_of(ha, pa) - 2) * 24)
                    turned, left = ring[0:NT, (N_A - 1) % RING, 0:P], mleft[:, pa, :]
                    nc.vector.tensor_scalar(mpart[:, pa, 0, :], turned, -1.0, None, ALU.mult).then_inc(m_split, 1)
                    dve.wait_ge(m_split, 3 * ha + 1)
                    nc.vector.scalar_tensor_tensor(out=left, in0=turned, scalar=-1.0, in1=mpart[:, pa, 0, :],
                                                   op0=ALU.mult, op1=ALU.subtract).then_inc(m_left, 1)
                    dve.wait_ge(m_left, 2 * ha + 1)
                    nc.vector.tensor_copy(mpart[:, pa, 1, :], left).then_inc(m_split, 1)
                    dve.wait_ge(m_split, 3 * ha + 2)
                    nc.vector.tensor_tensor(left, left, mpart[:, pa, 1, :], ALU.subtract).then_inc(m_left, 1)
                    dve.wait_ge(m_left, 2 * ha + 2)
                    nc.vector.tensor_copy(mpart[:, pa, 2, :], left).then_inc(m_split, 1)
                if hb is not None:
                    dve.wait_ge(pv, (hb + 1) * N_B)
                    if not isinstance(hb, int) or hb > 1:
                        dve.wait_ge(ctx_out[pb], (loads_of(hb, pb) - 2) * 8 * NB)
                    nc.vector.tensor_copy(ctx_sb[:, pb, :], ctx_ps[:]).then_inc(ctx_kept, 1)

            iterations(dve, run)


def shifted(rows):
    (step, _), _ = rows.ap
    return bass.AP(rows.tensor, rows.offset, [[1, CL], [step, DK], [1, TABW]])


def repeated(rows):
    (step, _), _ = rows.ap
    return bass.AP(rows.tensor, rows.offset, [[0, CL], [step, DK], [1, T]])


def strided(cols, step, n):
    part, (one, w) = cols.ap
    return bass.AP(cols.tensor, cols.offset, [list(part), [step, n], [one, w]])


def output_phase(nc, keep, scratch):
    with ExitStack() as ctx:
        def sb(name, shape, dt=F32):
            return ctx.enter_context(nc.sbuf_tensor(name, shape, dt))

        def sem(name):
            return keep["semaphores"].enter_context(nc.semaphore(name))

        ps = ctx.enter_context(nc.psum_tensor("ou_ps", [P, 8, BANK], F32))
        ctxT = sb("ou_ctxT", [P, T])
        den = sb("ou_den", [H, T])
        spread = sb("ou_spread", [H, P])
        ones_row = sb("ou_ones", [1, P])
        loaded, made, inverse, spread_ps, normed, out_ps, added = (
            sem(n) for n in ("ou_loaded", "ou_made", "inverse", "spread_ps", "normed", "out_ps", "added"))
        block = ctx.enter_context(nc.Block())

        @block.sync
        def _(sp):
            for h in range(H):
                sp.dma_start(ctxT[DK * h:DK * (h + 1), :], scratch["ctx"][h, 0:DK, :]).then_inc(loaded, 16)
            sp.dma_start(den[:], scratch["ctx"][:, DK, :]).then_inc(loaded, 16)

        @block.gpsimd
        def _(pool):
            nc.gpsimd.memset(ones_row[:], 1.0).then_inc(made, 1)
            nc.gpsimd.memset(spread[:], 1.0).then_inc(made, 1)
            pool.wait_ge(made, 2)
            nc.gpsimd.affine_select(out=spread[:], in_=spread[:], compare_op=ALU.is_ge, fill=0.0,
                                    base=0, pattern=[[1, P]], channel_multiplier=-DK).then_inc(made, 1)
            pool.wait_ge(made, 3)
            nc.gpsimd.affine_select(out=spread[:], in_=spread[:], compare_op=ALU.is_ge, fill=0.0,
                                    base=DK - 1, pattern=[[-1, P]], channel_multiplier=DK).then_inc(made, 1)

        @block.tensor
        def _(pe):
            pe.wait_ge(inverse, 1)
            pe.wait_ge(made, 4)
            for b in range(NB):
                nc.tensor.matmul(ps[:, b, :], spread[:], den[:, b * BANK:(b + 1) * BANK],
                                 start=True, stop=True).then_inc(spread_ps, 1)
            for b in range(NB):
                pe.wait_ge(normed, b + 1)
                for s in range(4):
                    t = 4 * b + s
                    o = ps[:, 4 + b, s * P:(s + 1) * P]
                    nc.tensor.matmul(o, ctxT[:, t * P:(t + 1) * P], keep["woT"][:], start=True, stop=False)
                    last = nc.tensor.matmul(o, ones_row[:], keep["bo_row"][:], start=False, stop=True)
                last.then_inc(out_ps, 1)

        @block.vector
        def _(dve):
            dve.wait_ge(loaded, 16 * (H + 1))
            nc.vector.reciprocal(den[:], den[:]).then_inc(inverse, 1)
            for b in range(NB):
                dve.wait_ge(spread_ps, b + 1)
                c = ctxT[:, b * BANK:(b + 1) * BANK]
                nc.vector.tensor_tensor(c, c, ps[:, b, :], ALU.mult).then_inc(normed, 1)
            for b in range(NB):
                dve.wait_ge(out_ps, b + 1)
                c = keep["x_nat"][:, 4 * b:4 * b + 4, :].rearrange("p s d -> p (s d)")
                nc.vector.tensor_tensor(c, c, ps[:, 4 + b, :], ALU.add).then_inc(added, 1)
            dve.wait_ge(added, NB)


DEPTH = 8
NODES = 2 ** DEPTH - 1
LEAVES = 2 ** DEPTH
LW = 16
W1, W2, B1, B2 = 0, LW * D, 2 * LW * D, 2 * LW * D + LW
LEAF_ROW = B2 + D
SCALE_F = float(D ** -0.5)


def norm_phase(nc, a, keep):
    x_nat, ident, modc = keep["x_nat"], keep["ident"], keep["modc"]
    xf, xfT = keep["xf"], keep["xfT"]
    with ExitStack() as ctx:
        def sb(name, shape, dt=F32):
            return ctx.enter_context(nc.sbuf_tensor(name, shape, dt))

        def sem(name):
            return keep["semaphores"].enter_context(nc.semaphore(name))

        ps = ctx.enter_context(nc.psum_tensor("no_ps", [P, 8, BANK], F32))
        stats = sb("no_stats", [P, NT, 6])
        mv = sb("no_mv", [P, 2, NT, 2])
        rstd = sb("no_rstd", [P, 2, NT])
        expo = sb("no_expo", [P, 2, NT])
        mod_rows = sb("no_mod", [P, 2, D])
        h2 = sb("no_h2", [P, NT, D])
        rows_ps, vec, var_ok, rstd_ok, pooled, turned = (
            sem(n) for n in ("rows_ps", "no_vec", "no_var_ok", "no_rstd_ok", "pooled", "turned"))
        xf_ok, xfT_ok, nodes_in = sem("xf_ok"), sem("xfT_ok"), sem("nodes_in")
        block = ctx.enter_context(nc.Block())

        @block.sync
        def _(sp):
            nodes, n_loads = keep["nodes"], 0
            for n, tree in enumerate("qkvf"):
                sp.dma_start(nodes["nw"][:, n, :], a[f"{tree}_nwT"]).then_inc(nodes_in, 16)
                for c, size in enumerate(NODE_CHUNK):
                    sp.dma_start(nodes["nb"][0:size, n, c:c + 1], a[f"{tree}_nb"][c * P:c * P + size, :]
                                 ).then_inc(nodes_in, 16)
            for c, size in enumerate(NODE_CHUNK):
                sp.dma_start(nodes["paths"][0:size, c, :], a["paths"][c * P:c * P + size, :]).then_inc(nodes_in, 16)
            sp.dma_start(nodes["turns"][:], a["turns"]).then_inc(nodes_in, 16)
            sp.dma_start(nodes["number"][:], a["number"]).then_inc(nodes_in, 16)
            sp.wait_ge(nodes_in, 16 * (3 * 4 + 4))

        @block.gpsimd
        def _(pool):
            n_pooled = 0

            def step(ins):
                nonlocal n_pooled
                n_pooled += 1
                ins.then_inc(pooled, 1)
                pool.wait_ge(pooled, n_pooled)

            step(nc.gpsimd.memset(expo[:, 0, :], -0.5))
            step(nc.gpsimd.memset(expo[:, 1, :], 0.5))
            pool.wait_ge(var_ok, 1)
            step(nc.gpsimd.tensor_scalar(rstd[:, 0, :], mv[:, 0, :, 1], EPS, None, ALU.add))
            nc.gpsimd.tensor_tensor(rstd[:, 0, :], rstd[:, 0, :], expo[:, 0, :], ALU.pow).then_inc(rstd_ok, 1)
            pool.wait_ge(var_ok, 2)
            step(nc.gpsimd.tensor_scalar(rstd[:, 1, :], mv[:, 1, :, 1], D / (D - 1.0), None, ALU.mult))
            step(nc.gpsimd.tensor_tensor(rstd[:, 1, :], rstd[:, 1, :], expo[:, 1, :], ALU.pow))
            step(nc.gpsimd.tensor_scalar(rstd[:, 1, :], rstd[:, 1, :], EPS, None, ALU.add))
            nc.gpsimd.tensor_tensor(rstd[:, 1, :], rstd[:, 1, :], expo[:, 0, :], ALU.pow).then_inc(rstd_ok, 1)

        @block.tensor
        def _(pe):
            for n, col in enumerate((4, 3)):
                last = nc.tensor.matmul(ps[:, 0, n * D:(n + 1) * D], modc[:, col:col + 1].to_broadcast([P, P]),
                                        ident[:], start=True, stop=True)
            last.then_inc(rows_ps, 1)
            for t in range(NT):
                pe.wait_ge(xf_ok, t + 1)
                last = nc.tensor.transpose(ps[:, 4 + t // 4, t % 4 * P:(t % 4 + 1) * P], xf[:, t, :], ident[:])
                if t % 4 == 3:
                    last.then_inc(turned, 1)

        @block.vector
        def _(dve):
            n_vec = 0

            def step(ins):
                nonlocal n_vec
                n_vec += 1
                ins.then_inc(vec, 1)
                dve.wait_ge(vec, n_vec)

            def statistics(x, r):
                for t in range(NT):
                    ins = nc.vector.bn_stats(stats[:, t, :], x[:, t, :])
                step(ins)
                for t in range(NT):
                    ins = nc.vector.bn_aggr(mv[:, r, t, :], stats[:, t, :])
                ins.then_inc(var_ok, 1)
                dve.wait_ge(rstd_ok, r + 1)

            statistics(x_nat, 0)
            dve.wait_ge(rows_ps, 1)
            nc.vector.tensor_copy(mod_rows[:].rearrange("p a d -> p (a d)"), ps[:, 0, 0:2 * D])
            for t in range(NT):
                ins = nc.vector.tensor_scalar(h2[:, t, :], x_nat[:, t, :], mv[:, 0, t, 0:1], rstd[:, 0, t:t + 1],
                                              ALU.subtract, ALU.mult)
            step(ins)
            for n, op in enumerate((ALU.mult, ALU.add)):
                step(nc.vector.tensor_tensor(h2[:], h2[:], mod_rows[:, n:n + 1, :].to_broadcast([P, NT, D]), op))
            statistics(h2, 1)
            for t in range(NT):
                nc.vector.tensor_scalar(xf[:, t, :], h2[:, t, :], mv[:, 1, t, 0:1], rstd[:, 1, t:t + 1],
                                        ALU.subtract, ALU.mult).then_inc(xf_ok, 1)
            for b in range(NB):
                dve.wait_ge(turned, b + 1)
                nc.vector.tensor_copy(xfT[:, b * BANK:(b + 1) * BANK], ps[:, 4 + b, :]).then_inc(xfT_ok, 1)
            dve.wait_ge(xfT_ok, NB)


SLOTS = 4
NODE_CHUNK = (P, NODES - P)


def leaves_phase(nc, a, trees, keep, out=None):
    tag, N = trees[0], len(trees)
    ident, x, srcT, nodes, leaf = keep["ident"], keep["xf"], keep["xfT"], keep["nodes"], keep["leaf"]
    tree_no = ["qkvf".index(tree) for tree in trees]
    assert NT == SLOTS * NB and BANK == SLOTS * P
    with ExitStack() as ctx:
        def sb(name, shape, dt=F32):
            return ctx.enter_context(nc.sbuf_tensor(f"le_{tag}_{name}", shape, dt))

        def sem(name):
            return keep["semaphores"].enter_context(nc.semaphore(f"le_{tag}_{name}"))

        def sems(name):
            return [sem(f"{name}{s}") for s in range(SLOTS)]

        ps = ctx.enter_context(nc.psum_tensor(f"le_{tag}_ps", [P, 8, BANK], F32))
        ROUTE, NAMED = SLOTS, SLOTS + 2
        BACK = SLOTS
        rows = sb("rows", [P, SLOTS, LEAF_ROW])
        index = sb("index", [P, SLOTS], I32)
        prod1 = sb("prod1", [P, LW, D])
        prod2 = sb("prod2", [P, SLOTS, LW, D])
        hid = sb("hid", [P, SLOTS, 3, LW])
        went = sb("went", [P, 2, BANK], BF16)
        hit = sb("hit", [P, 2, BANK], BF16)
        if out is not None:
            mixT = sb("mixT", [P, SLOTS, D])
            outs = sb("outs", [P, SLOTS, D])
        gathered, summed, kept = sems("gathered"), sems("summed"), sems("kept")
        if out is not None:
            finished, stored = sems("finished"), sems("stored")
            back = sem("back")
        indexed, asked, multiplied, reduced, biased, active, scaled, b2_read = (
            sem(n) for n in ("indexed", "asked", "multiplied", "reduced", "biased", "active", "scaled", "b2_read"))
        logits, decided, counted, found, named, routed = (
            sem(n) for n in ("logits", "decided", "counted", "found", "named", "routed"))
        block = ctx.enter_context(nc.Block())

        def lots(eng, run, first=None):
            if first is not None:
                for b in range(NB):
                    first(b)
            for n in range(N):
                with eng.Fori(0, NB) as k:
                    run(n, k, NB * n + k, NB * (n + 1) + k, n + 1 if n + 1 < N else None)

        def tile_of(k, s):
            return SLOTS * k + s

        @block.gpsimd
        def _(pool):
            def run(n, k, uses, _lot, _next):
                pool.wait_ge(routed, uses + 1)
                for s in range(SLOTS):
                    pool.wait_ge(scaled, SLOTS * uses + s + 1)
                    pool.wait_ge(b2_read, SLOTS * uses + s + 1)
                    nc.gpsimd.tensor_copy(index[:, s:s + 1], leaf[:, tree_no[n], bass.ds(tile_of(k, s), 1)]
                                          ).then_inc(indexed, 1)
                    pool.wait_ge(indexed, SLOTS * uses + s + 1)
                    pool.sem_inc(asked, 1)
                    nc.gpsimd.indirect_dma_start(rows[:, s, :], None, a[f"{trees[n]}_leaves"],
                                                 bass.IndirectOffsetOnAxis(ap=index[:, s:s + 1], axis=0)
                                                 ).then_inc(gathered[s], 16)

            lots(pool, run)

        @block.vector
        def _(dve):
            def decide(n, lot):
                dve.wait_ge(logits, lot + 1)
                for c, size in enumerate(NODE_CHUNK):
                    nc.vector.tensor_scalar(went[0:size, c, :], ps[0:size, ROUTE + c, :],
                                            nodes["nb"][0:size, tree_no[n], c:c + 1], 0.0, ALU.add, ALU.is_gt
                                            ).then_inc(decided, 1)

            def find(lot):
                dve.wait_ge(counted, lot + 1)
                for c in range(2):
                    nc.vector.tensor_scalar(hit[:, c, :], ps[:, ROUTE + c, :], nodes["turns"][:, c:c + 1], None,
                                            ALU.is_equal).then_inc(found, 1)

            def keep_leaves(n, b, lot):
                dve.wait_ge(named, lot + 1)
                nc.vector.tensor_copy(leaf[:, tree_no[n], bass.ds(SLOTS * b, SLOTS)], ps[:, NAMED, 0:SLOTS]
                                      ).then_inc(routed, 1)

            def first(b):
                decide(0, b)
                find(b)
                keep_leaves(0, b, b)

            def hidden(n, k, uses, s):
                row, item = rows[:, s, :], SLOTS * uses + s
                dve.wait_ge(gathered[s], 16 * uses + 16)
                nc.vector.tensor_tensor(prod1[:], row[:, W1:W2].rearrange("p (l d) -> p l d", d=D),
                                        x[:, bass.ds(tile_of(k, s), 1), :].to_broadcast([P, LW, D]), ALU.mult
                                        ).then_inc(multiplied, 1)
                dve.wait_ge(multiplied, item + 1)
                nc.vector.tensor_reduce(hid[:, s, 0, :], prod1[:], AX.X, ALU.add).then_inc(reduced, 1)
                dve.wait_ge(reduced, item + 1)
                nc.vector.tensor_tensor(hid[:, s, 1, :], hid[:, s, 0, :], row[:, B1:B2], ALU.add).then_inc(biased, 1)
                if out is None:
                    dve.wait_ge(biased, item + 1)
                    nc.vector.tensor_scalar(hid[:, s, 2, :], hid[:, s, 1, :], 0.0, None, ALU.max).then_inc(active, 1)

            def run(n, k, uses, lot, nxt):
                hidden(n, k, uses, 0)
                hidden(n, k, uses, 1)
                if nxt is not None:
                    decide(nxt, lot)
                hidden(n, k, uses, 2)
                if nxt is not None:
                    find(lot)
                hidden(n, k, uses, 3)
                if nxt is not None:
                    keep_leaves(nxt, k, lot)

            lots(dve, run, first)

        @block.scalar
        def _(act):
            act.sem_inc(scaled, SLOTS)
            for s in range(SLOTS):
                act.sem_inc(kept[s], 1)
                if out is not None:
                    act.sem_inc(finished[s], 1)
                    act.sem_inc(stored[s], 1)

            def scale(uses, s):
                item = SLOTS * uses + s
                if out is not None:
                    act.wait_ge(biased, item + 1)
                    nc.scalar.activation(hid[:, s, 2, :], hid[:, s, 1, :], ACT.Gelu).then_inc(active, 1)
                act.wait_ge(active, item + 1)
                for l in range(LW):
                    ins = nc.scalar.mul(prod2[:, s, l, :], rows[:, s, W2 + l * D:W2 + (l + 1) * D],
                                        hid[:, s, 2, l:l + 1])
                ins.then_inc(scaled, 1)

            def keep_sum(n, k, uses, s):
                act.wait_ge(summed[s], uses + 1)
                if out is not None:
                    nc.scalar.mul(mixT[:, s, :], ps[:, s, 0:D], keep["modc"][:, 5:6]).then_inc(kept[s], 1)
                else:
                    nc.scalar.copy(keep["qkvT"][:, n, bass.ds(tile_of(k, s) * P, P)], ps[:, s, 0:D]
                                   ).then_inc(kept[s], 1)

            def finish(uses, s):
                act.wait_ge(back, SLOTS * uses + s + 1)
                act.wait_ge(stored[s], 16 * uses + 1)
                nc.scalar.copy(outs[:, s, :], ps[:, BACK + s, 0:D]).then_inc(finished[s], 1)

            def run(n, k, uses, _lot, _next):
                for s in range(SLOTS):
                    scale(uses, s)
                    if s >= 1:
                        keep_sum(n, k, uses, s - 1)
                    if out is not None and s >= 2:
                        finish(uses, s - 2)
                keep_sum(n, k, uses, SLOTS - 1)
                if out is not None:
                    finish(uses, SLOTS - 2)
                    finish(uses, SLOTS - 1)

            lots(act, run)

        @block.tensor
        def _(pe):
            pe.sem_inc(b2_read, SLOTS)

            def decide(n, b, lot):
                if not (isinstance(lot, int) and lot == 0):
                    pe.wait_ge(found, 2 * lot)
                for c, size in enumerate(NODE_CHUNK):
                    last = nc.tensor.matmul(ps[0:size, ROUTE + c, :], nodes["nw"][:, tree_no[n], c * P:c * P + size],
                                            srcT[:, bass.ds(b * BANK, BANK)], start=True, stop=True)
                last.then_inc(logits, 1)

            def count(lot):
                pe.wait_ge(decided, 2 * (lot + 1))
                for c in range(2):
                    for m, size in enumerate(NODE_CHUNK):
                        last = nc.tensor.matmul(ps[:, ROUTE + c, :], nodes["paths"][0:size, m, c * P:(c + 1) * P],
                                                went[0:size, m, :], start=(m == 0), stop=(m == 1))
                last.then_inc(counted, 1)

            def name(lot):
                pe.wait_ge(found, 2 * (lot + 1))
                if not (isinstance(lot, int) and lot == 0):
                    pe.wait_ge(routed, lot)
                for s in range(SLOTS):
                    for c in range(2):
                        last = nc.tensor.matmul(ps[:, NAMED, s:s + 1], hit[:, c, s * P:(s + 1) * P],
                                                nodes["number"][:, c:c + 1], start=(c == 0), stop=(c == 1),
                                                skip_group_check=True)
                last.then_inc(named, 1)

            def first(b):
                decide(0, b, b)
                count(b)
                name(b)

            def total(k, uses, s):
                item = SLOTS * uses + s
                pe.wait_ge(gathered[s], 16 * uses + 16)
                pe.wait_ge(kept[s], uses + 1)
                o = ps[:, s, 0:D]
                nc.tensor.matmul(o, rows[:, s, B2:B2 + D], ident[:], is_transpose=True, start=True, stop=False
                                 ).then_inc(b2_read, 1)
                pe.wait_ge(scaled, SLOTS + item + 1)
                for l in range(LW):
                    end = nc.tensor.matmul(o, prod2[:, s, l, :], ident[:], is_transpose=True, start=False,
                                           stop=(out is None and l == LW - 1))
                if out is not None:
                    end = nc.tensor.matmul(o, ident[:], keep["xfT"][:, bass.ds(tile_of(k, s) * P, P)],
                                           start=False, stop=True)
                end.then_inc(summed[s], 1)

            def turn_back(k, uses, s):
                pe.wait_ge(kept[s], uses + 2)
                pe.wait_ge(finished[s], uses + 1)
                o = ps[:, BACK + s, 0:D]
                nc.tensor.matmul(o, mixT[:, s, :], ident[:], is_transpose=True, start=True, stop=False)
                nc.tensor.matmul(o, ident[:], keep["x_nat"][:, bass.ds(tile_of(k, s), 1), :].rearrange("p a d -> p (a d)"),
                                 start=False, stop=True).then_inc(back, 1)

            def run(n, k, uses, lot, nxt):
                if nxt is not None:
                    decide(nxt, k, lot)
                for s in range(SLOTS):
                    total(k, uses, s)
                    if out is not None and s >= 1:
                        turn_back(k, uses, s - 1)
                    if nxt is not None and s == 0:
                        count(lot)
                    if nxt is not None and s == 1:
                        name(lot)
                if out is not None:
                    turn_back(k, uses, SLOTS - 1)

            lots(pe, run, first)

        if out is not None:
            @block.sync
            def _(sp):
                def run(n, k, uses, _lot, _next):
                    for s in range(SLOTS):
                        sp.wait_ge(finished[s], uses + 2)
                        sp.dma_start(out[0, bass.ds(tile_of(k, s) * P, P), :], outs[:, s, :]).then_inc(stored[s], 16)

                lots(sp, run)
                for s in range(SLOTS):
                    sp.wait_ge(stored[s], 16 * NB + 1)


def attend_phase(nc, keep):
    ident, qkvT, xf, xfT = keep["ident"], keep["qkvT"], keep["xf"], keep["xfT"]
    with ExitStack() as ctx:
        def sb(name, shape, dt=F32):
            return ctx.enter_context(nc.sbuf_tensor(f"fa_{name}", shape, dt))

        def sem(name):
            return keep["semaphores"].enter_context(nc.semaphore(f"fa_{name}"))

        scores = ctx.enter_context(nc.psum_tensor("fa_scores", [P, NB, BANK], F32))
        turn = ctx.enter_context(nc.psum_tensor("fa_turn", [P, 2, BANK], F32))
        mixed = ctx.enter_context(nc.psum_tensor("fa_mixed", [P, 2, BANK], F32))
        v = sb("v", [P, NT, D])
        q = sb("q", [P, 2, P])
        prob = sb("prob", [P, 2, T])
        probT = sb("probT", [P, 2, NT, P])
        top = sb("top", [P, 2, 4])
        den = sb("den", [P, 2, 2])
        v_ps, v_ok, q_ok, scored, half_max, max_ok, neg_ok, exped, turned, kept_act, kept_dve, mixed_ok, inv_ok, y_ok = (
            sem(n) for n in ("v_ps", "v_ok", "q_ok", "scored", "half_max", "max_ok", "neg_ok", "exped", "turned",
                             "kept_act", "kept_dve", "mixed", "inv_ok", "y_ok"))
        yT_ps, yT_ok = sem("yT_ps"), sem("yT_ok")
        block = ctx.enter_context(nc.Block())

        def iterations(eng, run):
            run(0, 0, None, 1)
            with eng.Fori(0, NT // 2 - 1) as pair:
                run(2 * pair + 1, 1, 2 * pair, 0)
                run(2 * pair + 2, 0, 2 * pair + 1, 1)
            run(NT - 1, 1, NT - 2, 0)
            run(None, 0, NT - 1, 1)

        @block.gpsimd
        def _(pool):
            def run(i, p, _j, _p):
                if i is None:
                    return
                if not isinstance(i, int) or i > 1:
                    pool.wait_ge(scored, NB * (i - 1))
                nc.gpsimd.tensor_copy(q[:, p, :], qkvT[:, 0, bass.ds(i * P, P)]).then_inc(q_ok, 1)

            iterations(pool, run)

        @block.tensor
        def _(pe):
            for g in range(4):
                if g >= 2:
                    pe.wait_ge(v_ok, g - 1)
                for s in range(4):
                    t = 4 * g + s
                    last = nc.tensor.transpose(turn[:, g % 2, s * P:(s + 1) * P], qkvT[:, 2, t * P:(t + 1) * P], ident[:])
                last.then_inc(v_ps, 1)
            pe.wait_ge(v_ok, 4)

            def run(i, p, j, pj):
                if i is not None:
                    pe.wait_ge(q_ok, i + 1)
                    pe.wait_ge(exped, i)
                    for b in range(NB):
                        nc.tensor.matmul(scores[:, b, :], q[:, p, :], qkvT[:, 1, b * BANK:(b + 1) * BANK],
                                         start=True, stop=True).then_inc(scored, 1)
                if j is not None:
                    pe.wait_ge(exped, j + 1)
                    for g in range(4):
                        if g < 2:
                            pe.wait_ge(kept_dve, 2 * j)
                        else:
                            pe.wait_ge(kept_act, 2 * j + g - 1)
                        for s in range(4):
                            t = 4 * g + s
                            last = nc.tensor.transpose(turn[:, g % 2, s * P:(s + 1) * P], prob[:, pj, t * P:(t + 1) * P],
                                                       ident[:])
                        last.then_inc(turned, 1)
                    pe.wait_ge(y_ok, j)
                    for t in range(NT):
                        if t % 4 == 0:
                            g = t // 4
                            pe.wait_ge(kept_act if g < 2 else kept_dve, 2 * j + g % 2 + 1)
                        last = nc.tensor.matmul(mixed[:, pj, 0:D], probT[:, pj, t, :], v[:, t, :],
                                                start=(t == 0), stop=(t == NT - 1))
                    last.then_inc(mixed_ok, 1)

            iterations(pe, run)
            for g in range(4):
                pe.wait_ge(y_ok, NT)
                for s in range(4):
                    t = 4 * g + s
                    last = nc.tensor.transpose(scores[:, g, s * P:(s + 1) * P], xf[:, t, :], ident[:])
                last.then_inc(yT_ps, 1)

        @block.scalar
        def _(act):
            def run(i, p, j, pj):
                if j is not None:
                    for g in range(2):
                        act.wait_ge(turned, 4 * j + g + 1)
                        if g == 0:
                            act.wait_ge(mixed_ok, j)
                        nc.scalar.copy(probT[:, pj, 4 * g:4 * g + 4, :].rearrange("p s q -> p (s q)"), turn[:, g, :]
                                       ).then_inc(kept_act, 1)
                if i is not None:
                    act.wait_ge(neg_ok, i + 1)
                    if not isinstance(i, int) or i > 1:
                        act.wait_ge(turned, 4 * (i - 1))
                        act.wait_ge(y_ok, i - 1)
                    nc.scalar.activation(prob[:, p, :], scores[:].rearrange("p b k -> p (b k)"), ACT.Exp,
                                         bias=top[:, p, 3:4], scale=SCALE_F, accum_out=den[:, p, 0:1]).then_inc(exped, 1)

            iterations(act, run)

        @block.vector
        def _(dve):
            for g in range(4):
                dve.wait_ge(v_ps, g + 1)
                nc.vector.tensor_copy(v[:, 4 * g:4 * g + 4, :].rearrange("p s d -> p (s d)"), turn[:, g % 2, :]
                                      ).then_inc(v_ok, 1)

            def run(i, p, j, pj):
                if i is not None:
                    if not isinstance(i, int) or i > 1:
                        dve.wait_ge(exped, i - 1)
                    for half in range(2):
                        dve.wait_ge(scored, NB * i + 2 * half + 2)
                        nc.vector.tensor_reduce(top[:, p, half:half + 1], scores[:, 2 * half:2 * half + 2, :], AX.XY,
                                                ALU.max).then_inc(half_max, 1)
                    dve.wait_ge(half_max, 2 * i + 2)
                    nc.vector.tensor_tensor(top[:, p, 2:3], top[:, p, 0:1], top[:, p, 1:2], ALU.max).then_inc(max_ok, 1)
                    dve.wait_ge(max_ok, i + 1)
                    nc.vector.tensor_scalar(top[:, p, 3:4], top[:, p, 2:3], -SCALE_F, None, ALU.mult).then_inc(neg_ok, 1)
                if j is not None:
                    for g in range(2, 4):
                        dve.wait_ge(turned, 4 * j + g + 1)
                        if g == 2:
                            dve.wait_ge(mixed_ok, j)
                        nc.vector.tensor_copy(probT[:, pj, 4 * g:4 * g + 4, :].rearrange("p s q -> p (s q)"),
                                              turn[:, g - 2, :]).then_inc(kept_dve, 1)
                    dve.wait_ge(exped, j + 1)
                    nc.vector.reciprocal(den[:, pj, 1:2], den[:, pj, 0:1]).then_inc(inv_ok, 1)
                    dve.wait_ge(inv_ok, j + 1)
                    dve.wait_ge(mixed_ok, j + 1)
                    tile = xf[:, bass.ds(j, 1), :].rearrange("p a d -> p (a d)")
                    nc.vector.scalar_tensor_tensor(out=tile, in0=mixed[:, pj, 0:D], scalar=den[:, pj, 1:2], in1=tile,
                                                   op0=ALU.mult, op1=ALU.add).then_inc(y_ok, 1)

            iterations(dve, run)
            for g in range(4):
                dve.wait_ge(yT_ps, g + 1)
                nc.vector.tensor_copy(xfT[:, g * BANK:(g + 1) * BANK], scores[:, g, :]).then_inc(yT_ok, 1)
            dve.wait_ge(yT_ok, 4)


def feed_forward_phase(nc, a, keep, out):
    with ExitStack() as ctx:
        def sb(name, shape, dt=F32):
            return ctx.enter_context(nc.sbuf_tensor(name, shape, dt))

        keep["xf"] = sb("xf", [P, NT, D])
        keep["xfT"] = sb("xfT", [P, T])
        keep["qkvT"] = sb("qkvT", [P, 3, T])
        keep["leaf"] = sb("leaf", [P, 4, NT], I32)
        keep["nodes"] = {
            "nw": sb("nodes_nw", [P, 4, NODES]),
            "nb": sb("nodes_nb", [P, 4, 2]),
            "paths": sb("nodes_paths", [P, 2, LEAVES], BF16),
            "turns": sb("nodes_turns", [P, 2]),
            "number": sb("nodes_number", [P, 2], BF16),
        }
        norm_phase(nc, a, keep)
        leaves_phase(nc, a, ("q", "k", "v"), keep)
        attend_phase(nc, keep)
        leaves_phase(nc, a, ("f",), keep, out)


def adaln_block(nc, a, out):
    with ExitStack() as ctx:
        def sb(name, shape, dt=F32):
            return ctx.enter_context(nc.sbuf_tensor(name, shape, dt))

        keep = {
            "semaphores": ctx,
            "x_nat": sb("x_nat", [P, NT, D]),
            "ident": sb("ident", [P, P]),
            "modc": sb("modc", [P, 8]),
            "woT": sb("woT", [P, D]),
            "bo_row": sb("bo_row", [1, D]),
        }
        scratch = {
            "ext": nc.dram_tensor("ext_scratch", [2, P, EXT], F32, kind="Internal").ap(),
            "qk": nc.dram_tensor("qk_scratch", [2, P, T], F32, kind="Internal").ap(),
            "qst": nc.dram_tensor("q_stack", [H, ROW_M, T], BF16, kind="Internal").ap(),
            "klst": nc.dram_tensor("k_left_stack", [H, ROWS, T], BF16, kind="Internal").ap(),
            "krst": nc.dram_tensor("k_right_stack", [H, ROWS, T], BF16, kind="Internal").ap(),
            "ctx": nc.dram_tensor("context", [H, DK + 1, T], F32, kind="Internal").ap(),
        }
        with ExitStack() as inner:
            keep["v_all"] = inner.enter_context(nc.sbuf_tensor("v_all", [P, NT, D], F32))
            setup_phase(nc, a, keep, scratch)
            attention_phase(nc, keep, scratch)
        output_phase(nc, keep, scratch)
        feed_forward_phase(nc, a, keep, out)


_OUT = (1, T, D)


def path_constants():
    paths = np.zeros((NODES, LEAVES), np.float32)
    turns = np.zeros((LEAVES, 1), np.float32)
    for leaf in range(LEAVES):
        for level in range(DEPTH):
            right = leaf >> (DEPTH - 1 - level) & 1
            paths[2 ** level - 1 + (leaf >> (DEPTH - level)), leaf] = 1 if right else -1
            turns[leaf] += right
    number = np.arange(LEAVES, dtype=np.float32).reshape(2, P).T
    return paths, np.ascontiguousarray(turns.reshape(2, P).T), np.ascontiguousarray(number)


def kernel(**inputs):
    import concourse.bacc as _bacc
    import ml_dtypes as _ml
    from concourse.bass_utils import run_bass_kernel_spmd as _run

    def given(name):
        return np.asarray(inputs[f"L0_{name}"])

    lay = {"x": given("attn_x"), "wmod": given("wmod"), "Wo": given("attn_Wo")}
    for w in ("Wq", "Wk", "Wv", "Wpk", "Wpq"):
        lay[w + "T"] = given("attn_" + w).T
    lay["relT"] = given("attn_rel_emb").T
    lay["relT_rev"] = given("attn_rel_emb")[::-1].T
    lay["c"] = given("c").reshape(D, 1)
    for b in ("bq", "bk", "bpk", "bpq", "bo"):
        lay[b] = given("attn_" + b).reshape(D, 1)
    lay["bv"] = given("attn_bv").reshape(1, D)
    for tree in "qkvf":
        w1, b1, w2, b2 = (given(f"ffn_{tree}_{n}") for n in ("w1", "b1", "w2", "b2"))
        lay[f"{tree}_leaves"] = np.concatenate(
            [w1.transpose(0, 2, 1).reshape(LEAVES, LW * D), w2.reshape(LEAVES, LW * D), b1, b2], axis=1)
        lay[f"{tree}_nwT"] = given(f"ffn_{tree}_nw").T
        lay[f"{tree}_nb"] = given(f"ffn_{tree}_nb").reshape(NODES, 1)
    paths, turns, number = path_constants()
    lay["paths"], lay["turns"], lay["number"] = paths.astype(_ml.bfloat16), turns, number.astype(_ml.bfloat16)

    nc = _bacc.Bacc("TRN2", target_bir_lowering=False, num_devices=1)
    arrays, a = {}, {}
    for name, value in lay.items():
        arrays[f"in_{name}"] = value = np.ascontiguousarray(value)
        a[name] = nc.dram_tensor(f"in_{name}", value.shape, mybir.dt.from_np(value.dtype), kind="ExternalInput").ap()
    out = nc.dram_tensor("out_0", _OUT, F32, kind="ExternalOutput").ap()
    adaln_block(nc, a, out)
    r = _run(nc, [arrays], core_ids=[0])
    return r.results[0]["out_0"]
```

```python
from contextlib import ExitStack

import numpy as np

import concourse.bass as bass
from concourse import mybir

ALU = mybir.AluOpType
ACT = mybir.ActivationFunctionType
AX = mybir.AxisListType
F32 = mybir.dt.float32
BF16 = mybir.dt.bfloat16
I32 = mybir.dt.int32

P = 128
D = 128
T = 2048
NT = T // P
BANK = 512
NB = T // BANK
H = 16
DK = D // H
SPAN = 64
R = 2 * SPAN
SCALE = float((3 * DK) ** -0.5)
EPS = 1e-5

PART_A = (0, 0, 1, 1, 0, 2)
PART_B = (0, 1, 0, 1, 2, 0)
ROW_QK = len(PART_A) * DK
ROW_CL = ROW_QK
ROW_CR = ROW_CL + 3
ROW_S = ROW_CR + 3
ROW_M = ROW_S + 3
ROWS = ROW_M + 3

CL = P // DK
WIN = 2 * P
EXT = WIN + P - 1
TABW = EXT - CL + 1
KEY0 = P - CL
QRY0 = WIN - CL


def near_far(i):
    lo, hi = max(P * i - SPAN, 0), min(P * i - SPAN + WIN, T)
    return (lo, hi), (0, lo), (hi, T)


def far_units(i):
    _, left, right = near_far(i)
    pieces = [(True, *left), (False, *right)]
    total = sum(b - a for _, a, b in pieces)
    size = total // FU
    units = []
    for u in range(FU):
        a, b, at, unit = u * size, (u + 1) * size, 0, []
        for is_left, p, q in pieces:
            s, e = max(a, at), min(b, at + q - p)
            if e > s:
                unit.append((is_left, p + s - at, e - s, s - a))
            at += q - p
        units.append((size, unit))
    return units


FU = 4
N_C2P = 8
N_WIN = 8
N_FAR = NT * FU
N_A = N_C2P + N_WIN + N_FAR + 1
RING = 3
assert N_A % RING == 0
FIRST_NEAR = 3
FIRST_SHARE, LAST_SHARE = 1.8, 0.3
N_B = 2 * NT
GI = NT // 2


def setup_phase(nc, a, keep, scratch):
    x_nat, ident, modc = keep["x_nat"], keep["ident"], keep["modc"]
    with ExitStack() as ctx:
        def sb(name, shape, dt=F32):
            return ctx.enter_context(nc.sbuf_tensor(name, shape, dt))

        def sem(name):
            return keep["semaphores"].enter_context(nc.semaphore(name))

        ps = ctx.enter_context(nc.psum_tensor("su_ps", [P, 8, BANK], F32))
        wmod = sb("su_wmod", [P, 6 * D])
        wts = sb("su_wts", [P, 6, D])
        rel = sb("su_rel", [P, 2, R])
        cols = sb("su_cols", [P, 8])
        bvrow = sb("su_bvrow", [1, D])
        ones_row = sb("su_ones_row", [1, P])
        silu = sb("su_silu", [P, 4])
        stats = sb("su_stats", [P, NT, 6])
        mv = sb("su_mv", [P, NT, 2])
        rstd = sb("su_rstd", [P, NT])
        expo = sb("su_expo", [P, NT])
        xn = sb("su_xn", [P, NT, D])
        hT = sb("su_hT", [P, T])
        qkT = sb("su_qkT", [P, 2, T])
        posT = sb("su_posT", [P, 2, R])
        ext = sb("su_ext", [P, 2, EXT])
        head_mask = sb("su_hm", [P, H])
        ends = sb("su_ends", [P, 2, 2, H])
        aux = sb("su_aux", [4 * H, T])
        rest = sb("su_rest", [P, 2, T])
        part = sb("su_part", [P, 2, 3, T], BF16)
        auxp = sb("su_auxp", [4 * H, 3, T], BF16)
        oz = sb("su_oz", [H, 2, T], BF16)
        zer = sb("su_zer", [P, P])
        clampt = sb("su_clamp", [P, 4, 2])
        wog = sb("su_wog", [P, D])

        in_x, in_w, in_small = sem("in_x"), sem("in_w"), sem("in_small")
        made, vec, sil = sem("made"), sem("vec"), sem("sil")
        mod_ps, xt_ps, pos_ps, qk_ps, aux_ps, v_ps, wo_ps = (
            sem(n) for n in ("mod_ps", "xt_ps", "pos_ps", "qk_ps", "aux_ps", "v_ps", "wo_ps"))
        xn_ok, hT_ok, pos_ok, q_ok, k_ok, ends_ok, wog_ok, v_ok, mod_ok = (
            sem(n) for n in ("xn_ok", "hT_ok", "pos_ok", "su_q_ok", "su_k_ok", "ends_ok", "wog_ok", "v_ok", "mod_ok"))
        ext_ok, q_parts, k_parts, k_left, aux_ok, aux_parts, stored = (
            sem(n) for n in ("ext_ok", "q_parts", "k_parts", "k_left", "aux_ok", "aux_parts", "stored"))
        var_ok, rstd_ok = sem("var_ok"), sem("rstd_ok")
        block = ctx.enter_context(nc.Block())

        @block.sync
        def _(sp):
            sp.dma_start(x_nat[:], a["x"].rearrange("a (n p) d -> p (a n) d", p=P)).then_inc(in_x, 16)
            sp.dma_start(wmod[:], a["wmod"]).then_inc(in_w, 16)
            for n, name in enumerate(("WqT", "WkT", "WvT", "WpkT", "WpqT", "Wo")):
                sp.dma_start(wts[:, n, :], a[name]).then_inc(in_w, 16)
            sp.dma_start(rel[:, 0, :], a["relT"]).then_inc(in_w, 16)
            sp.dma_start(rel[:, 1, :], a["relT_rev"]).then_inc(in_w, 16)
            for n, name in enumerate(("c", "bq", "bk", "bpk", "bpq", "bo")):
                sp.dma_start(cols[:, n:n + 1], a[name]).then_inc(in_small, 16)
            sp.dma_start(bvrow[:], a["bv"]).then_inc(in_small, 16)
            n_stored = 0

            def store(dst, src):
                nonlocal n_stored
                sp.dma_start(dst, src).then_inc(stored, 16)
                n_stored += 1

            sp.wait_ge(made, 9)
            qs, kl, kr = scratch["qst"], scratch["klst"], scratch["krst"]
            for r in range(3):
                store(qs[:, ROW_S + r, :], oz[:, 0, :])
                store(kl[:, ROW_CL + r, :], oz[:, 0, :])
                store(kl[:, ROW_CR + r, :], oz[:, 1, :])
                store(kr[:, ROW_CL - ROW_QK + r, :], oz[:, 1, :])
                store(kr[:, ROW_CR - ROW_QK + r, :], oz[:, 0, :])
                store(kl[:, ROW_M + r, :], oz[:, 0, :])
                store(kr[:, ROW_M - ROW_QK + r, :], oz[:, 0, :])
            sp.wait_ge(ext_ok, 2)
            store(scratch["ext"].rearrange("w c e -> c w e"), ext[:])
            sp.wait_ge(q_ok, NB)
            sp.wait_ge(k_ok, NB)
            store(scratch["qk"].rearrange("w c t -> c w t"), qkT[:])
            for r in range(3):
                for w, (dst, order, done) in enumerate(((qs, PART_A, q_parts), (kl, PART_B, k_parts))):
                    sp.wait_ge(done, r + 1)
                    for g in range(len(order)):
                        if order[g] == r:
                            store(dst[:, g * DK:(g + 1) * DK, :], part[:, w, r, :])
            for r in range(3):
                sp.wait_ge(aux_parts, r + 1)
                store(qs[:, ROW_CL + r, :], auxp[0:H, r, :])
                store(qs[:, ROW_CR + r, :], auxp[H:2 * H, r, :])
                store(kl[:, ROW_S + r, :], auxp[2 * H:3 * H, r, :])
                store(kr[:, ROW_S - ROW_QK + r, :], auxp[3 * H:4 * H, r, :])
            sp.wait_ge(stored, 16 * n_stored)

        @block.gpsimd
        def _(pool):
            n_made = 0

            def make(ins):
                nonlocal n_made
                n_made += 1
                ins.then_inc(made, 1)
                pool.wait_ge(made, n_made)

            make(nc.gpsimd.memset(ident[:], 0.0))
            make(nc.gpsimd.affine_select(out=ident[:], in_=ident[:], compare_op=ALU.not_equal, fill=1.0,
                                         base=0, pattern=[[-1, P]], channel_multiplier=1))
            make(nc.gpsimd.memset(oz[:, 0, :], 1.0))
            make(nc.gpsimd.memset(oz[:, 1, :], 0.0))
            make(nc.gpsimd.memset(ones_row[:], 1.0))
            make(nc.gpsimd.memset(zer[:], 0.0))
            make(nc.gpsimd.memset(head_mask[:], 1.0))
            make(nc.gpsimd.affine_select(out=head_mask[:], in_=head_mask[:], compare_op=ALU.is_ge, fill=0.0,
                                         base=0, pattern=[[-DK, H]], channel_multiplier=1))
            make(nc.gpsimd.affine_select(out=head_mask[:], in_=head_mask[:], compare_op=ALU.is_ge, fill=0.0,
                                         base=DK - 1, pattern=[[DK, H]], channel_multiplier=-1))
            pool.wait_ge(var_ok, 1)
            make(nc.gpsimd.memset(expo[:], -0.5))
            make(nc.gpsimd.tensor_scalar(rstd[:], mv[:, :, 1], EPS, None, ALU.add))
            nc.gpsimd.tensor_tensor(rstd[:], rstd[:], expo[:], ALU.pow).then_inc(rstd_ok, 1)
            for r in range(2):
                pool.wait_ge(k_parts, r + 1)
                if r:
                    pool.wait_ge(k_left, r)
                nc.gpsimd.tensor_tensor(rest[:, 1, :], rest[:, 1, :] if r else qkT[:, 1, :], part[:, 1, r, :],
                                        ALU.subtract).then_inc(k_left, 1)

        @block.scalar
        def _(act):
            act.wait_ge(in_small, 16 * 7)
            nc.scalar.activation(silu[:, 0:1], cols[:, 0:1], ACT.Exp, scale=-1.0).then_inc(sil, 1)
            for b in range(NB):
                act.wait_ge(qk_ps, NB + b + 1)
                nc.scalar.activation(qkT[:, 1, b * BANK:(b + 1) * BANK], ps[:, 4 + b, :], ACT.Identity,
                                     bias=cols[:, 2:3]).then_inc(k_ok, 1)
            act.wait_ge(k_ok, NB)
            nc.scalar.copy(part[:, 1, 0, :], qkT[:, 1, :]).then_inc(k_parts, 1)
            for r in range(2):
                act.wait_ge(k_left, r + 1)
                nc.scalar.copy(part[:, 1, r + 1, :], rest[:, 1, :]).then_inc(k_parts, 1)
            for b in range(NB):
                act.wait_ge(v_ps, b + 1)
                nc.scalar.copy(keep["v_all"][:, 4 * b:4 * b + 4, :], ps[:, 4 + b, :].rearrange("p (s d) -> p s d", s=4)
                               ).then_inc(v_ok, 1)
            act.wait_ge(v_ok, NB)

        @block.tensor
        def _(pe):
            pe.wait_ge(in_w, 16 * 9)
            pe.wait_ge(sil, 2)
            for n in range(6):
                last = nc.tensor.matmul(ps[:, 0, n:n + 1], wmod[:, n * D:(n + 1) * D], silu[:, 3:4],
                                        start=True, stop=True)
            last.then_inc(mod_ps, 1)
            for w in range(2):
                last = nc.tensor.matmul(ps[:, 1 + w, 0:R], wts[:, 3 + w, :], rel[:, w, :], start=True, stop=True)
            last.then_inc(pos_ps, 1)
            pe.wait_ge(made, 9)
            pe.wait_ge(xn_ok, NT)
            for b in range(NB):
                for s in range(4):
                    last = nc.tensor.transpose(ps[:, 4 + b, s * P:(s + 1) * P], xn[:, 4 * b + s, :], ident[:])
                last.then_inc(xt_ps, 1)
            pe.wait_ge(pos_ok, 2)
            pe.wait_ge(mod_ok, 1)
            for w in range(2):
                for b in range(NB):
                    pe.wait_ge(hT_ok, b + 1)
                    nc.tensor.matmul(ps[:, 4 * w + b, :], wts[:, w, :], hT[:, b * BANK:(b + 1) * BANK],
                                     start=True, stop=True).then_inc(qk_ps, 1)
            pe.wait_ge(ends_ok, 4)
            pe.wait_ge(q_ok, NB)
            for b in range(NB):
                pe.wait_ge(k_ok, b + 1)
                for w in range(2):
                    last = nc.tensor.matmul(ps[2 * H * w:2 * H * (w + 1), b, :],
                                            ends[:, w, :, :].rearrange("p e h -> p (e h)"),
                                            qkT[:, w, b * BANK:(b + 1) * BANK], start=True, stop=True,
                                            skip_group_check=True)
                last.then_inc(aux_ps, 1)
            for b in range(NB):
                for s in range(4):
                    t = 4 * b + s
                    nc.tensor.matmul(ps[:, 4 + b, s * P:(s + 1) * P], hT[:, t * P:(t + 1) * P], wts[:, 2, :],
                                     start=True, stop=False)
                    last = nc.tensor.matmul(ps[:, 4 + b, s * P:(s + 1) * P], ones_row[:], bvrow[:],
                                            start=False, stop=True)
                last.then_inc(v_ps, 1)
            pe.wait_ge(wog_ok, 2)
            pe.wait_ge(aux_ok, NB)
            nc.tensor.transpose(ps[:, 0, 0:D], wog[:], ident[:])
            nc.tensor.matmul(ps[0:1, 1, 0:D], cols[:, 6:7], ident[:], start=True, stop=True).then_inc(wo_ps, 1)

        @block.vector
        def _(dve):
            n_vec = 0

            def step(ins, *more):
                nonlocal n_vec
                n_vec += 1
                ins.then_inc(vec, 1)
                dve.wait_ge(vec, n_vec)

            dve.wait_ge(in_x, 16)
            for t in range(NT):
                ins = nc.vector.bn_stats(stats[:, t, :], x_nat[:, t, :])
            step(ins)
            for t in range(NT):
                ins = nc.vector.bn_aggr(mv[:, t, :], stats[:, t, :])
            ins.then_inc(var_ok, 1)
            dve.wait_ge(rstd_ok, 1)
            for t in range(NT):
                nc.vector.tensor_scalar(xn[:, t, :], x_nat[:, t, :], mv[:, t, 0:1], rstd[:, t:t + 1],
                                        ALU.subtract, ALU.mult).then_inc(xn_ok, 1)
            dve.wait_ge(sil, 1)
            step(nc.vector.tensor_scalar(silu[:, 1:2], silu[:, 0:1], 1.0, None, ALU.add))
            step(nc.vector.reciprocal(silu[:, 2:3], silu[:, 1:2]))
            nc.vector.tensor_tensor(silu[:, 3:4], silu[:, 2:3], cols[:, 0:1], ALU.mult).then_inc(sil, 1)
            dve.wait_ge(mod_ps, 1)
            step(nc.vector.tensor_copy(modc[:, 0:6], ps[:, 0, 0:6]))
            for n, g in enumerate((2, 5)):
                step(nc.vector.tensor_scalar(clampt[:, 0, n:n + 1], modc[:, g:g + 1], 0.0, 2.0, ALU.is_ge, ALU.mult))
                step(nc.vector.tensor_scalar(clampt[:, 1, n:n + 1], clampt[:, 0, n:n + 1], -1.0, None, ALU.add))
                step(nc.vector.tensor_scalar(clampt[:, 2, n:n + 1], modc[:, g:g + 1], -1.0, None, ALU.mult))
                step(nc.vector.tensor_tensor(clampt[:, 3, n:n + 1], modc[:, g:g + 1], clampt[:, 2, n:n + 1], ALU.max))
                step(nc.vector.scalar_tensor_tensor(out=modc[:, g:g + 1], in0=clampt[:, 3, n:n + 1], scalar=0.25,
                                                    in1=clampt[:, 1, n:n + 1], op0=ALU.max, op1=ALU.mult))
                step(nc.vector.tensor_scalar(modc[:, g - 1:g], modc[:, g - 1:g], 1.0, None, ALU.add))
            nc.vector.tensor_copy(silu[:, 0:1], modc[:, 0:1]).then_inc(mod_ok, 1)
            dve.wait_ge(pos_ps, 1)
            for w in range(2):
                nc.vector.tensor_scalar(posT[:, w, :], ps[:, 1 + w, 0:R], cols[:, 3 + w:4 + w], None,
                                        ALU.add).then_inc(pos_ok, 1)
            dve.wait_ge(pos_ok, 2)
            dve.wait_ge(made, 9)
            for w in range(2):
                first = P - 1 + w
                nc.vector.tensor_scalar(ext[:, w, 0:first], columns(zer, first), posT[:, w, 0:1], None, ALU.add)
                nc.vector.tensor_copy(ext[:, w, first:first + R], posT[:, w, :])
                nc.vector.tensor_scalar(ext[:, w, first + R:EXT], columns(zer, EXT - first - R), posT[:, w, R - 1:R],
                                        None, ALU.add).then_inc(ext_ok, 1)
                for e in range(2):
                    col = 0 if e == w else R - 1
                    nc.vector.tensor_scalar(ends[:, w, e, :], head_mask[:], posT[:, w, col:col + 1], None,
                                            ALU.mult).then_inc(ends_ok, 1)
            for b in range(NB):
                dve.wait_ge(xt_ps, b + 1)
                nc.vector.tensor_scalar(hT[:, b * BANK:(b + 1) * BANK], ps[:, 4 + b, :], modc[:, 1:2], modc[:, 0:1],
                                        ALU.mult, ALU.add).then_inc(hT_ok, 1)
            for b in range(NB):
                dve.wait_ge(qk_ps, b + 1)
                nc.vector.tensor_scalar(qkT[:, 0, b * BANK:(b + 1) * BANK], ps[:, b, :], cols[:, 1:2],
                                        None, ALU.add).then_inc(q_ok, 1)
            dve.wait_ge(q_ok, NB)

            def split(out, whole, left, done):
                ins = nc.vector.tensor_copy(out[:, 0, :], whole)
                ins.then_inc(done, 1)
                dve.wait_ge(done, 1)
                step(nc.vector.tensor_tensor(left, whole, out[:, 0, :], ALU.subtract))
                nc.vector.tensor_copy(out[:, 1, :], left).then_inc(done, 1)
                dve.wait_ge(done, 2)
                step(nc.vector.tensor_tensor(left, left, out[:, 1, :], ALU.subtract))
                nc.vector.tensor_copy(out[:, 2, :], left).then_inc(done, 1)

            split(part[:, 0], qkT[:, 0, :], rest[:, 0, :], q_parts)
            for b in range(NB):
                dve.wait_ge(aux_ps, b + 1)
                nc.vector.tensor_copy(aux[:, b * BANK:(b + 1) * BANK], ps[0:4 * H, b, :]).then_inc(aux_ok, 1)
            dve.wait_ge(aux_ok, NB)
            dve.wait_ge(q_parts, 3)
            split(auxp, aux[:], rest[0:4 * H, 0, :], aux_parts)
            nc.vector.tensor_scalar(wog[:], wts[:, 5, :], modc[:, 2:3], None, ALU.mult).then_inc(wog_ok, 1)
            nc.vector.tensor_tensor(cols[:, 6:7], cols[:, 5:6], modc[:, 2:3], ALU.mult).then_inc(wog_ok, 1)
            dve.wait_ge(wo_ps, 1)
            nc.vector.tensor_copy(keep["woT"][:], ps[:, 0, 0:D])
            nc.vector.tensor_copy(keep["bo_row"][:], ps[0:1, 1, 0:D])


def columns(zer, n):
    return zer[:, 0:n]


def attention_phase(nc, keep, scratch):
    ident = keep["ident"]
    with ExitStack() as ctx:
        def sb(name, shape, dt=F32):
            return ctx.enter_context(nc.sbuf_tensor(name, shape, dt))

        def sem(name):
            return keep["semaphores"].enter_context(nc.semaphore(name))

        ring = ctx.enter_context(nc.psum_tensor("at_ring", [P, RING, BANK], F32))
        scores = ctx.enter_context(nc.psum_tensor("at_scores", [P, 2, 2, BANK], F32))
        ctx_ps = ctx.enter_context(nc.psum_tensor("at_ctx", [P, BANK], F32))

        qa, la, ra = (sb(f"at_{n}a", [P, 2, T], BF16) for n in "qlr")
        qb, lb, rb = (sb(f"at_{n}b", [ROWS, 2, T], BF16) for n in "qlr")
        tab = sb("at_tab", [P, 2, TABW])
        diag = sb("at_diag", [P, 2, T])
        class_mask = sb("at_class", [P, CL])
        c2p = sb("at_c2p", [P, 2, NT, P])
        win = sb("at_win", [P, 2, NT, WIN + 2 * SPAN])
        mx = sb("at_mx", [P, NT, 8])
        mrow = sb("at_mrow", [P, 2, NT])
        mpart = sb("at_mpart", [NT, 2, 3, P], BF16)
        mleft = sb("at_mleft", [NT, 2, P])
        onlym = sb("at_onlym", [ROWS, P], BF16)
        prob = sb("at_prob", [P, 4, 2 * BANK])
        vh = sb("at_vh", [P, 2, NT, 32])
        ctx_sb = sb("at_ctx_sb", [P, 2, BANK])

        stack_a = [sem("stack_a0"), sem("stack_a1")]
        stack_b = [sem("stack_b0"), sem("stack_b1")]
        m_rows = [sem("m_rows0"), sem("m_rows1")]
        tables_in, tables_ok = ([sem(f"{n}{w}") for w in range(2)] for n in ("tables_in", "tables_ok"))
        made, v_ok = sem("at_made"), sem("vh_ok")
        unit, c2p_kept, win_kept, win_max, far_max, m_turned, m_split, maxed = (
            sem(n) for n in ("unit", "c2p_kept", "win_kept", "win_max", "far_max", "m_turned", "m_split", "maxed"))
        cleared, m_left = sem("cleared"), sem("m_left")
        score, exped, pv, ctx_kept = (sem(n) for n in ("score", "exped", "pv", "ctx_kept"))
        ctx_out = [sem("ctx_out0"), sem("ctx_out1")]
        block = ctx.enter_context(nc.Block())

        STEPS = NT + 1
        near, far = iter(range(N_C2P + N_WIN)), iter(range(N_C2P + N_WIN, N_A - 1))
        rest = N_FAR - FIRST_NEAR
        spaced = [1] * FIRST_NEAR + [rest * (n + 1) // (N_C2P + N_WIN - FIRST_NEAR) -
                                     rest * n // (N_C2P + N_WIN - FIRST_NEAR)
                                     for n in range(N_C2P + N_WIN - FIRST_NEAR)]
        ORDER = [n for few in spaced for n in (next(near), *(next(far) for _ in range(few)))] + [N_A - 1]
        weight = [2 if n < N_C2P else 4 if n < N_C2P + N_WIN else 1 for n in ORDER]
        share = [FIRST_SHARE] + [1.0] * (NT - 1) + [LAST_SHARE]
        ends = [sum(share[:s + 1]) * sum(weight[:-1]) / sum(share) for s in range(STEPS)]
        step_of = [next(s for s in range(STEPS) if sum(weight[:pos]) < ends[s] + 1e-6) for pos in range(N_A - 1)] + [NT]

        def bank(ha, pos):
            n = pos % (RING + 4)
            if isinstance(ha, int) and ha == 0 and pos < N_A - 1 and n >= RING:
                return scores[:, (n - RING) // 2, (n - RING) % 2, :]
            return ring[:, n if isinstance(ha, int) and ha == 0 and pos < N_A - 1 else pos % RING, :]

        def merged(ha, hb):
            for s in range(STEPS):
                us = [("a", pos) for pos in range(N_A) if step_of[pos] == s] if ha is not None else []
                ks = [("b", 2 * (s - 1)), ("b", 2 * (s - 1) + 1)] if hb is not None and s > 0 else []
                n = max(len(us), 1)
                for x in range(n):
                    yield from us[x:x + 1]
                    yield from ks[x * len(ks) // n:(x + 1) * len(ks) // n]

        def iterations(eng, run):
            run(0, 0, None, 1)
            run(1, 1, 0, 0)
            with eng.Fori(0, H // 2 - 2) as pair:
                run(2 * pair + 2, 0, 2 * pair + 1, 1)
                run(2 * pair + 3, 1, 2 * pair + 2, 0)
            run(H - 2, 0, H - 3, 1)
            run(H - 1, 1, H - 2, 0)
            run(None, 0, H - 1, 1)

        def loads_of(h, p):
            return h - p + 2

        def window_tiles(n):
            q, g = n // 2, n % 2
            first, end = g * GI, (g + 1) * GI
            if q == 0 and g == 0:
                first += 1
            if q == 3 and g == 1:
                end -= 1
            return q, first, end

        @block.sync
        def _(sp):
            def load_tables(h, w):
                sp.dma_start(tab[:, w, :], shifted(scratch["ext"][w, bass.ds(h * DK, DK), :])).then_inc(tables_in[w], 16)
                sp.dma_start(diag[:, w, :], repeated(scratch["qk"][w, bass.ds(h * DK, DK), :])).then_inc(tables_in[w], 16)

            def load_rows(dst, stack, h, rows, done):
                sp.dma_start(dst, scratch[stack][bass.ds(h, 1), 0:rows].rearrange("a r t -> (a r) t")).then_inc(done, 16)

            def load_stacks(h, p, q, l, r, done):
                load_rows(q[0:ROW_M, p, :], "qst", h, ROW_M, done[p])
                load_rows(l[0:ROWS, p, :], "klst", h, ROWS, done[p])
                load_rows(r[0:ROW_QK, p, :], "klst", h, ROW_QK, done[p])
                load_rows(r[ROW_QK:ROWS, p, :], "krst", h, ROWS - ROW_QK, done[p])

            def load_stacks_a(h, p):
                load_stacks(h, p, qa, la, ra, stack_a)
                load_rows(qa[SPAN:SPAN + ROW_QK, p, :], "qst", h, ROW_QK, stack_a[p])
                load_rows(la[SPAN:SPAN + ROW_QK, p, :], "klst", h, ROW_QK, stack_a[p])

            for p in range(2):
                sp.sem_inc(ctx_out[p], 16)
            load_tables(0, 0)
            load_stacks_a(0, 0)
            load_tables(0, 1)

            def run(ha, pa, hb, pb):
                if ha is not None and not (isinstance(ha, int) and ha == H - 1):
                    if hb is not None:
                        sp.wait_ge(m_turned, ha)
                    load_stacks_a(ha + 1, 1 - pa)
                if ha is not None:
                    if not isinstance(ha, int) or ha > 1:
                        sp.wait_ge(pv, (ha - 1) * N_B)
                    load_stacks(ha, pa, qb, lb, rb, stack_b)
                    if not (isinstance(ha, int) and ha == H - 1):
                        sp.wait_ge(c2p_kept, (ha + 1) * N_C2P)
                        load_tables(ha + 1, 0)
                        sp.wait_ge(win_kept, (ha + 1) * N_WIN)
                        load_tables(ha + 1, 1)
                    sp.wait_ge(m_split, 3 * (ha + 1))
                    for r in range(3):
                        sp.dma_start(qb[ROW_M + r:ROW_M + r + 1, pa, :].rearrange("a (n q) -> a n q", q=P),
                                     mpart[:, pa, r, :]).then_inc(m_rows[pa], 16)
                if hb is not None:
                    sp.wait_ge(ctx_kept, hb + 1)
                    for g in range(NB):
                        sp.dma_start(scratch["ctx"][bass.ds(hb, 1), :, g * BANK:(g + 1) * BANK].rearrange("a r t -> (a r) t"),
                                     ctx_sb[32 * g:32 * g + DK + 1, pb, :]).then_inc(ctx_out[pb], 16)

            iterations(sp, run)
            for p in range(2):
                sp.wait_ge(ctx_out[p], 16 * NB * (H // 2) + 16)

        @block.gpsimd
        def _(pool):
            n_made = 0

            def make(ins):
                nonlocal n_made
                n_made += 1
                ins.then_inc(made, 1)
                pool.wait_ge(made, n_made)

            make(nc.gpsimd.memset(class_mask[:], 1.0))
            make(nc.gpsimd.affine_select(out=class_mask[:], in_=class_mask[:], compare_op=ALU.is_ge, fill=0.0,
                                         base=-DK * (CL - 1), pattern=[[DK, CL]], channel_multiplier=1))
            make(nc.gpsimd.affine_select(out=class_mask[:], in_=class_mask[:], compare_op=ALU.is_ge, fill=0.0,
                                         base=P - 1, pattern=[[-DK, CL]], channel_multiplier=-1))
            def mask_classes(ha):
                for w in range(2):
                    pool.wait_ge(tables_in[w], (ha + 1) * 32)
                    v = diag[:, w, :].rearrange("p (n t) -> p n t", t=CL)
                    nc.gpsimd.tensor_tensor(v, v, class_mask[:, None, :].to_broadcast([P, T // CL, CL]), ALU.mult
                                            ).then_inc(tables_ok[w], 1)

            mask_classes(0)
            make(nc.gpsimd.memset(win[:], 0.0))
            make(nc.gpsimd.memset(onlym[:], 1.0))
            make(nc.gpsimd.affine_select(out=onlym[:], in_=onlym[:], compare_op=ALU.is_ge, fill=0.0,
                                         base=-ROW_M, pattern=[[0, P]], channel_multiplier=1))
            make(nc.gpsimd.memset(vh[:], 0.0))
            make(nc.gpsimd.memset(vh[:, :, :, DK:DK + 1], 1.0))

            def run(ha, pa, hb, pb):
                if ha is None:
                    return
                if not (isinstance(ha, int) and ha == 0):
                    mask_classes(ha)
                if not isinstance(ha, int) or ha > 1:
                    pool.wait_ge(pv, (ha - 1) * N_B)
                nc.gpsimd.tensor_copy(vh[:, pa, :, 0:DK], keep["v_all"][:, :, bass.ds(ha * DK, DK)]).then_inc(v_ok, 1)

            iterations(pool, run)

        @block.tensor
        def _(pe):
            def free_ring(ha, pos):
                if isinstance(ha, int) and ha == 1 and pos < RING:
                    pe.wait_ge(m_split, 3)
                    return
                pos -= RING + 4 if isinstance(ha, int) and ha == 0 else RING
                if pos < 0:
                    if isinstance(ha, int) and ha == 0:
                        return
                    ha, pos = ha - 1, pos + N_A
                n = ORDER[pos]
                if n < N_C2P:
                    pe.wait_ge(c2p_kept, ha * N_C2P + n + 1)
                elif n < N_C2P + N_WIN:
                    pe.wait_ge(win_kept, ha * N_WIN + n - N_C2P + 1)
                elif n < N_A - 1:
                    pe.wait_ge(far_max, ha * N_FAR + n - N_C2P - N_WIN + 1)
                else:
                    pe.wait_ge(m_split, 3 * (ha + 1))

            def unit_a(ha, pa, pos):
                n, out = ORDER[pos], bank(ha, pos)
                free_ring(ha, pos)
                if n == 0:
                    pe.wait_ge(tables_ok[0], ha + 1)
                    pe.wait_ge(stack_a[pa], loads_of(ha, pa) * 48)
                if n < N_C2P:
                    half, qh, g = n // 4, n // 2 % 2, n % 2
                    v = out.rearrange("p (i q) -> p i q", q=P // 2)
                    toks = diag[:, 0, g * GI * P:(g + 1) * GI * P].rearrange("p (i q) -> p i q", q=P)
                    for c in range(4):
                        col = KEY0 + P * half - CL * (4 * qh + c)
                        at = P // 2 * qh + CL * c
                        last = nc.tensor.matmul(v[:, :, CL * c:CL * (c + 1)], tab[:, 0, col:col + P],
                                                toks[:, :, at:at + CL], start=(c == 0), stop=True,
                                                skip_group_check=True)
                elif n < N_C2P + N_WIN:
                    q, first, end = window_tiles(n - N_C2P)
                    if n == N_C2P:
                        pe.wait_ge(tables_ok[1], ha + 1)
                        pe.wait_ge(c2p_kept, (ha + 1) * N_C2P)
                    v = out.rearrange("p (i k) -> p i k", k=SPAN)[:, 0:end - first, :]
                    k0 = P * first - SPAN + SPAN * q
                    for c in range(4):
                        col = QRY0 - CL * (4 * q + c)
                        nc.tensor.matmul(v[:, :, CL * c:CL * (c + 1)], tab[:, 1, col:col + P],
                                         strided(diag[:, 1, k0 + CL * c:k0 + CL * (c + 1)], P, end - first),
                                         start=(c == 0), stop=False, skip_group_check=True)
                    keys = slice(SPAN * (q % 2), SPAN * (q % 2 + 1))
                    rows = slice(keys.start, keys.start + ROW_QK)
                    for i in range(first, end):
                        nc.tensor.matmul(v[:, i - first, :], qa[rows, pa, P * i:P * (i + 1)],
                                         la[rows, pa, P * i - SPAN + SPAN * q:P * i + SPAN * q],
                                         start=False, stop=False, skip_group_check=True)
                    for i in range(first, end):
                        last = nc.tensor.matmul(v[:, i - first, :], c2p[keys, q // 2, i, :], ident[keys, keys],
                                                is_transpose=True, start=False, stop=True, skip_group_check=True)
                elif n < N_A - 1:
                    i, u = divmod(n - N_C2P - N_WIN, FU)
                    for is_left, k, width, col in far_units(i)[u][1]:
                        last = nc.tensor.matmul(out[:, col:col + width], qa[0:ROW_M, pa, P * i:P * (i + 1)],
                                                (la if is_left else ra)[0:ROW_M, pa, k:k + width],
                                                start=True, stop=True, skip_group_check=True)
                else:
                    pe.wait_ge(maxed, ha + 1)
                    last = nc.tensor.transpose(out[0:NT, 0:P], mrow[:, pa, :], ident[:])
                    last.then_inc(m_turned, 1)
                    return
                last.then_inc(unit, 1)

            def scores_b(hb, pb, n):
                j, half = divmod(n, 2)
                if n == 0:
                    if isinstance(hb, int) and hb == 0:
                        pe.wait_ge(made, 8)
                    pe.wait_ge(stack_b[pb], loads_of(hb, pb) * 32)
                    pe.wait_ge(m_rows[pb], loads_of(hb, pb) * 24)
                    pe.wait_ge(win_kept, (hb + 1) * N_WIN)
                if n >= 2:
                    pe.wait_ge(exped, hb * N_B + n - 1)
                for b in range(2):
                    bank = scores[:, half, b, :]
                    i = first = 4 * (2 * half + b)
                    while i < first + 4:
                        o = P * (i - first)
                        if abs(i - j) <= 1:
                            off = P - P * (i - j)
                            blk = bank[:, o:o + P]
                            nc.tensor.matmul(blk, win[:, pb, i, off:off + P], ident[:], is_transpose=True,
                                             start=True, stop=False, skip_group_check=True)
                            last = nc.tensor.matmul(blk, onlym[:], qb[0:ROWS, pb, P * i:P * (i + 1)],
                                                    start=False, stop=(i == j), skip_group_check=True)
                            if i != j:
                                lo = 0 if i == j + 1 else SPAN
                                last = nc.tensor.matmul(bank[lo:lo + SPAN, o:o + P],
                                                        (lb if i > j else rb)[0:ROW_M, pb, P * j + lo:P * j + lo + SPAN],
                                                        qb[0:ROW_M, pb, P * i:P * (i + 1)],
                                                        start=False, stop=True, skip_group_check=True)
                            i += 1
                        else:
                            e = i
                            while e < first + 4 and abs(e - j) > 1 and (e > j) == (i > j):
                                e += 1
                            last = nc.tensor.matmul(bank[:, o:o + P * (e - i)],
                                                    (lb if i > j else rb)[:, pb, P * j:P * (j + 1)],
                                                    qb[:, pb, P * i:P * e], start=True, stop=True,
                                                    skip_group_check=True)
                            i = e
                last.then_inc(score, 1)

            def values_b(hb, pb, n):
                j, half = divmod(n, 2)
                if n == 0:
                    pe.wait_ge(v_ok, hb + 1)
                    if not (isinstance(hb, int) and hb == 0):
                        pe.wait_ge(ctx_kept, hb)
                pe.wait_ge(exped, hb * N_B + n + 1)
                for b in range(2):
                    g = 2 * half + b
                    last = nc.tensor.matmul(ctx_ps[32 * g:32 * (g + 1), :], vh[:, pb, j, :],
                                            prob[:, n % 4, b * BANK:(b + 1) * BANK], start=(j == 0), stop=(j == NT - 1),
                                            skip_group_check=True)
                last.then_inc(pv, 1)

            def run(ha, pa, hb, pb):
                for kind, n in merged(ha, hb):
                    if kind == "a":
                        unit_a(ha, pa, n)
                    else:
                        scores_b(hb, pb, n)
                        if n > 1:
                            values_b(hb, pb, n - 2)
                if hb is not None:
                    values_b(hb, pb, N_B - 2)
                    values_b(hb, pb, N_B - 1)

            iterations(pe, run)

        @block.scalar
        def _(act):
            def run(ha, pa, hb, pb):
                for kind, n in merged(ha, hb):
                    if kind == "a":
                        pos, n = n, ORDER[n]
                    if kind == "b":
                        act.wait_ge(score, hb * N_B + n + 1)
                        if not (isinstance(hb, int) and hb == 0 and n < 4):
                            act.wait_ge(pv, hb * N_B + max(n - 3, 0))
                        nc.scalar.activation(prob[:, n % 4, :], scores[:, n % 2, :, :].rearrange("p b q -> p (b q)"),
                                             ACT.Exp, scale=SCALE).then_inc(exped, 1)
                    elif n < N_C2P:
                        act.wait_ge(unit, ha * (N_A - 1) + pos + 1)
                        half, qh, g = n // 4, n // 2 % 2, n % 2
                        nc.scalar.copy(c2p[:, half, g * GI:(g + 1) * GI, P // 2 * qh:P // 2 * (qh + 1)],
                                       bank(ha, pos).rearrange("p (i q) -> p i q", q=P // 2)
                                       ).then_inc(c2p_kept, 1)
                    elif n < N_C2P + N_WIN:
                        act.wait_ge(unit, ha * (N_A - 1) + pos + 1)
                        if n == N_C2P and isinstance(ha, int) and ha == 0:
                            act.wait_ge(made, 4)
                        if n == N_C2P and not (isinstance(ha, int) and ha < 2):
                            act.wait_ge(pv, (ha - 1) * N_B)
                        q, first, end = window_tiles(n - N_C2P)
                        nc.scalar.copy(win[:, pa, first:end, SPAN * (q + 1):SPAN * (q + 2)],
                                       bank(ha, pos)[:, 0:SPAN * (end - first)].rearrange("p (i k) -> p i k", k=SPAN)
                                       ).then_inc(win_kept, 1)

            iterations(act, run)

        @block.vector
        def _(dve):
            nc.vector.memset(mx[:], -3.0e38).then_inc(cleared, 1)
            dve.wait_ge(cleared, 1)

            def run(ha, pa, hb, pb):
                if ha is not None:
                    if not (isinstance(ha, int) and ha == 0):
                        dve.wait_ge(maxed, ha)
                    for pos, n in enumerate(ORDER[:-1]):
                        if n < N_C2P:
                            continue
                        if n >= N_C2P + N_WIN:
                            dve.wait_ge(unit, ha * (N_A - 1) + pos + 1)
                        if n < N_C2P + N_WIN:
                            q, first, end = window_tiles(n - N_C2P)
                            dve.wait_ge(win_kept, ha * N_WIN + n - N_C2P + 1)
                            nc.vector.reduce_max(mx[:, first:end, q], win[:, pa, first:end, SPAN * (q + 1):SPAN * (q + 2)], AX.X).then_inc(win_max, 1)
                        else:
                            i, u = divmod(n - N_C2P - N_WIN, FU)
                            nc.vector.reduce_max(mx[:, i, 4 + u:5 + u], bank(ha, pos)[:, 0:far_units(i)[u][0]], AX.X
                                                 ).then_inc(far_max, 1)
                    dve.wait_ge(far_max, (ha + 1) * N_FAR)
                    nc.vector.reduce_max(mrow[:, pa, :], mx[:], AX.X).then_inc(maxed, 1)
                    dve.wait_ge(m_turned, ha + 1)
                    if not isinstance(ha, int) or ha > 1:
                        dve.wait_ge(m_rows[pa], (loads_of(ha, pa) - 2) * 24)
                    turned, left = ring[0:NT, (N_A - 1) % RING, 0:P], mleft[:, pa, :]
                    nc.vector.tensor_scalar(mpart[:, pa, 0, :], turned, -1.0, None, ALU.mult).then_inc(m_split, 1)
                    dve.wait_ge(m_split, 3 * ha + 1)
                    nc.vector.scalar_tensor_tensor(out=left, in0=turned, scalar=-1.0, in1=mpart[:, pa, 0, :],
                                                   op0=ALU.mult, op1=ALU.subtract).then_inc(m_left, 1)
                    dve.wait_ge(m_left, 2 * ha + 1)
                    nc.vector.tensor_copy(mpart[:, pa, 1, :], left).then_inc(m_split, 1)
                    dve.wait_ge(m_split, 3 * ha + 2)
                    nc.vector.tensor_tensor(left, left, mpart[:, pa, 1, :], ALU.subtract).then_inc(m_left, 1)
                    dve.wait_ge(m_left, 2 * ha + 2)
                    nc.vector.tensor_copy(mpart[:, pa, 2, :], left).then_inc(m_split, 1)
                if hb is not None:
                    dve.wait_ge(pv, (hb + 1) * N_B)
                    if not isinstance(hb, int) or hb > 1:
                        dve.wait_ge(ctx_out[pb], (loads_of(hb, pb) - 2) * 8 * NB + 16)
                    nc.vector.tensor_copy(ctx_sb[:, pb, :], ctx_ps[:]).then_inc(ctx_kept, 1)

            iterations(dve, run)


def shifted(rows):
    (step, _), _ = rows.ap
    return bass.AP(rows.tensor, rows.offset, [[1, CL], [step, DK], [1, TABW]])


def repeated(rows):
    (step, _), _ = rows.ap
    return bass.AP(rows.tensor, rows.offset, [[0, CL], [step, DK], [1, T]])


def strided(cols, step, n):
    part, (one, w) = cols.ap
    return bass.AP(cols.tensor, cols.offset, [list(part), [step, n], [one, w]])


def output_phase(nc, keep, scratch):
    with ExitStack() as ctx:
        def sb(name, shape, dt=F32):
            return ctx.enter_context(nc.sbuf_tensor(name, shape, dt))

        def sem(name):
            return keep["semaphores"].enter_context(nc.semaphore(name))

        PART = T // DK
        ps = ctx.enter_context(nc.psum_tensor("ou_ps", [P, 8, BANK], F32))
        ctxT = sb("ou_ctxT", [P, T])
        den = sb("ou_den", [P, PART])
        spread = sb("ou_spread", [P, DK, H, DK])
        ones_row = sb("ou_ones", [1, P])
        den_in, loaded, made, inverse, bias_ps, biased, spread_ps, normed, out_ps, added = (
            sem(n) for n in ("ou_den_in", "ou_loaded", "ou_made", "inverse", "bias_ps", "ou_biased", "spread_ps", "normed",
                             "out_ps", "added"))
        block = ctx.enter_context(nc.Block())

        @block.sync
        def _(sp):
            den_src, ctx_src = scratch["ctx"][:, DK, :], scratch["ctx"][:, 0:DK, :]
            (head, _), (one, _) = den_src.ap
            sp.dma_start(den[:], bass.AP(den_src.tensor, den_src.offset, [[head, H], [PART * one, DK], [one, PART]])
                         ).then_inc(den_in, 16)
            for b in range(NB):
                cols = slice(b * BANK, (b + 1) * BANK)
                sp.dma_start(ctxT[:, cols], ctx_src[:, :, cols]).then_inc(loaded, 16)

        @block.gpsimd
        def _(pool):
            nc.gpsimd.memset(ones_row[:], 1.0).then_inc(made, 1)
            nc.gpsimd.memset(spread[:], 1.0).then_inc(made, 1)
            pool.wait_ge(made, 2)
            for n, sign in enumerate((1, -1)):
                nc.gpsimd.affine_select(out=spread[:], in_=spread[:], compare_op=ALU.is_ge, fill=0.0, base=0,
                                        pattern=[[-sign, DK], [-sign * DK, H], [0, DK]], channel_multiplier=sign
                                        ).then_inc(made, 1)
                pool.wait_ge(made, 3 + n)

        @block.tensor
        def _(pe):
            pe.wait_ge(made, 1)
            nc.tensor.matmul(ps[:, 4, 0:D], ones_row[:], keep["bo_row"][:], start=True, stop=True).then_inc(bias_ps, 1)
            pe.wait_ge(made, 4)
            pe.wait_ge(inverse, 1)
            for c in range(DK):
                b, half = divmod(c, 2)
                last = nc.tensor.matmul(ps[:, b, half * PART:(half + 1) * PART],
                                        spread[:, c].rearrange("p h d -> p (h d)"), den[:], start=True, stop=True)
                if half:
                    last.then_inc(spread_ps, 1)
            pe.wait_ge(biased, 1)
            for b in range(NB):
                pe.wait_ge(normed, b + 1)
                for s in range(4):
                    t = 4 * b + s
                    o = ps[:, 4 + b, s * P:(s + 1) * P]
                    last = nc.tensor.matmul(o, ctxT[:, t * P:(t + 1) * P], keep["woT"][:], start=True, stop=True)
                last.then_inc(out_ps, 1)

        @block.vector
        def _(dve):
            dve.wait_ge(den_in, 16)
            nc.vector.reciprocal(den[:], den[:]).then_inc(inverse, 1)
            dve.wait_ge(bias_ps, 1)
            nc.vector.tensor_tensor(keep["x_nat"][:], keep["x_nat"][:], ps[:, 4:5, 0:D].to_broadcast([P, NT, D]), ALU.add
                                    ).then_inc(biased, 1)
            dve.wait_ge(loaded, 16 * NB)
            for b in range(NB):
                dve.wait_ge(spread_ps, b + 1)
                c = ctxT[:, b * BANK:(b + 1) * BANK]
                nc.vector.tensor_tensor(c, c, ps[:, b, :], ALU.mult).then_inc(normed, 1)
            dve.wait_ge(biased, 1)
            for b in range(NB):
                dve.wait_ge(out_ps, b + 1)
                c = keep["x_nat"][:, 4 * b:4 * b + 4, :].rearrange("p s d -> p (s d)")
                nc.vector.tensor_tensor(c, c, ps[:, 4 + b, :], ALU.add).then_inc(added, 1)
            dve.wait_ge(added, NB)


DEPTH = 8
NODES = 2 ** DEPTH - 1
LEAVES = 2 ** DEPTH
LW = 16
W1, W2, B1, B2 = 0, LW * D, 2 * LW * D, 2 * LW * D + LW
LEAF_ROW = B2 + D
SCALE_F = float(D ** -0.5)


def norm_phase(nc, a, keep):
    x_nat, ident, modc = keep["x_nat"], keep["ident"], keep["modc"]
    xf, xfT = keep["xf"], keep["xfT"]
    with ExitStack() as ctx:
        def sb(name, shape, dt=F32):
            return ctx.enter_context(nc.sbuf_tensor(name, shape, dt))

        def sem(name):
            return keep["semaphores"].enter_context(nc.semaphore(name))

        ps = ctx.enter_context(nc.psum_tensor("no_ps", [P, 8, BANK], F32))
        stats = sb("no_stats", [P, NT, 6])
        mv = sb("no_mv", [P, 2, NT, 2])
        rstd = sb("no_rstd", [P, 2, NT])
        expo = sb("no_expo", [P, 2, NT])
        mod_rows = sb("no_mod", [P, 2, D])
        h2 = sb("no_h2", [P, NT, D])
        rows_ps, vec, var_ok, rstd_ok, pooled, turned = (
            sem(n) for n in ("rows_ps", "no_vec", "no_var_ok", "no_rstd_ok", "pooled", "turned"))
        xf_ok, xfT_ok, nodes_in = sem("xf_ok"), sem("xfT_ok"), sem("nodes_in")
        block = ctx.enter_context(nc.Block())

        @block.sync
        def _(sp):
            nodes, n_loads = keep["nodes"], 0
            for n, tree in enumerate("qkvf"):
                sp.dma_start(nodes["nw"][:, n, :], a[f"{tree}_nwT"]).then_inc(nodes_in, 16)
                for c, size in enumerate(NODE_CHUNK):
                    sp.dma_start(nodes["nb"][0:size, n, c:c + 1], a[f"{tree}_nb"][c * P:c * P + size, :]
                                 ).then_inc(nodes_in, 16)
            for c, size in enumerate(NODE_CHUNK):
                sp.dma_start(nodes["paths"][0:size, c, :], a["paths"][c * P:c * P + size, :]).then_inc(nodes_in, 16)
            sp.dma_start(nodes["turns"][:], a["turns"]).then_inc(nodes_in, 16)
            sp.dma_start(nodes["number"][:], a["number"]).then_inc(nodes_in, 16)
            sp.wait_ge(nodes_in, 16 * (3 * 4 + 4))

        @block.gpsimd
        def _(pool):
            n_pooled = 0

            def step(ins):
                nonlocal n_pooled
                n_pooled += 1
                ins.then_inc(pooled, 1)
                pool.wait_ge(pooled, n_pooled)

            step(nc.gpsimd.memset(expo[:, 0, :], -0.5))
            step(nc.gpsimd.memset(expo[:, 1, :], 0.5))
            pool.wait_ge(var_ok, 1)
            step(nc.gpsimd.tensor_scalar(rstd[:, 0, :], mv[:, 0, :, 1], EPS, None, ALU.add))
            nc.gpsimd.tensor_tensor(rstd[:, 0, :], rstd[:, 0, :], expo[:, 0, :], ALU.pow).then_inc(rstd_ok, 1)
            pool.wait_ge(var_ok, 2)
            step(nc.gpsimd.tensor_scalar(rstd[:, 1, :], mv[:, 1, :, 1], D / (D - 1.0), None, ALU.mult))
            step(nc.gpsimd.tensor_tensor(rstd[:, 1, :], rstd[:, 1, :], expo[:, 1, :], ALU.pow))
            step(nc.gpsimd.tensor_scalar(rstd[:, 1, :], rstd[:, 1, :], EPS, None, ALU.add))
            nc.gpsimd.tensor_tensor(rstd[:, 1, :], rstd[:, 1, :], expo[:, 0, :], ALU.pow).then_inc(rstd_ok, 1)

        @block.tensor
        def _(pe):
            for n, col in enumerate((4, 3)):
                last = nc.tensor.matmul(ps[:, 0, n * D:(n + 1) * D], modc[:, col:col + 1].to_broadcast([P, P]),
                                        ident[:], start=True, stop=True)
            last.then_inc(rows_ps, 1)
            for t in range(NT):
                pe.wait_ge(xf_ok, t + 1)
                last = nc.tensor.transpose(ps[:, 4 + t // 4, t % 4 * P:(t % 4 + 1) * P], xf[:, t, :], ident[:])
                if t % 4 == 3:
                    last.then_inc(turned, 1)

        @block.vector
        def _(dve):
            n_vec = 0

            def step(ins):
                nonlocal n_vec
                n_vec += 1
                ins.then_inc(vec, 1)
                dve.wait_ge(vec, n_vec)

            def statistics(x, r):
                for t in range(NT):
                    ins = nc.vector.bn_stats(stats[:, t, :], x[:, t, :])
                step(ins)
                for t in range(NT):
                    ins = nc.vector.bn_aggr(mv[:, r, t, :], stats[:, t, :])
                ins.then_inc(var_ok, 1)
                dve.wait_ge(var_ok, r + 1)

            dve.wait_ge(rows_ps, 1)
            step(nc.vector.tensor_copy(mod_rows[:].rearrange("p a d -> p (a d)"), ps[:, 0, 0:2 * D]))
            statistics(x_nat, 0)
            for t in range(NT):
                ins = nc.vector.scalar_tensor_tensor(out=h2[:, t, :], in0=x_nat[:, t, :], scalar=mv[:, 0, t, 0:1],
                                                     in1=mod_rows[:, 0, :], op0=ALU.subtract, op1=ALU.mult)
            step(ins)
            dve.wait_ge(rstd_ok, 1)
            for t in range(NT):
                ins = nc.vector.scalar_tensor_tensor(out=h2[:, t, :], in0=h2[:, t, :], scalar=rstd[:, 0, t:t + 1],
                                                     in1=mod_rows[:, 1, :], op0=ALU.mult, op1=ALU.add)
            step(ins)
            statistics(h2, 1)
            dve.wait_ge(rstd_ok, 2)
            for t in range(NT):
                nc.vector.tensor_scalar(xf[:, t, :], h2[:, t, :], mv[:, 1, t, 0:1], rstd[:, 1, t:t + 1],
                                        ALU.subtract, ALU.mult).then_inc(xf_ok, 1)
            for b in range(NB):
                dve.wait_ge(turned, b + 1)
                nc.vector.tensor_copy(xfT[:, b * BANK:(b + 1) * BANK], ps[:, 4 + b, :]).then_inc(xfT_ok, 1)
            dve.wait_ge(xfT_ok, NB)


SLOTS = 4
LEAD = 2
NODE_CHUNK = (P, NODES - P)


def leaves_phase(nc, a, trees, keep):
    tag, N = trees[0], len(trees)
    ident, x, srcT, nodes, leaf = keep["ident"], keep["xf"], keep["xfT"], keep["nodes"], keep["leaf"]
    tree_no = ["qkvf".index(tree) for tree in trees]
    assert NT == SLOTS * NB and BANK == SLOTS * P
    with ExitStack() as ctx:
        def sb(name, shape, dt=F32):
            return ctx.enter_context(nc.sbuf_tensor(f"le_{tag}_{name}", shape, dt))

        def sem(name):
            return keep["semaphores"].enter_context(nc.semaphore(f"le_{tag}_{name}"))

        def sems(name):
            return [sem(f"{name}{s}") for s in range(SLOTS)]

        ps = ctx.enter_context(nc.psum_tensor(f"le_{tag}_ps", [P, 8, BANK], F32))
        ROUTE, NAMED = SLOTS, SLOTS + 2
        rows = sb("rows", [P, SLOTS, LEAF_ROW])
        index = sb("index", [P, SLOTS], I32)
        prod1 = sb("prod1", [P, LW, D])
        prod2 = sb("prod2", [P, SLOTS, LW, D])
        hid = sb("hid", [P, SLOTS, 3, LW])
        went = sb("went", [P, 2, BANK], BF16)
        hit = sb("hit", [P, 2, BANK], BF16)
        gathered, summed, kept = sems("gathered"), sems("summed"), sems("kept")
        indexed, asked, multiplied, reduced, biased, active, scaled, b2_read = (
            sem(n) for n in ("indexed", "asked", "multiplied", "reduced", "biased", "active", "scaled", "b2_read"))
        logits, decided, counted, found, named, routed = (
            sem(n) for n in ("logits", "decided", "counted", "found", "named", "routed"))
        block = ctx.enter_context(nc.Block())

        def lots(eng, run, first=None):
            if first is not None:
                for b in range(LEAD):
                    first(b)
            for n in range(N):
                for half in range(NB // LEAD):
                    with eng.Fori(0, LEAD) as k:
                        at, ahead = (half + 1) % (NB // LEAD) * LEAD, n + (half + 1) // (NB // LEAD)
                        run(n, half * LEAD + k, NB * n + half * LEAD + k, ahead if ahead < N else None, at + k)

        def tile_of(k, s):
            return SLOTS * k + s

        @block.gpsimd
        def _(pool):
            def run(n, k, uses, _nxt, _b):
                pool.wait_ge(routed, uses + 1)
                for s in range(SLOTS):
                    pool.wait_ge(scaled, SLOTS * uses + s + 1)
                    pool.wait_ge(b2_read, SLOTS * uses + s + 1)
                    nc.gpsimd.tensor_copy(index[:, s:s + 1], leaf[:, tree_no[n], bass.ds(tile_of(k, s), 1)]
                                          ).then_inc(indexed, 1)
                    pool.wait_ge(indexed, SLOTS * uses + s + 1)
                    pool.sem_inc(asked, 1)
                    nc.gpsimd.indirect_dma_start(rows[:, s, :], None, a[f"{trees[n]}_leaves"],
                                                 bass.IndirectOffsetOnAxis(ap=index[:, s:s + 1], axis=0)
                                                 ).then_inc(gathered[s], 16)

            lots(pool, run)

        @block.vector
        def _(dve):
            def decide(n, lot):
                dve.wait_ge(logits, lot + 1)
                for c, size in enumerate(NODE_CHUNK):
                    nc.vector.tensor_scalar(went[0:size, c, :], ps[0:size, ROUTE + c, :],
                                            nodes["nb"][0:size, tree_no[n], c:c + 1], 0.0, ALU.add, ALU.is_gt
                                            ).then_inc(decided, 1)

            def find(lot):
                dve.wait_ge(counted, lot + 1)
                for c in range(2):
                    nc.vector.tensor_scalar(hit[:, c, :], ps[:, ROUTE + c, :], nodes["turns"][:, c:c + 1], None,
                                            ALU.is_equal).then_inc(found, 1)

            def keep_leaves(n, b, lot):
                dve.wait_ge(named, lot + 1)
                nc.vector.tensor_copy(leaf[:, tree_no[n], bass.ds(SLOTS * b, SLOTS)], ps[:, NAMED, 0:SLOTS]
                                      ).then_inc(routed, 1)

            def first(b):
                decide(0, b)
                find(b)
                keep_leaves(0, b, b)

            def hidden(n, k, uses, s):
                row, item = rows[:, s, :], SLOTS * uses + s
                dve.wait_ge(gathered[s], 16 * uses + 16)
                nc.vector.tensor_tensor(prod1[:], row[:, W1:W2].rearrange("p (l d) -> p l d", d=D),
                                        x[:, bass.ds(tile_of(k, s), 1), :].to_broadcast([P, LW, D]), ALU.mult
                                        ).then_inc(multiplied, 1)
                dve.wait_ge(multiplied, item + 1)
                nc.vector.tensor_reduce(hid[:, s, 0, :], prod1[:], AX.X, ALU.add).then_inc(reduced, 1)
                dve.wait_ge(reduced, item + 1)
                nc.vector.tensor_tensor(hid[:, s, 1, :], hid[:, s, 0, :], row[:, B1:B2], ALU.add).then_inc(biased, 1)
                dve.wait_ge(biased, item + 1)
                nc.vector.tensor_scalar(hid[:, s, 2, :], hid[:, s, 1, :], 0.0, None, ALU.max).then_inc(active, 1)

            def run(n, k, uses, nxt, b):
                lot = uses + LEAD
                hidden(n, k, uses, 0)
                hidden(n, k, uses, 1)
                if nxt is not None:
                    decide(nxt, lot)
                hidden(n, k, uses, 2)
                if nxt is not None:
                    find(lot)
                hidden(n, k, uses, 3)
                if nxt is not None:
                    keep_leaves(nxt, b, lot)

            lots(dve, run, first)

        @block.scalar
        def _(act):
            act.sem_inc(scaled, SLOTS)
            for s in range(SLOTS):
                act.sem_inc(kept[s], 1)

            def scale(uses, s):
                act.wait_ge(active, SLOTS * uses + s + 1)
                for l in range(LW):
                    ins = nc.scalar.mul(prod2[:, s, l, :], rows[:, s, W2 + l * D:W2 + (l + 1) * D],
                                        hid[:, s, 2, l:l + 1])
                ins.then_inc(scaled, 1)

            def keep_sum(n, k, uses, s):
                act.wait_ge(summed[s], uses + 1)
                nc.scalar.copy(keep["qkvT"][:, n, bass.ds(tile_of(k, s) * P, P)], ps[:, s, 0:D]).then_inc(kept[s], 1)

            def run(n, k, uses, _nxt, _b):
                for s in range(SLOTS):
                    scale(uses, s)
                    if s >= 1:
                        keep_sum(n, k, uses, s - 1)
                keep_sum(n, k, uses, SLOTS - 1)

            lots(act, run)

        @block.tensor
        def _(pe):
            pe.sem_inc(b2_read, SLOTS)

            def decide(n, b, lot):
                if not (isinstance(lot, int) and lot == 0):
                    pe.wait_ge(found, 2 * lot)
                for c, size in enumerate(NODE_CHUNK):
                    last = nc.tensor.matmul(ps[0:size, ROUTE + c, :], nodes["nw"][:, tree_no[n], c * P:c * P + size],
                                            srcT[:, bass.ds(b * BANK, BANK)], start=True, stop=True)
                last.then_inc(logits, 1)

            def count(lot):
                pe.wait_ge(decided, 2 * (lot + 1))
                for c in range(2):
                    for m, size in enumerate(NODE_CHUNK):
                        last = nc.tensor.matmul(ps[:, ROUTE + c, :], nodes["paths"][0:size, m, c * P:(c + 1) * P],
                                                went[0:size, m, :], start=(m == 0), stop=(m == 1))
                last.then_inc(counted, 1)

            def name(lot):
                pe.wait_ge(found, 2 * (lot + 1))
                if not (isinstance(lot, int) and lot == 0):
                    pe.wait_ge(routed, lot)
                for s in range(SLOTS):
                    for c in range(2):
                        last = nc.tensor.matmul(ps[:, NAMED, s:s + 1], hit[:, c, s * P:(s + 1) * P],
                                                nodes["number"][:, c:c + 1], start=(c == 0), stop=(c == 1),
                                                skip_group_check=True)
                last.then_inc(named, 1)

            def first(b):
                decide(0, b, b)
                count(b)
                name(b)

            def total(k, uses, s):
                item = SLOTS * uses + s
                pe.wait_ge(gathered[s], 16 * uses + 16)
                pe.wait_ge(kept[s], uses + 1)
                o = ps[:, s, 0:D]
                nc.tensor.matmul(o, rows[:, s, B2:B2 + D], ident[:], is_transpose=True, start=True, stop=False
                                 ).then_inc(b2_read, 1)
                pe.wait_ge(scaled, SLOTS + item + 1)
                for l in range(LW):
                    end = nc.tensor.matmul(o, prod2[:, s, l, :], ident[:], is_transpose=True, start=False,
                                           stop=(l == LW - 1))
                end.then_inc(summed[s], 1)

            def run(n, k, uses, nxt, b):
                lot = uses + LEAD
                if nxt is not None:
                    decide(nxt, b, lot)
                for s in range(SLOTS):
                    total(k, uses, s)
                    if nxt is not None and s == 0:
                        count(lot)
                    if nxt is not None and s == 1:
                        name(lot)

            lots(pe, run, first)


NS = 3


def mix_phase(nc, a, keep, out):
    ident, qkvT, xf, xfT, nodes = keep["ident"], keep["qkvT"], keep["xf"], keep["xfT"], keep["nodes"]
    MIX, ROUTE, HIDDEN, SCALE, END = 1, 2, 4, 5, 6
    F = 3
    with ExitStack() as ctx:
        def sb(name, shape, dt=F32):
            return ctx.enter_context(nc.sbuf_tensor(f"mi_{name}", shape, dt))

        def sem(name):
            return keep["semaphores"].enter_context(nc.semaphore(f"mi_{name}"))

        scores = ctx.enter_context(nc.psum_tensor("mi_scores", [P, NB, BANK], F32))
        turn = ctx.enter_context(nc.psum_tensor("mi_turn", [P, 2, BANK], F32))
        mixed = ctx.enter_context(nc.psum_tensor("mi_mixed", [P, BANK], F32))
        leaf_sum, leaf_back, y_ps = (mixed[:, n * D:(n + 1) * D] for n in range(3))
        routing = ctx.enter_context(nc.psum_tensor("mi_routing", [P, BANK], F32))
        yT_ps, count_ps, node_ps, named_ps = (routing[:, 0:P], routing[:, 0:2 * P], routing[:, P:3 * P],
                                              routing[:, 3 * P:3 * P + 1])
        v = sb("v", [P, NT, D])
        q = sb("q", [P, NS, P])
        prob = sb("prob", [P, NS, T])
        probT = sb("probT", [P, NT, P])
        top = sb("top", [P, NS, 4])
        y = sb("y", [P, NS, D])
        den = sb("den", [P, NS, 2])
        went = sb("went", [P, 2, P], BF16)
        hit = sb("hit", [P, 2, P], BF16)
        index = sb("index", [P, NS], I32)
        rows = sb("rows", [P, NS, LEAF_ROW])
        b2 = sb("b2", [P, NS, D])
        prod1 = sb("prod1", [P, LW, D])
        prod2 = sb("prod2", [P, NS, LW, D])
        hid = sb("hid", [P, NS, 3, LW])
        mixT = sb("mixT", [P, NS, D])
        outs = sb("outs", [P, NS, D])

        v_ps, v_ok = sem("v_ps"), sem("v_ok")
        q_ok, scored, half_max, max_ok, neg_ok, exped = (
            sem(n) for n in ("q_ok", "scored", "half_max", "max_ok", "neg_ok", "exped"))
        turned, kept_act, kept_dve, mixed_ok, inv_ok, y_ok = (
            sem(n) for n in ("turned", "kept_act", "kept_dve", "mixed_ok", "inv_ok", "y_ok"))
        yT_turned, yT_kept, logits, decided, counted, found, named, routed, asked = (
            sem(n) for n in ("yT_turned", "yT_kept", "logits", "decided", "counted", "found", "named", "routed",
                             "asked"))
        multiplied, reduced, biased, active, scaled, b2_kept = (
            sem(n) for n in ("multiplied", "reduced", "biased", "active", "scaled", "b2_kept"))
        summed, sum_kept, back, finished = (sem(n) for n in ("summed", "sum_kept", "back", "finished"))
        gathered, stored = ([sem(f"{n}{s}") for s in range(NS)] for n in ("gathered", "stored"))
        block = ctx.enter_context(nc.Block())

        def steps(eng, run):
            for c in range(END):
                run(0, c)
            whole = (NT - END) // NS
            with eng.Fori(0, whole) as g:
                for c in range(END, END + NS):
                    run(g, c)
            for c in range(END + NS * whole, NT + END):
                run(0, c)

        def tile(g, c, stage):
            t = c - stage
            if isinstance(g, int) and not 0 <= t < NT:
                return None, None
            return NS * g + t, t % NS

        def uses(g, c, stage):
            return g + (c - stage) // NS

        @block.gpsimd
        def _(pool):
            nc.gpsimd.tensor_copy(q[:, 0, :], qkvT[:, 0, 0:P]).then_inc(q_ok, 1)

            def run(g, c):
                i, p = tile(g, c, -1)
                if i is not None:
                    if c + 1 >= NS:
                        pool.wait_ge(scored, NB * (i - NS + 1))
                    pool.sem_inc(asked, 1)
                    nc.gpsimd.tensor_copy(q[:, p, :], qkvT[:, 0, bass.ds(i * P, P)]).then_inc(q_ok, 1)
                i, p = tile(g, c, ROUTE)
                if i is not None:
                    pool.wait_ge(routed, i + 1)
                    if c - ROUTE >= NS:
                        pool.wait_ge(scaled, i - NS + 1)
                        pool.wait_ge(b2_kept, i - NS + 1)
                    pool.sem_inc(asked, 1)
                    nc.gpsimd.indirect_dma_start(rows[:, p, :], None, a["f_leaves"],
                                                 bass.IndirectOffsetOnAxis(ap=index[:, p:p + 1], axis=0)
                                                 ).then_inc(gathered[p], 16)
                i, p = tile(g, c, HIDDEN)
                if i is not None:
                    pool.wait_ge(gathered[p], 16 * uses(g, c, HIDDEN) + 16)
                    if isinstance(g, int) and i >= NS:
                        pool.wait_ge(summed, i - NS + 1)
                    pool.sem_inc(asked, 1)
                    nc.gpsimd.tensor_copy(b2[:, p, :], rows[:, p, B2:B2 + D]).then_inc(b2_kept, 1)

            steps(pool, run)

        @block.tensor
        def _(pe):
            for g in range(4):
                if g >= 2:
                    pe.wait_ge(v_ok, g - 1)
                for s in range(4):
                    t = 4 * g + s
                    last = nc.tensor.transpose(turn[:, g % 2, s * P:(s + 1) * P], qkvT[:, 2, t * P:(t + 1) * P], ident[:])
                last.then_inc(v_ps, 1)
            pe.wait_ge(v_ok, 4)

            def score(i, p, half):
                for b in (2 * half, 2 * half + 1):
                    nc.tensor.matmul(scores[:, b, :], q[:, p, :], qkvT[:, 1, b * BANK:(b + 1) * BANK],
                                     start=True, stop=True).then_inc(scored, 1)

            def turn_group(j, p, g):
                if g >= 2:
                    pe.wait_ge(kept_act, 2 * j + g - 1)
                elif not (isinstance(j, int) and j == 0):
                    pe.wait_ge(kept_dve, 2 * j)
                for s in range(4):
                    t = 4 * g + s
                    last = nc.tensor.transpose(turn[:, g % 2, s * P:(s + 1) * P], prob[:, p, t * P:(t + 1) * P], ident[:])
                last.then_inc(turned, 1)

            def mix_group(j, g):
                pe.wait_ge(kept_act if g < 2 else kept_dve, 2 * j + g % 2 + 1)
                for s in range(4):
                    t = 4 * g + s
                    last = nc.tensor.matmul(y_ps, probT[:, t, :], v[:, t, :], start=(t == 0), stop=(t == NT - 1),
                                            skip_group_check=True)
                if g == 3:
                    last.then_inc(mixed_ok, 1)

            def run(g, c):
                i, p = tile(g, c, 0)
                j, pj = tile(g, c, MIX)
                r, pr = tile(g, c, ROUTE)
                e, pe_ = tile(g, c, END)
                if i is not None:
                    pe.wait_ge(q_ok, i + 1)
                    if c >= 1:
                        pe.wait_ge(exped, i)
                    score(i, p, 0)
                if e is not None:
                    if r is not None:
                        pe.wait_ge(y_ok, r + 1)
                    elif e >= 1:
                        pe.wait_ge(finished, e)
                    pe.wait_ge(scaled, e + 1)
                    pe.wait_ge(b2_kept, e + 1)
                    for l in range(LW):
                        nc.tensor.matmul(leaf_sum, prod2[:, pe_, l, :], ident[:], is_transpose=True,
                                         start=(l == 0), stop=False, skip_group_check=True)
                    nc.tensor.matmul(leaf_sum, b2[:, pe_, :], ident[:], is_transpose=True, start=False, stop=False,
                                     skip_group_check=True)
                    nc.tensor.matmul(leaf_sum, ident[:], xfT[:, bass.ds(e * P, P)], start=False, stop=True,
                                     skip_group_check=True).then_inc(summed, 1)
                if r is not None:
                    pe.wait_ge(y_ok, r + 1)
                    if c - ROUTE >= 1:
                        pe.wait_ge(routed, r)
                    nc.tensor.transpose(yT_ps, y[:, pr, :], ident[:]).then_inc(yT_turned, 1)
                if i is not None:
                    score(i, p, 1)
                if r is not None:
                    pe.wait_ge(yT_kept, r + 1)
                    for m, size in enumerate(NODE_CHUNK):
                        last = nc.tensor.matmul(node_ps[0:size, m * P:(m + 1) * P], nodes["nw"][:, F, m * P:m * P + size],
                                                xfT[:, bass.ds(r * P, P)], start=True, stop=True, skip_group_check=True)
                    last.then_inc(logits, 1)
                if j is not None:
                    pe.wait_ge(exped, j + 1)
                    turn_group(j, pj, 0)
                    turn_group(j, pj, 1)
                if e is not None:
                    pe.wait_ge(sum_kept, e + 1)
                    nc.tensor.matmul(leaf_back, mixT[:, pe_, :], ident[:], is_transpose=True, start=True, stop=False,
                                     skip_group_check=True)
                    nc.tensor.matmul(leaf_back, ident[:],
                                     keep["x_nat"][:, bass.ds(e, 1), :].rearrange("p a d -> p (a d)"),
                                     start=False, stop=True, skip_group_check=True).then_inc(back, 1)
                if r is not None:
                    pe.wait_ge(decided, 2 * r + 2)
                    for n in range(2):
                        for m, size in enumerate(NODE_CHUNK):
                            last = nc.tensor.matmul(count_ps[:, n * P:(n + 1) * P],
                                                    nodes["paths"][0:size, m, n * P:(n + 1) * P], went[0:size, m, :],
                                                    start=(m == 0), stop=(m == 1), skip_group_check=True)
                    last.then_inc(counted, 1)
                if j is not None:
                    turn_group(j, pj, 2)
                    if e is not None:
                        pe.wait_ge(finished, e + 1)
                    elif c - MIX >= 1:
                        pe.wait_ge(y_ok, j)
                    mix_group(j, 0)
                    turn_group(j, pj, 3)
                    mix_group(j, 1)
                if r is not None:
                    pe.wait_ge(found, 2 * r + 2)
                    for m in range(2):
                        last = nc.tensor.matmul(named_ps, hit[:, m, :], nodes["number"][:, m:m + 1],
                                                start=(m == 0), stop=(m == 1), skip_group_check=True)
                    last.then_inc(named, 1)
                if j is not None:
                    mix_group(j, 2)
                    mix_group(j, 3)

            steps(pe, run)

        @block.scalar
        def _(act):
            for s in range(NS):
                act.sem_inc(stored[s], 16)

            def scale(k, p, ls):
                for l in ls:
                    ins = nc.scalar.mul(prod2[:, p, l, :], rows[:, p, W2 + l * D:W2 + (l + 1) * D],
                                        hid[:, p, 2, l:l + 1])
                if ls[-1] == LW - 1:
                    ins.then_inc(scaled, 1)

            def run(g, c):
                i, p = tile(g, c, 0)
                j, _pj = tile(g, c, MIX)
                r, _pr = tile(g, c, ROUTE)
                k, pk = tile(g, c, SCALE)
                e, pe_ = tile(g, c, END)
                if k is not None:
                    act.wait_ge(biased, k + 1)
                    nc.scalar.activation(hid[:, pk, 2, :], hid[:, pk, 1, :], ACT.Gelu).then_inc(active, 1)
                    act.wait_ge(active, k + 1)
                    scale(k, pk, range(LW * 3 // 4))
                if r is not None:
                    act.wait_ge(yT_turned, r + 1)
                    nc.scalar.copy(xfT[:, bass.ds(r * P, P)], yT_ps).then_inc(yT_kept, 1)
                if e is not None:
                    act.wait_ge(summed, e + 1)
                    nc.scalar.mul(mixT[:, pe_, :], leaf_sum, keep["modc"][:, 5:6]).then_inc(sum_kept, 1)
                if k is not None:
                    scale(k, pk, range(LW * 3 // 4, LW))
                if j is not None:
                    for n in range(2):
                        act.wait_ge(turned, 4 * j + n + 1)
                        nc.scalar.copy(probT[:, 4 * n:4 * n + 4, :].rearrange("p s q -> p (s q)"), turn[:, n, :]
                                       ).then_inc(kept_act, 1)
                if e is not None:
                    act.wait_ge(back, e + 1)
                    act.wait_ge(stored[pe_], 16 * uses(g, c, END) + 16)
                    nc.scalar.copy(outs[:, pe_, :], leaf_back).then_inc(finished, 1)
                if i is not None:
                    act.wait_ge(neg_ok, i + 1)
                    if c >= NS:
                        act.wait_ge(turned, 4 * (i - NS + 1))
                        act.wait_ge(y_ok, i - NS + 1)
                    nc.scalar.activation(prob[:, p, :], scores[:].rearrange("p b k -> p (b k)"), ACT.Exp,
                                         bias=top[:, p, 3:4], scale=SCALE_F, accum_out=den[:, p, 0:1]).then_inc(exped, 1)

            steps(act, run)

        @block.vector
        def _(dve):
            for g in range(4):
                dve.wait_ge(v_ps, g + 1)
                nc.vector.tensor_copy(v[:, 4 * g:4 * g + 4, :].rearrange("p s d -> p (s d)"), turn[:, g % 2, :]
                                      ).then_inc(v_ok, 1)

            def top_of(i, p, half):
                dve.wait_ge(scored, NB * i + 2 * half + 2)
                nc.vector.tensor_reduce(top[:, p, half:half + 1], scores[:, 2 * half:2 * half + 2, :], AX.XY,
                                        ALU.max).then_inc(half_max, 1)

            def run(g, c):
                i, p = tile(g, c, 0)
                j, pj = tile(g, c, MIX)
                r, pr = tile(g, c, ROUTE)
                h, ph = tile(g, c, HIDDEN)
                if h is not None:
                    dve.wait_ge(gathered[ph], 16 * uses(g, c, HIDDEN) + 16)
                    nc.vector.tensor_tensor(prod1[:], rows[:, ph, W1:W2].rearrange("p (l d) -> p l d", d=D),
                                            y[:, ph:ph + 1, :].to_broadcast([P, LW, D]), ALU.mult
                                            ).then_inc(multiplied, 1)
                if i is not None:
                    if c >= NS:
                        dve.wait_ge(exped, i - NS + 1)
                    top_of(i, p, 0)
                if h is not None:
                    dve.wait_ge(multiplied, h + 1)
                    nc.vector.tensor_reduce(hid[:, ph, 0, :], prod1[:], AX.X, ALU.add).then_inc(reduced, 1)
                if r is not None:
                    dve.wait_ge(logits, r + 1)
                    for m, size in enumerate(NODE_CHUNK):
                        nc.vector.tensor_scalar(went[0:size, m, :], node_ps[0:size, m * P:(m + 1) * P],
                                                nodes["nb"][0:size, F, m:m + 1], 0.0, ALU.add, ALU.is_gt
                                                ).then_inc(decided, 1)
                if i is not None:
                    top_of(i, p, 1)
                if h is not None:
                    dve.wait_ge(reduced, h + 1)
                    nc.vector.tensor_tensor(hid[:, ph, 1, :], hid[:, ph, 0, :], rows[:, ph, B1:B2], ALU.add
                                            ).then_inc(biased, 1)
                if i is not None:
                    dve.wait_ge(half_max, 2 * i + 2)
                    nc.vector.tensor_tensor(top[:, p, 2:3], top[:, p, 0:1], top[:, p, 1:2], ALU.max).then_inc(max_ok, 1)
                    dve.wait_ge(max_ok, i + 1)
                    nc.vector.tensor_scalar(top[:, p, 3:4], top[:, p, 2:3], -SCALE_F, None, ALU.mult).then_inc(neg_ok, 1)
                if r is not None:
                    dve.wait_ge(counted, r + 1)
                    for m in range(2):
                        nc.vector.tensor_scalar(hit[:, m, :], count_ps[:, m * P:(m + 1) * P], nodes["turns"][:, m:m + 1],
                                                None, ALU.is_equal).then_inc(found, 1)
                if j is not None:
                    for n in range(2, 4):
                        dve.wait_ge(turned, 4 * j + n + 1)
                        nc.vector.tensor_copy(probT[:, 4 * n:4 * n + 4, :].rearrange("p s q -> p (s q)"),
                                              turn[:, n - 2, :]).then_inc(kept_dve, 1)
                if r is not None:
                    dve.wait_ge(named, r + 1)
                    if c - ROUTE >= NS:
                        dve.wait_ge(gathered[pr], 16 * uses(g, c, ROUTE))
                    nc.vector.tensor_copy(index[:, pr:pr + 1], named_ps).then_inc(routed, 1)
                if j is not None:
                    nc.vector.reciprocal(den[:, pj, 1:2], den[:, pj, 0:1]).then_inc(inv_ok, 1)
                    dve.wait_ge(inv_ok, j + 1)
                    dve.wait_ge(mixed_ok, j + 1)
                    nc.vector.scalar_tensor_tensor(out=y[:, pj, :], in0=y_ps, scalar=den[:, pj, 1:2],
                                                   in1=xf[:, bass.ds(j, 1), :].rearrange("p a d -> p (a d)"),
                                                   op0=ALU.mult, op1=ALU.add).then_inc(y_ok, 1)

            steps(dve, run)

        @block.sync
        def _(sp):
            def run(g, c):
                e, pe_ = tile(g, c, END)
                if e is not None:
                    sp.wait_ge(finished, e + 1)
                    sp.dma_start(out[0, bass.ds(e * P, P), :], outs[:, pe_, :]).then_inc(stored[pe_], 16)

            steps(sp, run)
            for s in range(NS):
                sp.wait_ge(stored[s], 16 + 16 * len(range(s, NT, NS)))


def feed_forward_phase(nc, a, keep, out):
    with ExitStack() as ctx:
        def sb(name, shape, dt=F32):
            return ctx.enter_context(nc.sbuf_tensor(name, shape, dt))

        keep["xf"] = sb("xf", [P, NT, D])
        keep["xfT"] = sb("xfT", [P, T])
        keep["qkvT"] = sb("qkvT", [P, 3, T])
        keep["leaf"] = sb("leaf", [P, 4, NT], I32)
        keep["nodes"] = {
            "nw": sb("nodes_nw", [P, 4, NODES]),
            "nb": sb("nodes_nb", [P, 4, 2]),
            "paths": sb("nodes_paths", [P, 2, LEAVES], BF16),
            "turns": sb("nodes_turns", [P, 2]),
            "number": sb("nodes_number", [P, 2], BF16),
        }
        norm_phase(nc, a, keep)
        leaves_phase(nc, a, ("q", "k", "v"), keep)
        mix_phase(nc, a, keep, out)


def adaln_block(nc, a, out):
    with ExitStack() as ctx:
        def sb(name, shape, dt=F32):
            return ctx.enter_context(nc.sbuf_tensor(name, shape, dt))

        keep = {
            "semaphores": ctx,
            "x_nat": sb("x_nat", [P, NT, D]),
            "ident": sb("ident", [P, P]),
            "modc": sb("modc", [P, 8]),
            "woT": sb("woT", [P, D]),
            "bo_row": sb("bo_row", [1, D]),
        }
        scratch = {
            "ext": nc.dram_tensor("ext_scratch", [2, P, EXT], F32, kind="Internal").ap(),
            "qk": nc.dram_tensor("qk_scratch", [2, P, T], F32, kind="Internal").ap(),
            "qst": nc.dram_tensor("q_stack", [H, ROW_M, T], BF16, kind="Internal").ap(),
            "klst": nc.dram_tensor("k_left_stack", [H, ROWS, T], BF16, kind="Internal").ap(),
            "krst": nc.dram_tensor("k_right_stack", [H, ROWS - ROW_QK, T], BF16, kind="Internal").ap(),
            "ctx": nc.dram_tensor("context", [H, DK + 1, T], F32, kind="Internal").ap(),
        }
        with ExitStack() as inner:
            keep["v_all"] = inner.enter_context(nc.sbuf_tensor("v_all", [P, NT, D], F32))
            setup_phase(nc, a, keep, scratch)
            attention_phase(nc, keep, scratch)
        output_phase(nc, keep, scratch)
        feed_forward_phase(nc, a, keep, out)


_OUT = (1, T, D)


def path_constants():
    paths = np.zeros((NODES, LEAVES), np.float32)
    turns = np.zeros((LEAVES, 1), np.float32)
    for leaf in range(LEAVES):
        for level in range(DEPTH):
            right = leaf >> (DEPTH - 1 - level) & 1
            paths[2 ** level - 1 + (leaf >> (DEPTH - level)), leaf] = 1 if right else -1
            turns[leaf] += right
    number = np.arange(LEAVES, dtype=np.float32).reshape(2, P).T
    return paths, np.ascontiguousarray(turns.reshape(2, P).T), np.ascontiguousarray(number)


def kernel(**inputs):
    import concourse.bacc as _bacc
    import ml_dtypes as _ml
    from concourse.bass_utils import run_bass_kernel_spmd as _run

    def given(name):
        return np.asarray(inputs[f"L0_{name}"])

    lay = {"x": given("attn_x"), "wmod": given("wmod"), "Wo": given("attn_Wo")}
    for w in ("Wq", "Wk", "Wv", "Wpk", "Wpq"):
        lay[w + "T"] = given("attn_" + w).T
    lay["relT"] = given("attn_rel_emb").T
    lay["relT_rev"] = given("attn_rel_emb")[::-1].T
    lay["c"] = given("c").reshape(D, 1)
    for b in ("bq", "bk", "bpk", "bpq", "bo"):
        lay[b] = given("attn_" + b).reshape(D, 1)
    lay["bv"] = given("attn_bv").reshape(1, D)
    for tree in "qkvf":
        w1, b1, w2, b2 = (given(f"ffn_{tree}_{n}") for n in ("w1", "b1", "w2", "b2"))
        lay[f"{tree}_leaves"] = np.concatenate(
            [w1.transpose(0, 2, 1).reshape(LEAVES, LW * D), w2.reshape(LEAVES, LW * D), b1, b2], axis=1)
        lay[f"{tree}_nwT"] = given(f"ffn_{tree}_nw").T
        lay[f"{tree}_nb"] = given(f"ffn_{tree}_nb").reshape(NODES, 1)
    paths, turns, number = path_constants()
    lay["paths"], lay["turns"], lay["number"] = paths.astype(_ml.bfloat16), turns, number.astype(_ml.bfloat16)

    nc = _bacc.Bacc("TRN2", target_bir_lowering=False, num_devices=1)
    arrays, a = {}, {}
    for name, value in lay.items():
        arrays[f"in_{name}"] = value = np.ascontiguousarray(value)
        a[name] = nc.dram_tensor(f"in_{name}", value.shape, mybir.dt.from_np(value.dtype), kind="ExternalInput").ap()
    out = nc.dram_tensor("out_0", _OUT, F32, kind="ExternalOutput").ap()
    adaln_block(nc, a, out)
    r = _run(nc, [arrays], core_ids=[0])
    return r.results[0]["out_0"]
```
